# Optimizing a Trainium2 kernel written in Bass

```python
import numpy as np
import jax
import jax.numpy as jnp

def _softmax(x, axis=-1):
    return jax.nn.softmax(x, axis=axis)

def _gelu(x):
    return jax.nn.gelu(x, approximate=True)

def _silu(x):
    return jax.nn.silu(x)

def _sigmoid(x):
    return jax.nn.sigmoid(x)

def _layernorm(x, axis=-1, eps=1e-05):
    m = jnp.mean(x, axis=axis, keepdims=True)
    v = jnp.var(x, axis=axis, keepdims=True)
    return (x - m) / jnp.sqrt(v + eps)

def _scatter_add(tgt, idx, src, axis=0):
    return tgt.at[idx].add(src)

def _segment_sum(src, seg, n):
    return jax.ops.segment_sum(src, seg, n)
kernel_name = 'mk_gnn_ffn_d1_gnn_r64_75e456'

def setup_inputs(seed: int=0):
    np.random.seed(seed)
    _w = jnp.asarray

    def _rec_inputs():
        import jax
        import jax.numpy as jnp
        _gk = jax.random.key(seed)
        x = -0.0003019 + 1 * jax.random.normal(jax.random.fold_in(_gk, 1), (10000, 1024), jnp.float32)
        src = jax.random.randint(jax.random.fold_in(_gk, 2), (5000,), 0, 10000, jnp.int32)
        dst = jax.random.randint(jax.random.fold_in(_gk, 3), (5000,), 0, 10000, jnp.int32)
        _o = jnp.argsort(dst, stable=True)
        src = src[_o]
        dst = dst[_o]
        return (x, src, dst)
    x, src, dst = _rec_inputs()

    def _L0_gnn_setup():
        import jax, jax.numpy as jnp
        import numpy as np
        N = 20000
        E = 5000
        IN = 1024
        HID = 256
        H = 4
        D = HID // H
        OUT = 1024
        EPS = 1e-06
        NEG_SLOPE = 0.2
        key = jax.random.key(seed)
        ks = jax.random.split(key, 8)
        x = jax.random.normal(ks[0], (N, IN), dtype=jnp.float32)
        edge_index = jax.random.randint(ks[1], (2, E), 0, N, dtype=jnp.int64)
        s = 0.02
        return {'x': x, 'edge_index': edge_index, 'rms_w': jnp.ones((IN,), dtype=jnp.float32), 'W_down': jax.random.normal(ks[2], (IN, HID), dtype=jnp.float32) * s, 'Wl': jax.random.normal(ks[3], (HID, HID), dtype=jnp.float32) * s, 'Wr': jax.random.normal(ks[4], (HID, HID), dtype=jnp.float32) * s, 'att': jax.random.normal(ks[5], (H, D), dtype=jnp.float32) * s, 'W_up': jax.random.normal(ks[6], (HID, OUT), dtype=jnp.float32) * s}
    _L0_gnn_all = _L0_gnn_setup()
    _L0_gnn_in = {k: v for k, v in _L0_gnn_all.items() if k in ('rms_w', 'W_down', 'Wl', 'Wr', 'att', 'W_up')}
    del _L0_gnn_all

    def _L0_ffn_setup():
        import jax, jax.numpy as jnp
        import numpy as np
        D_MODEL = 1024
        D_HIDDEN = 64
        NUM_EXPERT = 8
        TOP_K = 2
        B, N = (1, 128)

        def _expert_mlp(x, W1, b1, W2, b2, W3, b3):
            h = jax.nn.gelu(jnp.einsum('bnd,dh->bnh', x, W1) + b1, approximate=False)
            h = jax.nn.gelu(jnp.einsum('bnh,hk->bnk', h, W2) + b2, approximate=False)
            return jnp.einsum('bnh,hd->bnd', h, W3) + b3
        key = jax.random.key(seed)
        ks = jax.random.split(key, 8)
        s1 = 1.0 / np.sqrt(D_MODEL)
        s2 = 1.0 / np.sqrt(D_HIDDEN)
        return {'x': jax.random.normal(ks[0], (B, N, D_MODEL), jnp.float32), 'expert_tokens': jax.random.normal(ks[1], (NUM_EXPERT, D_MODEL), jnp.float32), 'W1': jax.random.normal(ks[2], (NUM_EXPERT, D_MODEL, D_HIDDEN), jnp.float32) * s1, 'b1': jnp.zeros((NUM_EXPERT, D_HIDDEN), jnp.float32), 'W2': jax.random.normal(ks[3], (NUM_EXPERT, D_HIDDEN, D_HIDDEN), jnp.float32) * s2, 'b2': jnp.zeros((NUM_EXPERT, D_HIDDEN), jnp.float32), 'W3': jax.random.normal(ks[4], (NUM_EXPERT, D_HIDDEN, D_MODEL), jnp.float32) * s2, 'b3': jnp.zeros((NUM_EXPERT, D_MODEL), jnp.float32)}
    _L0_ffn_all = _L0_ffn_setup()
    _L0_ffn_in = {k: v for k, v in _L0_ffn_all.items() if k in ('expert_tokens', 'W1', 'b1', 'W2', 'b2', 'W3', 'b3')}
    del _L0_ffn_all
    return {'x': x, 'src': src, 'dst': dst, 'L0_gnn_rms_w': _L0_gnn_in['rms_w'], 'L0_gnn_W_down': _L0_gnn_in['W_down'], 'L0_gnn_Wl': _L0_gnn_in['Wl'], 'L0_gnn_Wr': _L0_gnn_in['Wr'], 'L0_gnn_att': _L0_gnn_in['att'], 'L0_gnn_W_up': _L0_gnn_in['W_up'], 'L0_ffn_expert_tokens': _L0_ffn_in['expert_tokens'], 'L0_ffn_W1': _L0_ffn_in['W1'], 'L0_ffn_b1': _L0_ffn_in['b1'], 'L0_ffn_W2': _L0_ffn_in['W2'], 'L0_ffn_b2': _L0_ffn_in['b2'], 'L0_ffn_W3': _L0_ffn_in['W3'], 'L0_ffn_b3': _L0_ffn_in['b3']}

def reference(x, src, dst, L0_gnn_rms_w, L0_gnn_W_down, L0_gnn_Wl, L0_gnn_Wr, L0_gnn_att, L0_gnn_W_up, L0_ffn_expert_tokens, L0_ffn_W1, L0_ffn_b1, L0_ffn_W2, L0_ffn_b2, L0_ffn_W3, L0_ffn_b3):
    import jax
    import jax.numpy as jnp

    def _L0_gnn_ref(x, edge_index, rms_w, W_down, Wl, Wr, att, W_up):
        import jax, jax.numpy as jnp
        import numpy as np
        N = 20000
        E = 5000
        IN = 1024
        HID = 256
        H = 4
        D = HID // H
        OUT = 1024
        EPS = 1e-06
        NEG_SLOPE = 0.2
        n = x.shape[0]
        ms = jnp.mean(jnp.square(x), axis=-1, keepdims=True)
        x = x * jax.lax.rsqrt(ms + EPS) * rms_w
        x = x @ W_down
        loop = jnp.arange(n, dtype=edge_index.dtype)
        src = jnp.concatenate([edge_index[0], loop])
        dst = jnp.concatenate([edge_index[1], loop])
        xl = (x @ Wl).reshape(n, H, D)
        xr = (x @ Wr).reshape(n, H, D)
        msg = xl[src] + xr[dst]
        act = jnp.where(msg > 0, msg, NEG_SLOPE * msg)
        e = jnp.einsum('ehd,hd->eh', act, att)
        m = jax.ops.segment_max(e, dst, num_segments=n)
        p = jnp.exp(e - m[dst])
        denom = jax.ops.segment_sum(p, dst, num_segments=n)
        alpha = p / (denom[dst] + 1e-16)
        out = jax.ops.segment_sum(alpha[..., None] * xl[src], dst, num_segments=n)
        out = out.reshape(n, HID)
        return out @ W_up

    def _L0_ffn_ref(x, expert_tokens, W1, b1, W2, b2, W3, b3):
        import jax, jax.numpy as jnp
        import numpy as np
        D_MODEL = 1024
        D_HIDDEN = 64
        NUM_EXPERT = 8
        TOP_K = 2
        B, N = (1, 128)

        def _expert_mlp(x, W1, b1, W2, b2, W3, b3):
            h = jax.nn.gelu(jnp.einsum('bnd,dh->bnh', x, W1) + b1, approximate=False)
            h = jax.nn.gelu(jnp.einsum('bnh,hk->bnk', h, W2) + b2, approximate=False)
            return jnp.einsum('bnh,hd->bnd', h, W3) + b3
        scores = jnp.einsum('bnd,ed->bne', x, expert_tokens)
        _, topk_idx = jax.lax.top_k(scores, TOP_K)
        outputs = jnp.zeros_like(x)
        num_expert = W1.shape[0]
        for i in range(num_expert):
            w = jnp.mean((topk_idx == i).astype(x.dtype), axis=-1, keepdims=True)
            y = _expert_mlp(x, W1[i], b1[i], W2[i], b2[i], W3[i], b3[i])
            outputs = outputs + y * w
        return outputs
    edge_index = jnp.stack([src, dst])
    x = x + _L0_gnn_ref(_layernorm(x, axis=-1), edge_index, L0_gnn_rms_w, L0_gnn_W_down, L0_gnn_Wl, L0_gnn_Wr, L0_gnn_att, L0_gnn_W_up)
    x = x + _L0_ffn_ref(_layernorm(x, axis=-1)[None], L0_ffn_expert_tokens, L0_ffn_W1, L0_ffn_b1, L0_ffn_W2, L0_ffn_b2, L0_ffn_W3, L0_ffn_b3)[0]
    return x

_drawn_inputs = setup_inputs


def setup_inputs(seed=0):
    import zlib

    import numpy as np

    out = dict(_drawn_inputs(seed))
    spreads = {'L0_gnn_rms_w': (1.0, 0.2),
     'L0_ffn_b1': (0.0, 0.277),
     'L0_ffn_b2': (0.0, 0.1),
     'L0_ffn_b3': (0.0, 0.1)}
    factors = {'L0_gnn_Wr': 46.19, 'L0_gnn_att': 35.706}
    for name, (base, spread) in spreads.items():
        noise = np.random.default_rng([zlib.crc32(name.encode()), seed]).standard_normal(out[name].shape)
        drawn = base * np.exp(spread * noise) if base else spread * noise
        out[name] = jnp.asarray(drawn.astype(out[name].dtype))
    for name, factor in factors.items():
        out[name] = (out[name] * factor).astype(out[name].dtype)
    return out
```

```python
from contextlib import ExitStack

import concourse.bass as bass
from concourse import mybir

N, D = 10000, 1024
E = 5000
HID, H = 256, 4
HD = HID // H
NE, EH = 8, 64
P, J = 125, 4
G = P * J
NG = N // G
KD = D // 128
KH = HID // 128
MF = NE * EH // 128
HALF = 512
NC = E // P
CB = 4
NB = NC // CB
SPLIT = 112
LN_EPS, RMS_EPS = 1e-5, 1e-6
SLOPE = 0.2
TABLE = N + E // 2
CPG = NC // NG
MAPW = 100
FAR = -3.0e38

F32, F32R, BF16, I32 = mybir.dt.float32, mybir.dt.float32r, mybir.dt.bfloat16, mybir.dt.int32
ALU = mybir.AluOpType
ACT = mybir.ActivationFunctionType
AX = mybir.AxisListType


def wait(engine, sem, value):
    if isinstance(value, int) and value <= 0:
        return
    engine.wait_ge(sem, value)


def build(nc, x, src, dst, rms_w, w_down, wl, wr, att, w_up, tok, w1, b1, w2, b2, w3, b3, out):
    ctx = ExitStack()
    with ctx:
        base = [(nc.sbuf_base + 31) // 32 * 32]
        origin = base[0]

        def put(name, shape, dt, at):
            return nc.alloc_sbuf_tensor_at(name, shape, dt, offset=origin + at)

        def run_of(at, *items):
            made = []
            for name, shape, dt in items:
                made.append(put(name, shape, dt, at))
                size = 2 if dt == BF16 else 4
                for n in shape[1:]:
                    size *= n
                at += (size + 31) // 32 * 32
            return (*made, at)

        def sem(name):
            return ctx.enter_context(nc.semaphore(name))

        bank = [ctx.enter_context(nc.psum_tensor(f"bank{i}", [128, HALF], F32)) for i in range(8)]
        table = nc.dram_tensor("node_table", [TABLE, 2 * HID], F32)
        where_from = nc.dram_tensor("where_from", [N + P, 1], I32)

        (ident, rmsw, b1c, b2c, neg_half, comb, dup_mask, dup_rest, dst_col, dst_next_col, src_idx, dst_idx,
         scat_idx, row_of_edge, idx_now, row_now, from_idx, trash, last_of_chunk, eq_last, earlier, pe_pair, pexp, lsb, tie, at0) = run_of(
            0,
            ("ident", [128, 128], F32), ("rmsw", [128, KD], F32),
            ("b1c", [128, MF], F32), ("b2c", [128, MF], F32), ("neg_half", [P, J], F32),
            ("comb", [2 * NE, NE], F32), ("dup_mask", [2 * NE, 1], F32), ("dup_rest", [2 * NE, 1], F32),
            ("dst_col", [P, NC], F32), ("dst_next_col", [P, NC], F32), ("src_idx", [P, NC], I32),
            ("dst_idx", [P, NC], I32), ("scat_idx", [P, NC], I32), ("row_of_edge", [P, NC], I32), ("idx_now", [P, J], I32),
            ("row_now", [P, CPG], I32), ("from_idx", [P, NG, J], I32), ("trash", [P, 1], F32),
            ("last_of_chunk", [NC, 1], F32), ("eq_last", [P, NC], F32), ("earlier", [NC, NC], F32),
            ("pe_pair", [P, 2, H, NC], F32), ("pexp", [P, 2, H, NC], F32), ("lsb", [NC, HID + H], F32), ("tie", [P, NE, NE], F32))
        (att_bc, stat, mv, var, rstd, nbias, tok_st, b3_hl, expand, at1) = run_of(
            at0,
            ("att_bc", [P, HID], F32), ("stat", [P, J, 12], F32), ("mv", [P, 2, J, 2], F32),
            ("var", [P, 2, J], F32), ("rstd", [P, 2, J], F32), ("nbias", [P, 2, J], F32),
            ("tok_st", [128, KD, 128], F32R), ("b3_hl", [2 * NE, D], F32R), ("expand", [NE, NE * EH], F32R))

        wup_hi, wup_lo, w1_hi, w1_lo, at2 = run_of(
            at1,
            ("wup_hi", [128, KH, D], F32R), ("wup_lo", [128, KH, D], F32R),
            ("w1_hi", [128, KD, HALF], F32R), ("w1_lo", [128, KD, HALF], F32R))
        wup_raw = put("wup_raw", [128, KH, D], F32, at1 + KH * D * 4)
        w1_raw = put("w1_raw", [128, KD, HALF], F32, at1 + 2 * KH * D * 4 + KD * HALF * 4)
        w2_hi, w2_lo, w3_hi, w3_lo, at3 = run_of(
            at2,
            ("w2_hi", [128, MF, 128], F32R), ("w2_lo", [128, MF, 128], F32R), ("w3_hi", [128, MF, D], F32R), ("w3_lo", [128, MF, D], F32R))
        w2_raw = put("w2_raw", [128, MF, 128], F32, at2 + MF * 128 * 4)
        w3_raw = put("w3_raw", [128, MF, D], F32, at3 - MF * D * 4)

        (ax, axn, axt_hi, axt_lo, ht_hi, ht_lo, trow, wd_hi, wd_lo, wlr_hi, wlr_lo, a_end) = run_of(
            at2,
            ("ax", [P, 2, J * D], F32), ("axn", [P, 2, J, D], F32),
            ("axt_hi", [128, 4, G], F32R), ("axt_lo", [128, 4, G], F32R),
            ("ht_hi", [128, 2, KH, G], F32R), ("ht_lo", [128, 2, KH, G], F32R),
            ("trow", [P, 2, J * 2 * HID], F32),
            ("wd_hi", [128, KD, HID], F32R), ("wd_lo", [128, KD, HID], F32R),
            ("wlr_hi", [128, KH, 2 * HID], F32R), ("wlr_lo", [128, KH, 2 * HID], F32R))
        wd_raw = put("wd_raw", [128, KD, HID], F32, a_end - 2 * KH * 2 * HID * 4 - KD * HID * 4)
        wlr_raw = put("wlr_raw", [128, KH, 2 * HID], F32, a_end - KH * 2 * HID * 4)
        (idx_rows, idx_f, tok_rows, b3_raw, b3_hi, b3_lo, expand_raw, own_rows, _) = run_of(
            at1,
            ("idx_rows", [NC, 3, P], I32), ("idx_f", [NC, 3, P], F32), ("tok_rows", [NE, D], F32),
            ("b3_raw", [2 * NE, D], F32), ("b3_hi", [2 * NE, D], F32R), ("b3_lo", [2 * NE, D], F32),
            ("expand_raw", [NE, NE * EH], F32), ("own_rows", [MAPW, N // MAPW], I32))

        xls, xld, dst_row, at4 = run_of(
            at2, ("xls", [P, NC, HID], F32), ("xld", [P, NC, HID], F32), ("dst_row", [P, E], I32))
        td, msg, at5 = run_of(
            at4, ("td", [P, 2, CB, 2 * HID], F32), ("msg", [P, 2, 2 * CB, HID], F32))
        fresh, b_end = run_of(at5, ("fresh", [H, E + 8], BF16))
        max_row, max_t, _ = run_of(at4, ("max_row", [H, E], F32), ("max_t", [NC * 2, 2, P], F32))
        (zsel, zmat, smat, bmat, orow, tot, rden, psr, _) = run_of(
            at4,
            ("zsel", [P, NC, NC], F32), ("zmat", [P, 2, CB, NC], F32), ("smat", [P, 2, CB, P], F32),
            ("bmat", [NC, 2, CB, P], F32), ("orow", [P, 2, CB, HID], F32), ("tot", [P, H, CB], F32),
            ("rden", [P, H, CB], F32), ("psr", [P, 2, H, CB], F32))

        (cx, cxn, cxt_hi, cxt_lo, gl, h_hi, h_lo, agg, aggt_hi, aggt_lo, sc_t, w_t, score, beats, beats2, rank,
         wdup, c_end) = run_of(
            at3,
            ("cx", [P, 2, J, D], F32), ("cxn", [P, J, D], F32),
            ("cxt_hi", [128, 2, G], F32R), ("cxt_lo", [128, 2, G], F32R), ("gl", [128, 2, G], F32),
            ("h_hi", [128, MF, G], F32R), ("h_lo", [128, MF, G], F32R), ("agg", [P, J, HID], F32),
            ("aggt_hi", [128, KH, G], F32R), ("aggt_lo", [128, KH, G], F32R),
            ("sc_t", [2 * NE, G], F32), ("w_t", [2 * NE, G], F32R), ("score", [P, J, NE], F32),
            ("beats", [P, J, NE, NE], F32), ("beats2", [P, J, NE, NE], F32), ("rank", [P, J, NE], F32),
            ("wdup", [P, J, 2, NE], F32))
        assert origin + max(a_end, b_end, c_end, at3) <= nc.sbuf_usable_end, (a_end, b_end, c_end)

        consts = sem("consts")
        raw_idx, raw_small, raw_wa, raw_wc = sem("raw_idx"), sem("raw_small"), sem("raw_wa"), sem("raw_wc")
        raw_dst_row, raw_w3 = sem("raw_dst_row"), sem("raw_w3")
        setup_v, setup_t, setup_s, setup_p = sem("setup_v"), sem("setup_t"), sem("setup_s"), sem("setup_p")
        ax_loaded = [sem("ax_loaded0"), sem("ax_loaded1")]
        a_bn, a_aggr, a_var, a_rstd, a_nb = sem("a_bn"), sem("a_aggr"), sem("a_var"), sem("a_rstd"), sem("a_nb")
        a_xn, a_tp, a_hi, a_lo, a_mm = sem("a_xn"), sem("a_tp"), sem("a_hi"), sem("a_lo"), sem("a_mm")
        a_hhi, a_hlo, a_lr = sem("a_hhi"), sem("a_hlo"), sem("a_lr")
        a_ev_s, a_ev_v = sem("a_ev_s"), sem("a_ev_v")
        t_stored = [sem("t_stored0"), sem("t_stored1")]
        gathered = [sem("gathered0"), sem("gathered1")]
        b_split_s, b_split_v, b_fresh = sem("b_split_s"), sem("b_split_v"), sem("b_fresh")
        b_add, b_xld, b_leak, b_mul, b_red = sem("b_add"), sem("b_xld"), sem("b_leak"), sem("b_mul"), sem("b_red")
        b_max, b_max_t, b_rows, b_scan, b_back, b_exp = (
            sem("b_max"), sem("b_max_t"), sem("b_rows"), sem("b_scan"), sem("b_back"), sem("b_exp"))
        b_zsel, b_v, b_z, b_l, b_lsb = sem("b_zsel"), sem("b_v"), sem("b_z"), sem("b_l"), sem("b_lsb")
        b_sb, b_num, b_den, b_self, b_out = sem("b_sb"), sem("b_num"), sem("b_den"), sem("b_self"), sem("b_out")
        b_scaled = sem("b_scaled")
        map_copied, map_put, map_loaded = sem("map_copied"), sem("map_put"), sem("map_loaded")
        rows_stored = [sem("rows_stored0"), sem("rows_stored1")]
        cx_loaded = [sem("cx_loaded0"), sem("cx_loaded1")]
        out_stored = [sem("out_stored0"), sem("out_stored1")]
        agg_loaded = sem("agg_loaded")
        c_tp, c_mm, c_atp, c_up, c_rs, c_w2, c_wtp, c_wx, c_w3 = (
            sem("c_tp"), sem("c_mm"), sem("c_atp"), sem("c_up"), sem("c_rs"), sem("c_w2"), sem("c_wtp"),
            sem("c_wx"), sem("c_w3"))
        c_hi, c_ahi, c_g1, c_h1hi, c_g2, c_h2hi, c_xn = (
            sem("c_hi"), sem("c_ahi"), sem("c_g1"), sem("c_h1hi"), sem("c_g2"), sem("c_h2hi"), sem("c_xn"))
        c_lo, c_alo, c_sc, c_h1lo, c_upv, c_w3v, c_rt, c_w, c_wt, c_wmul, c_h2lo = (
            sem("c_lo"), sem("c_alo"), sem("c_sc"), sem("c_h1lo"), sem("c_upv"), sem("c_w3v"), sem("c_rt"),
            sem("c_w"), sem("c_wt"), sem("c_wmul"), sem("c_h2lo"))
        c_bn, c_aggr, c_var, c_rstd, c_nb = sem("c_bn"), sem("c_aggr"), sem("c_var"), sem("c_rstd"), sem("c_nb")
        turns, turns_p = sem("turns"), sem("turns_p")
        w3_split_s, w3_split_v = sem("w3_split_s"), sem("w3_split_v")

        x_g = x.rearrange("(g p j) d -> g p (j d)", p=P, j=J)
        out_g = out.rearrange("(g p j) d -> g p (j d)", p=P, j=J)
        t_g = table[0:N, :].rearrange("(g p j) d -> g p (j d)", p=P, j=J)
        t_half = table[:, :].rearrange("n (a d) -> (n a) d", a=2)
        t_edge = t_half[2 * N:2 * N + E, :].rearrange("(c p) d -> p c d", p=P)

        T_A, H_A, X_A = bank[0:4], bank[4:6], bank[6:8]
        ACC, T_C, Y = bank[0:4], bank[4:6], bank[6:8]

        block = ctx.enter_context(nc.Block())

        def pairs(engine, body, last=NG):
            for par in range(2):
                body(par, par)
            with engine.Fori(1, last // 2 - 1) as i:
                for par in range(2):
                    body(2 * i + par, par)
            for par in range(2):
                body(last - 2 + par, par)

        def has(g, more):
            return not isinstance(g, int) or 0 <= g + more < NG

        def halves(g):
            return g // 2 + 1 if isinstance(g, int) else None

        @block.sync
        def _(sp):
            def load_x(g, par, fill):
                wait(sp, a_xn, J * (g - 1))
                sp.dma_start(ax[0:SPLIT, par, :], x_g[g, 0:SPLIT, :]).then_inc(ax_loaded[par], 16)
                sp.dma_start(ax[SPLIT:P, par, :], x_g[g, SPLIT:P, :]).then_inc(ax_loaded[par], 16)

            load_x(0, 0, 1)
            sp.dma_start(rmsw[:, :], rms_w.rearrange("(k p) -> p k", p=128),
                         allow_slow_non_contiguous=True).then_inc(raw_wa, 16)
            sp.dma_start(wd_raw[:, :, :], w_down.rearrange("(k p) n -> p k n", p=128)).then_inc(raw_wa, 16)
            sp.dma_start(wlr_raw[:, :, 0:HID], wl.rearrange("(k p) n -> p k n", p=128)).then_inc(raw_wa, 16)
            sp.dma_start(wlr_raw[:, :, HID:], wr.rearrange("(k p) n -> p k n", p=128)).then_inc(raw_wa, 16)
            load_x(1, 1, 1)
            sp.wait_ge(consts, 1)
            sp.dma_start(idx_rows[:, 0, :], src.rearrange("(c p) -> c p", p=P)).then_inc(raw_idx, 16)
            sp.dma_start(idx_rows[:, 1, :], dst.rearrange("(c p) -> c p", p=P)).then_inc(raw_idx, 16)
            sp.dma_start(idx_rows[0:NC - 1, 2, :],
                         dst[1:1 + (NC - 1) * P].rearrange("(c p) -> c p", p=P)).then_inc(raw_idx, 16)
            sp.dma_start(idx_rows[NC - 1:NC, 2, 0:P - 1],
                         dst[1 + (NC - 1) * P:E].rearrange("(c p) -> c p", c=1)).then_inc(raw_idx, 16)
            sp.dma_start(tok_rows[:, :], tok).then_inc(raw_small, 16)
            sp.dma_start(b3_raw[0:NE, :], b3).then_inc(raw_small, 16)
            sp.dma_start(b3_raw[NE:2 * NE, :], b3).then_inc(raw_small, 16)
            sp.dma_start(att_bc[:, :], att.rearrange("h d -> (h d)").partition_broadcast(P)).then_inc(raw_small, 16)
            sp.dma_start(b1c[:, :], b1.rearrange("(m a) h -> (a h) m", a=2),
                         allow_slow_non_contiguous=True).then_inc(raw_small, 16)
            sp.dma_start(b2c[:, :], b2.rearrange("(m a) h -> (a h) m", a=2),
                         allow_slow_non_contiguous=True).then_inc(raw_small, 16)

            def body(g, par):
                if has(g, 2):
                    load_x(g + 2, par, None)

            pairs(sp, body)

            sp.wait_ge(map_put, 16 * (1 + NC))
            sp.dma_start(from_idx[:, :, :],
                         where_from[0:N, :].rearrange("(g p j) a -> p g (j a)", p=P, j=J)).then_inc(map_loaded, 16)

            sp.wait_ge(setup_v, 12)
            sp.wait_ge(consts, 3)
            sp.dma_start(wup_raw[:, :, :], w_up.rearrange("(k p) n -> p k n", p=128)).then_inc(raw_wc, 16)
            for k in range(KD):
                sp.dma_start(w1_raw[:, k, :].rearrange("p (e h) -> p e h", e=NE),
                             w1[:, 128 * k:128 * (k + 1), :].rearrange("e p h -> p e h")).then_inc(raw_wc, 16)
            for par in range(2):
                sp.wait_ge(t_stored[par], 32 * (NG // 2))
            sp.dma_start(dst_row[:, :], dst.partition_broadcast(P)).then_inc(raw_dst_row, 16)

            sp.wait_ge(b_max, 3)
            sp.wait_ge(b_xld, NB)
            for q in range(2):
                sp.dma_start(max_row[2 * q:2 * q + 2, :].rearrange("h (c p) -> h c p", p=P),
                             max_t[:, q, :]).then_inc(b_rows, 16)
            sp.wait_ge(b_scan, 2)
            for q in range(2):
                sp.dma_start(max_t[:, q, :],
                             max_row[2 * q:2 * q + 2, :].rearrange("h (c p) -> h c p", p=P)).then_inc(b_rows, 16)

            def store_rows(b, par):
                sp.wait_ge(b_out, b + 1)
                sp.dma_start(t_edge[:, bass.ds(CB * b, CB), :], orow[:, par, :, :]).then_inc(rows_stored[par], 16)

            with sp.Fori(0, NB // 2) as i:
                for par in range(2):
                    store_rows(2 * i + par, par)

            for par in range(2):
                sp.wait_ge(rows_stored[par], 16 * (NB // 2))

            def load_cx(g, par):
                sp.dma_start(cx[0:SPLIT, par, :, :].rearrange("p j d -> p (j d)"),
                             x_g[g, 0:SPLIT, :]).then_inc(cx_loaded[par], 16)
                sp.dma_start(cx[SPLIT:P, par, :, :].rearrange("p j d -> p (j d)"),
                             x_g[g, SPLIT:P, :]).then_inc(cx_loaded[par], 16)

            load_cx(0, 0)
            sp.dma_start(w3_raw[:, :, :], w3.rearrange("(m a) h n -> (a h) m n", a=2)).then_inc(raw_w3, 16)
            sp.wait_ge(consts, 4)
            w2_pairs = w2.rearrange("(m a) h k -> a h m k", a=2)
            for a in range(2):
                sp.dma_start(w2_raw[EH * a:EH * (a + 1), :, EH * a:EH * (a + 1)], w2_pairs[a]).then_inc(raw_w3, 16)
            load_cx(1, 1)

            def body_c(g, par):
                sp.wait_ge(c_w3v, 8 * (g + 1))
                sp.dma_start(out_g[g, 0:SPLIT, :],
                             cx[0:SPLIT, par, :, :].rearrange("p j d -> p (j d)")).then_inc(out_stored[par], 16)
                sp.dma_start(out_g[g, SPLIT:P, :],
                             cx[SPLIT:P, par, :, :].rearrange("p j d -> p (j d)")).then_inc(out_stored[par], 16)
                if has(g, 2):
                    sp.wait_ge(out_stored[par], 16 * (g + 2 - par))
                    load_cx(g + 2, par)

            pairs(sp, body_c)
            for par in range(2):
                sp.wait_ge(out_stored[par], 16 * NG)

        @block.gpsimd
        def _(pool):
            pool.memset(idx_rows[:, :, :], -1)
            pool.memset(tok_st[:, :, :].bitcast(F32), 0.0)
            pool.memset(ident[:, :], 0.0).then_inc(consts, 1)
            pool.wait_ge(consts, 1)
            pool.affine_select(out=ident[:, :], in_=ident[:, :], compare_op=ALU.not_equal, fill=1.0, base=0,
                               pattern=[[-1, 128]], channel_multiplier=1).then_inc(consts, 1)
            pool.memset(neg_half[:, :], -0.5).then_inc(setup_p, 1)
            pool.memset(comb[:, :], 0.0)
            pool.memset(expand_raw[:, :], 1.0)
            pool.memset(dup_mask[:, :], 1.0)
            pool.memset(earlier[:, :], 1.0)
            pool.memset(tie[:, :, :], 1.0)
            pool.iota(own_rows[:, :], [[2, N // MAPW]], base=0, channel_multiplier=2 * N // MAPW)
            pool.iota(row_of_edge[:, :], [[P, NC]], base=2 * N, channel_multiplier=1)
            pool.iota(scat_idx[:, 0:1], [[0, 1]], base=N, channel_multiplier=1).then_inc(setup_p, 1)
            pool.wait_ge(setup_p, 2)
            pool.affine_select(out=comb[:, :], in_=comb[:, :], compare_op=ALU.not_equal, fill=1.0, base=0,
                               pattern=[[-1, NE]], channel_multiplier=1).then_inc(setup_p, 1)
            pool.affine_select(out=dup_mask[:, :], in_=dup_mask[:, :], compare_op=ALU.is_gt, fill=0.0, base=NE,
                               pattern=[[0, 1]], channel_multiplier=-1)
            pool.affine_select(out=expand_raw[:, :], in_=expand_raw[:, :], compare_op=ALU.is_ge, fill=0.0, base=0,
                               pattern=[[1, NE * EH]], channel_multiplier=-EH)
            pool.affine_select(out=earlier[:, :], in_=earlier[:, :], compare_op=ALU.is_gt, fill=0.0, base=0,
                               pattern=[[1, NC]], channel_multiplier=-1)
            pool.affine_select(out=tie[:, :, :], in_=tie[:, :, :], compare_op=ALU.is_gt, fill=0.0, base=0,
                               pattern=[[1, NE], [-1, NE]], channel_multiplier=0).then_inc(setup_p, 1)
            pool.wait_ge(setup_p, 4)
            pool.affine_select(out=comb[:, :], in_=comb[:, :], compare_op=ALU.not_equal, fill=1.0, base=-NE,
                               pattern=[[-1, NE]], channel_multiplier=1).then_inc(setup_p, 1)
            pool.affine_select(out=expand_raw[:, :], in_=expand_raw[:, :], compare_op=ALU.is_ge, fill=0.0,
                               base=EH - 1, pattern=[[-1, NE * EH]], channel_multiplier=EH).then_inc(consts, 1)

            pool.dma_start(where_from[0:N, :].rearrange("(p i) a -> p (i a)", p=MAPW), own_rows[:, :]
                           ).then_inc(map_put, 16)

            def rstd_a(g, par):
                pool.wait_ge(a_var, g + 1)
                pool.tensor_tensor(rstd[:, par, :], var[:, par, :], neg_half[:, :], ALU.pow).then_inc(a_rstd, 1)

            def body(g, par):
                if isinstance(g, int) and g == 0:
                    pool.wait_ge(setup_v, 9)
                pool.wait_ge(map_put, 16 * (CPG * g + 1))
                pool.sem_inc(turns_p, 1)
                pool.tensor_copy(idx_now[:, 0:CPG], scat_idx[:, bass.ds(CPG * g, CPG)])
                pool.tensor_copy(row_now[:, :], row_of_edge[:, bass.ds(CPG * g, CPG)]).then_inc(map_copied, 1)
                pool.wait_ge(map_copied, g + 1)
                pool.sem_inc(turns_p, 1)
                for q in range(CPG):
                    pool.wait_ge(map_put, 16 * (CPG * g + q + 1))
                    pool.sem_inc(turns_p, 1)
                    pool.indirect_dma_start(
                        out=where_from[:, :], out_offset=bass.IndirectOffsetOnAxis(ap=idx_now[:, q:q + 1], axis=0),
                        in_=row_now[:, q:q + 1], in_offset=None).then_inc(map_put, 16)
                if has(g, 2):
                    rstd_a(g + 2, par)

            rstd_a(0, 0)
            rstd_a(1, 1)

            pairs(pool, body)

            for par in range(2):
                pool.wait_ge(t_stored[par], 32 * (NG // 2))
            pool.wait_ge(setup_v, 9)
            for b in range(NB):
                if b >= 2:
                    pool.wait_ge(b_add, b - 1)
                    pool.wait_ge(b_xld, b - 1)
                for q in range(CB):
                    c = CB * b + q
                    pool.indirect_dma_start(
                        out=xls[:, c, :], out_offset=None, in_=t_half[0:2 * N, :],
                        in_offset=bass.IndirectOffsetOnAxis(ap=src_idx[:, c:c + 1], axis=0)
                    ).then_inc(gathered[b % 2], 16)
                    pool.indirect_dma_start(
                        out=td[:, b % 2, q, :], out_offset=None, in_=table[0:N, :],
                        in_offset=bass.IndirectOffsetOnAxis(ap=dst_idx[:, c:c + 1], axis=0)
                    ).then_inc(gathered[b % 2], 16)

            pool.wait_ge(b_back, 2)
            pool.memset(zsel[:, :, :], 0.0).then_inc(b_zsel, 1)
            pool.wait_ge(b_zsel, 1)
            pool.affine_select(out=zsel[:, :, :], in_=zsel[:, :, :], compare_op=ALU.not_equal, fill=1.0, base=0,
                               pattern=[[1, NC], [-1, NC]], channel_multiplier=0).then_inc(b_zsel, 1)

            for b in range(NB):
                pool.wait_ge(b_scaled, b + 1)
                rows = xld[:, CB * b:CB * (b + 1), :].rearrange("p c (h d) -> p c h d", h=H)
                pool.tensor_tensor(rows, rows,
                                   psr[:, b % 2, :, :].rearrange("p h c -> p c h").unsqueeze(3)
                                   .broadcast_to([P, CB, H, HD]), ALU.mult).then_inc(b_self, 1)
            pool.wait_ge(b_out, NB)
            pool.memset(w2_raw[:, :, :], 0.0).then_inc(consts, 1)

            def gather_rows(g):
                pool.tensor_copy(idx_now[:, :], from_idx[:, bass.ds(g, 1), :].rearrange("p g j -> p (g j)")
                                 ).then_inc(map_copied, 1)
                pool.wait_ge(map_copied, NG + 1 + g)
                pool.sem_inc(turns_p, 1)
                for j in range(J):
                    pool.indirect_dma_start(
                        out=agg[:, j, :], out_offset=None, in_=t_half,
                        in_offset=bass.IndirectOffsetOnAxis(ap=idx_now[:, j:j + 1], axis=0)
                    ).then_inc(agg_loaded, 16)

            def rstd_c(g, par):
                pool.wait_ge(c_var, g + 1)
                pool.tensor_tensor(rstd[:, par, :], var[:, par, :], neg_half[:, :], ALU.pow).then_inc(c_rstd, 1)

            pool.wait_ge(map_loaded, 16)
            for par in range(2):
                pool.wait_ge(rows_stored[par], 16 * (NB // 2))
            gather_rows(0)
            pool.wait_ge(c_atp, KH)
            gather_rows(1)
            rstd_c(0, 0)

            def body_c(g, par):
                if has(g, 2):
                    pool.wait_ge(c_atp, KH * (g + 2))
                    pool.sem_inc(turns_p, 1)
                    gather_rows(g + 2)
                if has(g, 1):
                    rstd_c(g + 1, 1 - par)

            pairs(pool, body_c)

        @block.scalar
        def _(act):
            act.wait_ge(setup_v, 1)
            act.activation(wd_hi[:, :, :], wd_raw[:, :, :], ACT.Copy).then_inc(setup_s, 1)
            act.activation(wlr_hi[:, :, :], wlr_raw[:, :, :], ACT.Copy).then_inc(setup_s, 1)

            def norm(g, par, j):
                act.wait_ge(a_nb, g + 1)
                wait(act, a_tp, KD * (g - 1))
                act.activation(axn[:, par, j, :], ax[:, par, D * j:D * (j + 1)], ACT.Identity,
                               bias=nbias[:, par, j:j + 1], scale=rstd[:, par, j:j + 1]).then_inc(a_xn, 1)

            def body(g, par):
                for k in range(KD):
                    t = KD * g + k
                    act.wait_ge(a_tp, t + 1)
                    wait(act, a_mm, t - 3)
                    act.activation(axt_hi[:, k % 4, :], T_A[k % 4][:, 0:G], ACT.Copy).then_inc(a_hi, 1)
                    if k < J and has(g, 1):
                        norm(g + 1, 1 - par, k)
                    if k == 5 and has(g, -2):
                        store_table(g - 2, par)
                for m in range(KH):
                    act.wait_ge(a_mm, KD * (g + 1))
                    wait(act, a_lr, J * (g - 1))
                    act.activation(ht_hi[:, par, m, :], H_A[m][:, 0:G], ACT.Copy).then_inc(a_hhi, 1)
                    if has(g, -1):
                        empty_lr(g - 1, 1 - par, 2 * m)

            def empty_lr(g, par, j):
                act.wait_ge(a_lr, J * g + j + 1)
                wait(act, t_stored[par], 16 * (g - par))
                act.activation(trow[:, par, 2 * HID * j:2 * HID * (j + 1)], X_A[0][0:P, :],
                               ACT.Copy).then_inc(a_ev_s, 1)

            def store_table(g, par):
                act.wait_ge(a_ev_s, 2 * (g + 1))
                act.wait_ge(a_ev_v, 2 * (g + 1))
                act.dma_start(t_g[g, 0:SPLIT, :], trow[0:SPLIT, par, :]).then_inc(t_stored[par], 16)
                act.dma_start(t_g[g, SPLIT:P, :], trow[SPLIT:P, par, :]).then_inc(t_stored[par], 16)

            for j in range(J):
                norm(0, 0, j)
            pairs(act, body)
            store_table(NG - 2, 0)
            empty_lr(NG - 1, 1, 0)
            empty_lr(NG - 1, 1, 2)
            store_table(NG - 1, 1)

            act.wait_ge(raw_wc, 16 * (1 + KD))
            act.activation(wup_hi[:, :, :], wup_raw[:, :, :], ACT.Copy).then_inc(b_split_s, 1)
            act.activation(w1_hi[:, :, :], w1_raw[:, :, :], ACT.Copy).then_inc(b_split_s, 1)

            def body_b(b, par):
                fills = 2 * CB * 16
                act.wait_ge(gathered[par], fills // 2 * (b - par) + fills)
                act.activation(xld[:, bass.ds(CB * b, CB), :], td[:, par, :, 0:HID], ACT.Copy).then_inc(b_xld, 1)

            with act.Fori(0, NB // 2) as i:
                for par in range(2):
                    body_b(2 * i + par, par)
            act.wait_ge(b_max, 6)
            act.activation(pexp[:, :, :, :], pe_pair[:, :, :, :], ACT.Exp).then_inc(b_exp, 1)

            def split_agg(m, g):
                act.wait_ge(c_atp, KH * g + m + 1)
                wait(act, c_up, 8 * g)
                act.activation(aggt_hi[:, m, :], Y[1][:, 0:G], ACT.Copy).then_inc(c_ahi, 1)

            def norm_c(g, par):
                for j in range(J):
                    act.wait_ge(c_nb, g + 1)
                    wait(act, c_tp, KD * g)
                    act.activation(cxn[:, j, :], cx[:, par, j, :], ACT.Identity,
                                   bias=nbias[:, par, j:j + 1], scale=rstd[:, par, j:j + 1]).then_inc(c_xn, 1)

            def gelu1(g, m):
                act.wait_ge(c_mm, KD * (g + 1))
                wait(act, c_h1lo, MF * g + m - 1) if m >= 2 else wait(act, c_h2lo, MF * g + m - 1)
                act.activation(gl[:, m % 2, :], ACC[m][:, 0:G], ACT.Gelu,
                               bias=b1c[:, m:m + 1]).then_inc(c_g1, 1)
                act.wait_ge(c_g1, MF * g + m + 1)
                wait(act, c_w3, 8 * g)
                act.activation(h_hi[:, m, :], gl[:, m % 2, :], ACT.Copy).then_inc(c_h1hi, 1)

            def gelu2(g, m):
                act.wait_ge(c_w2, MF * g + m + 1)
                act.wait_ge(c_h1lo, MF * g + m + 3) if m < 2 else act.wait_ge(c_h2lo, MF * g + m - 1)
                act.activation(gl[:, m % 2, :], ACC[m][:, 0:G], ACT.Gelu,
                               bias=b2c[:, m:m + 1]).then_inc(c_g2, 1)

            def high2(g, m):
                act.wait_ge(c_wmul, MF * g + m + 1)
                act.activation(h_hi[:, m, :], gl[:, m % 2, :], ACT.Copy).then_inc(c_h2hi, 1)

            def body_c(g, par):
                for k in range(KD):
                    t = KD * g + k
                    act.wait_ge(c_tp, t + 1)
                    wait(act, c_mm, t - 1)
                    act.activation(cxt_hi[:, k % 2, :], T_C[k % 2][:, 0:G], ACT.Copy).then_inc(c_hi, 1)
                    if k in (3, 6) and has(g, 1):
                        split_agg(k // 6, g + 1)
                for m in range(MF):
                    gelu1(g, m)
                gelu2(g, 0)
                for m in range(1, MF):
                    gelu2(g, m)
                    high2(g, m - 1)
                high2(g, MF - 1)
                if has(g, 1):
                    norm_c(g + 1, 1 - par)

            for m in range(KH):
                split_agg(m, 0)
            act.wait_ge(raw_w3, 16 * 3)
            act.activation(w2_hi[:, :, :], w2_raw[:, :, :], ACT.Copy)
            act.activation(w3_hi[:, :, :], w3_raw[:, :, :], ACT.Copy).then_inc(w3_split_s, 1)
            norm_c(0, 0)
            pairs(act, body_c)

        @block.vector
        def _(dve):
            def bn(g, par, piece, src_tile, done):
                j, n = piece // 2, piece % 2
                dve.bn_stats(stat[:, j, 6 * n:6 * n + 6],
                             src_tile[:, HALF * n:HALF * (n + 1)]).then_inc(done, 1)

            def moments(g, par, bn_sem, aggr_sem, var_sem, scale, shift):
                dve.wait_ge(bn_sem, 8 * (g + 1))
                dve.sem_inc(turns, 1)
                for j in range(J):
                    last = dve.bn_aggr(mv[:, par, j, :], stat[:, j, :])
                last.then_inc(aggr_sem, 1)
                dve.wait_ge(aggr_sem, g + 1)
                dve.tensor_scalar(var[:, par, :], mv[:, par, :, 1], scale, shift, ALU.mult, ALU.add
                                  ).then_inc(var_sem, 1)

            def bias_of(g, par, rstd_sem, nb_sem):
                dve.wait_ge(rstd_sem, g + 1)
                dve.scalar_tensor_tensor(nbias[:, par, :], mv[:, par, :, 0], -1.0, rstd[:, par, :],
                                         ALU.mult, ALU.mult).then_inc(nb_sem, 1)

            def moments_a(g, par):
                moments(g, par, a_bn, a_aggr, a_var, 1.0 + RMS_EPS, LN_EPS * RMS_EPS)

            def bn_a(g, par, piece):
                if piece == 0:
                    dve.wait_ge(ax_loaded[par], 16 * (g + 2 - par))
                    wait(dve, a_aggr, g)
                bn(g, par, piece, ax[:, par, D * (piece // 2):D * (piece // 2 + 1)], a_bn)

            for piece in range(8):
                bn_a(0, 0, piece)
            moments_a(0, 0)
            dve.wait_ge(raw_wa, 16 * 4)
            for k in range(KD):
                last = dve.tensor_scalar(wd_raw[:, k, :], wd_raw[:, k, :], rmsw[:, k:k + 1], None, ALU.mult)
            last.then_inc(setup_v, 1)
            bias_of(0, 0, a_rstd, a_nb)
            for piece in range(8):
                bn_a(1, 1, piece)
            moments_a(1, 1)
            dve.wait_ge(setup_s, 2)
            dve.tensor_tensor(wd_lo[:, :, :], wd_raw[:, :, :], wd_hi[:, :, :].bitcast(F32), ALU.subtract)
            dve.tensor_tensor(wlr_lo[:, :, :], wlr_raw[:, :, :], wlr_hi[:, :, :].bitcast(F32),
                              ALU.subtract).then_inc(setup_v, 1)
            bias_of(1, 1, a_rstd, a_nb)

            def small_setup():
                dve.wait_ge(raw_idx, 16 * 4)
                dve.tensor_copy(idx_f[:, :, :], idx_rows[:, :, :]).then_inc(setup_v, 1)
                dve.wait_ge(setup_t, 1)
                dve.tensor_scalar(src_idx[:, :], bank[0][0:P, 0:NC], 2.0, None, ALU.mult)
                dve.tensor_copy(dst_idx[:, :], bank[0][0:P, NC:2 * NC])
                dve.tensor_copy(dst_col[:, :], bank[0][0:P, NC:2 * NC])
                dve.tensor_copy(dst_next_col[:, :], bank[0][0:P, 2 * NC:3 * NC]).then_inc(setup_v, 1)
                dve.tensor_copy(last_of_chunk[:, :], idx_f[:, 1, P - 1:P])
                dve.wait_ge(setup_p, 2)
                dve.tensor_copy(trash[:, :], scat_idx[:, 0:1]).then_inc(setup_v, 1)
                dve.wait_ge(setup_v, 5)
                dve.tensor_tensor(dst_next_col[:, :], dst_next_col[:, :], dst_col[:, :],
                                  ALU.is_equal).then_inc(setup_v, 1)
                dve.tensor_scalar(eq_last[:, :], dst_col[:, :], -1.0, trash[:, 0:1], ALU.mult, ALU.add
                                  ).then_inc(setup_v, 1)
                dve.wait_ge(setup_v, 7)
                dve.tensor_tensor(dst_next_col[:, :], dst_next_col[:, :], eq_last[:, :],
                                  ALU.mult).then_inc(setup_v, 1)
                dve.wait_ge(setup_v, 8)
                dve.tensor_tensor(scat_idx[:, :], dst_col[:, :], dst_next_col[:, :], ALU.add
                                  ).then_inc(setup_v, 1)
                dve.wait_ge(setup_t, 2)
                tok_t = bank[1][:, 0:KD * NE].rearrange("p (k e) -> p k e", e=NE)
                dve.tensor_copy(tok_st[:, :, 0:NE], tok_t).then_inc(setup_v, 1)
                dve.wait_ge(setup_v, 10)
                dve.tensor_tensor(tok_st[:, :, NE:2 * NE], tok_t, tok_st[:, :, 0:NE].bitcast(F32), ALU.subtract)
                dve.tensor_copy(b3_hi[:, :], b3_raw[:, :])
                dve.tensor_scalar(dup_rest[:, :], dup_mask[:, :], -1.0, 1.0, ALU.mult, ALU.add)
                dve.wait_ge(consts, 3)
                dve.tensor_copy(expand[:, :], expand_raw[:, :]).then_inc(setup_v, 1)
                dve.wait_ge(setup_v, 11)
                dve.tensor_tensor(b3_lo[:, :], b3_raw[:, :], b3_hi[:, :].bitcast(F32), ALU.subtract
                                  ).then_inc(b_split_v, 1)
                dve.wait_ge(b_split_v, 1)
                dve.tensor_scalar(b3_lo[:, :], b3_lo[:, :], dup_rest[:, 0:1], None, ALU.mult).then_inc(b_split_v, 1)
                dve.wait_ge(b_split_v, 2)
                dve.scalar_tensor_tensor(b3_hl[:, :], b3_hi[:, :].bitcast(F32), dup_mask[:, 0:1], b3_lo[:, :],
                                         ALU.mult, ALU.add).then_inc(setup_v, 1)

            dve.wait_ge(raw_small, 16 * 6)
            small_setup()

            def empty_lr(g, par, j):
                dve.wait_ge(a_lr, J * g + j + 1)
                wait(dve, t_stored[par], 16 * (g - par))
                dve.tensor_copy(trow[:, par, 2 * HID * j:2 * HID * (j + 1)], X_A[1][0:P, :]).then_inc(a_ev_v, 1)

            def body(g, par):
                for k in range(KD):
                    dve.wait_ge(a_hi, KD * g + k + 1)
                    dve.tensor_tensor(axt_lo[:, k % 4, :], T_A[k % 4][:, 0:G],
                                      axt_hi[:, k % 4, :].bitcast(F32), ALU.subtract).then_inc(a_lo, 1)
                    if has(g, 2):
                        bn_a(g + 2, par, k)
                for m in range(KH):
                    dve.wait_ge(a_hhi, KH * g + m + 1)
                    dve.tensor_tensor(ht_lo[:, par, m, :], H_A[m][:, 0:G],
                                      ht_hi[:, par, m, :].bitcast(F32), ALU.subtract).then_inc(a_hlo, 1)
                if has(g, 2):
                    moments_a(g + 2, par)
                if has(g, -1):
                    empty_lr(g - 1, 1 - par, 1)
                if has(g, 2):
                    bias_of(g + 2, par, a_rstd, a_nb)
                if has(g, -1):
                    empty_lr(g - 1, 1 - par, 3)

            pairs(dve, body)
            empty_lr(NG - 1, 1, 1)
            empty_lr(NG - 1, 1, 3)

            dve.wait_ge(raw_dst_row, 16)
            dve.memset(fresh[:, :], 0.0).then_inc(b_fresh, 1)
            dve.tensor_tensor(eq_last[:, :], dst_col[:, :],
                              dst_row[:, P - 1:E:P], ALU.is_equal)
            dve.wait_ge(b_fresh, 1)
            dve.tensor_tensor(fresh[:, 1:E], dst_row[0:H, 1:E], dst_row[0:H, 0:E - 1], ALU.not_equal
                              ).then_inc(b_fresh, 1)
            dve.wait_ge(b_fresh, 2)
            dve.tensor_scalar(fresh[:, 1:E], fresh[:, 1:E], FAR, None, ALU.mult).then_inc(b_fresh, 1)
            for n, (lo, raw, hi) in enumerate(((wup_lo, wup_raw, wup_hi), (w1_lo, w1_raw, w1_hi))):
                dve.wait_ge(b_split_s, n + 1)
                dve.tensor_tensor(lo[:, :, :], raw[:, :, :], hi[:, :, :].bitcast(F32), ALU.subtract
                                  ).then_inc(b_split_v, 1)

            def add_messages(b, par):
                fills = 2 * CB * 16
                dve.wait_ge(gathered[par], fills // 2 * (b - par) + fills)
                wait(dve, b_red, 2 * (b - 1))
                dve.tensor_tensor(msg[:, par, 0:CB, :], xls[:, bass.ds(CB * b, CB), :],
                                  td[:, par, :, HID:2 * HID], ALU.add)
                dve.tensor_tensor(msg[:, par, CB:2 * CB, :], td[:, par, :, 0:HID],
                                  td[:, par, :, HID:2 * HID], ALU.add).then_inc(b_add, 1)

            def sum_scores(b, par):
                dve.wait_ge(b_add, b + 1)
                dve.scalar_tensor_tensor(msg[:, par, :, :], msg[:, par, :, :], SLOPE, msg[:, par, :, :],
                                         ALU.mult, ALU.max).then_inc(b_leak, 1)
                dve.wait_ge(b_leak, b + 1)
                dve.tensor_tensor(msg[:, par, :, :], msg[:, par, :, :],
                                  att_bc[:, :].unsqueeze(1).broadcast_to([P, 2 * CB, HID]),
                                  ALU.mult).then_inc(b_mul, 1)
                dve.wait_ge(b_mul, b + 1)
                for kind in range(2):
                    dve.tensor_reduce(
                        pe_pair[:, kind, :, bass.ds(CB * b, CB)].rearrange("p h c -> p c h"),
                        msg[:, par, CB * kind:CB * (kind + 1), :].rearrange("p c (h d) -> p c h d", h=H),
                        AX.X, ALU.add).then_inc(b_red, 1)

            add_messages(0, 0)
            add_messages(1, 1)
            sum_scores(0, 0)
            with dve.Fori(1, NB // 2) as i:
                add_messages(2 * i, 0)
                sum_scores(2 * i - 1, 1)
                add_messages(2 * i + 1, 1)
                sum_scores(2 * i, 0)
            sum_scores(NB - 1, 1)
            dve.wait_ge(b_red, 2 * NB)
            dve.tensor_tensor(pexp[:, 0, :, :], pe_pair[:, 0, :, :], pe_pair[:, 1, :, :], ALU.max
                              ).then_inc(b_max, 1)
            for q in range(2):
                dve.wait_ge(b_max_t, q + 1)
                dve.tensor_copy(max_t[:, q, :], bank[q][0:2 * NC, 0:P]).then_inc(b_max, 1)
            dve.wait_ge(b_rows, 32)
            dve.tensor_tensor_scan(max_row[:, :], fresh[:, 0:E], max_row[:, :], FAR, ALU.add, ALU.max
                                   ).then_inc(b_scan, 1)
            dve.wait_ge(b_scan, 1)
            dve.tensor_tensor_scan(max_row[:, ::-1], fresh[:, E:0:-1], max_row[:, ::-1], FAR, ALU.add, ALU.max
                                   ).then_inc(b_scan, 1)
            for kind in range(2):
                dve.wait_ge(b_back, 2)
                dve.tensor_tensor(pe_pair[:, kind, :, :], pe_pair[:, kind, :, :],
                                  bank[2][0:P, 0:H * NC].rearrange("p (h c) -> p h c", h=H),
                                  ALU.subtract).then_inc(b_max, 1)
            dve.wait_ge(b_max, 5)
            dve.tensor_copy(tot[:, :, :], pe_pair[:, 0, :, 0:CB]).then_inc(b_max, 1)

            dve.wait_ge(b_exp, 1)

            def weigh(b, par):
                wait(dve, b_l, b - 1)
                rows = xls[:, bass.ds(CB * b, CB), :].rearrange("p c (h d) -> p c h d", h=H)
                dve.tensor_tensor(rows, rows,
                                  pexp[:, 0, :, bass.ds(CB * b, CB)].rearrange("p h c -> p c h").unsqueeze(3)
                                  .broadcast_to([P, CB, H, HD]), ALU.mult)
                dve.tensor_tensor(zmat[:, par, :, :], zsel[:, bass.ds(CB * b, CB), :],
                                  eq_last[:, bass.ds(CB * b, CB)].unsqueeze(2).broadcast_to([P, CB, NC]),
                                  ALU.mult).then_inc(b_v, 1)

            dve.wait_ge(b_zsel, 2)
            weigh(0, 0)
            weigh(1, 1)
            with dve.Fori(1, NB // 2) as i:
                for par in range(2):
                    weigh(2 * i + par, par)
            dve.wait_ge(b_l, NB)
            dve.tensor_copy(lsb[:, 0:HID], bank[3][0:NC, 0:HID])
            dve.tensor_copy(lsb[:, HID:HID + H], bank[4][0:NC, 0:H]).then_inc(b_lsb, 1)

            def same_segment(b, par):
                wait(dve, b_num, b - 1)
                dve.tensor_tensor(smat[:, par, :, :],
                                  dst_row[:, bass.ds(CB * P * b, CB * P)].rearrange("p (c e) -> p c e", c=CB),
                                  dst_col[:, bass.ds(CB * b, CB)].unsqueeze(2).broadcast_to([P, CB, P]),
                                  ALU.is_equal)
                dve.scalar_tensor_tensor(
                    bmat[:, par, :, :],
                    dst_row[0:NC, bass.ds(CB * P * b, CB * P)].rearrange("p (c e) -> p c e", c=CB),
                    last_of_chunk[:, 0:1],
                    earlier[:, bass.ds(CB * b, CB)].unsqueeze(2).broadcast_to([NC, CB, P]),
                    ALU.is_equal, ALU.mult).then_inc(b_sb, 1)

            def finish(b, par):
                own = pexp[:, 1, :, bass.ds(CB * b, CB)]
                dve.wait_ge(b_num, b + 1)
                dve.scalar_tensor_tensor(tot[:, :, :],
                                         bank[2 + 5 * par][0:P, 0:CB * H].rearrange("p (c h) -> p h c", h=H),
                                         1e-16, own, ALU.add, ALU.add).then_inc(b_den, 1)
                dve.wait_ge(b_den, 3 * b + 1)
                dve.reciprocal(rden[:, :, :], tot[:, :, :]).then_inc(b_den, 1)
                dve.wait_ge(b_den, 3 * b + 2)
                wait(dve, b_self, b - 1)
                dve.tensor_tensor(psr[:, par, :, :], own, rden[:, :, :], ALU.mult).then_inc(b_scaled, 1)
                wait(dve, rows_stored[par], 8 * (b - par))
                for q in range(CB):
                    num = bank[5 * par + q // 2][0:P, HID * (q % 2):HID * (q % 2 + 1)]
                    last = dve.tensor_tensor(
                        orow[:, par, q, :].rearrange("p (h d) -> p h d", h=H),
                        num.rearrange("p (h d) -> p h d", h=H),
                        rden[:, :, q:q + 1].broadcast_to([P, H, HD]), ALU.mult)
                last.then_inc(b_den, 1)
                dve.wait_ge(b_den, 3 * b + 3)
                dve.wait_ge(b_self, b + 1)
                dve.tensor_tensor(orow[:, par, :, :], orow[:, par, :, :], xld[:, bass.ds(CB * b, CB), :],
                                  ALU.add).then_inc(b_out, 1)

            same_segment(0, 0)
            same_segment(1, 1)
            finish(0, 0)
            same_segment(2, 0)
            finish(1, 1)
            with dve.Fori(1, NB // 2 - 1) as i:
                same_segment(2 * i + 1, 1)
                finish(2 * i, 0)
                same_segment(2 * i + 2, 0)
                finish(2 * i + 1, 1)
            same_segment(NB - 1, 1)
            finish(NB - 2, 0)
            finish(NB - 1, 1)

            def low_agg(m, g):
                dve.wait_ge(c_ahi, KH * g + m + 1)
                dve.tensor_tensor(aggt_lo[:, m, :], Y[1][:, 0:G], aggt_hi[:, m, :].bitcast(F32),
                                  ALU.subtract).then_inc(c_alo, 1)

            def residual(g, par, u):
                j, n = u // 2, u % 2
                if u == 0:
                    dve.wait_ge(cx_loaded[par], 16 * (g + 2 - par))
                dve.wait_ge(c_up, 8 * g + u + 1)
                piece = cx[:, par, j, HALF * n:HALF * (n + 1)]
                dve.tensor_tensor(piece, piece, Y[(u + 1) % 2][0:P, :], ALU.add).then_inc(c_upv, 1)

            def bn_c(g, par, u):
                if u == 0:
                    wait(dve, c_aggr, g)
                dve.wait_ge(c_upv, 8 * g + u + 1)
                bn(g, par, u, cx[:, par, u // 2, :], c_bn)

            def moments_c(g, par):
                moments(g, par, c_bn, c_aggr, c_var, 1.0, LN_EPS)

            def low1(g, m):
                dve.wait_ge(c_h1hi, MF * g + m + 1)
                dve.tensor_tensor(h_lo[:, m, :], gl[:, m % 2, :], h_hi[:, m, :].bitcast(F32),
                                  ALU.subtract).then_inc(c_h1lo, 1)

            def low2(g, m):
                dve.wait_ge(c_h2hi, MF * g + m + 1)
                dve.tensor_tensor(h_lo[:, m, :], gl[:, m % 2, :], h_hi[:, m, :].bitcast(F32),
                                  ALU.subtract).then_inc(c_h2lo, 1)

            def weight(g, m):
                dve.wait_ge(c_g2, MF * g + m + 1)
                dve.wait_ge(c_wx, MF * g + m + 1)
                dve.tensor_tensor(gl[:, m % 2, :], gl[:, m % 2, :], T_C[m % 2][:, 0:G],
                                  ALU.mult).then_inc(c_wmul, 1)

            def route(g):
                dve.wait_ge(c_rs, g + 1)
                dve.tensor_copy(score[:, :, :], T_C[0][0:P, 0:J * NE].rearrange("p (j e) -> p j e", e=NE)
                                ).then_inc(c_rt, 1)
                dve.wait_ge(c_rt, 4 * g + 1)
                other = score[:, :, :].unsqueeze(2).broadcast_to([P, J, NE, NE])
                own = score[:, :, :].unsqueeze(3).broadcast_to([P, J, NE, NE])
                dve.tensor_tensor(beats[:, :, :, :], other, own, ALU.is_gt)
                dve.tensor_tensor(beats2[:, :, :, :], other, own, ALU.is_equal).then_inc(c_rt, 1)
                dve.wait_ge(c_rt, 4 * g + 2)
                dve.tensor_tensor(beats2[:, :, :, :], beats2[:, :, :, :],
                                  tie[:, :, :].unsqueeze(1).broadcast_to([P, J, NE, NE]), ALU.mult
                                  ).then_inc(c_rt, 1)
                dve.wait_ge(c_rt, 4 * g + 3)
                dve.tensor_tensor(beats[:, :, :, :], beats[:, :, :, :], beats2[:, :, :, :], ALU.add
                                  ).then_inc(c_rt, 1)
                dve.wait_ge(c_rt, 4 * g + 4)
                dve.tensor_reduce(rank[:, :, :], beats[:, :, :, :], AX.X, ALU.add).then_inc(c_w, 1)
                dve.wait_ge(c_w, 3 * g + 1)
                for a in range(2):
                    dve.tensor_scalar(wdup[:, :, a, :], rank[:, :, :], 2.0, 0.5, ALU.is_lt, ALU.mult
                                      ).then_inc(c_w, 1)

            def weights_t(g):
                dve.wait_ge(c_wtp, g + 1)
                wait(dve, c_w3, 8 * g)
                dve.tensor_copy(w_t[:, :], T_C[1][0:2 * NE, 0:G]).then_inc(c_wt, 1)

            def result(g, par, u):
                j, n = u // 2, u % 2
                dve.wait_ge(c_w3, 8 * g + u + 1)
                piece = cx[:, par, j, HALF * n:HALF * (n + 1)]
                dve.tensor_tensor(piece, piece, Y[(u + 1) % 2][0:P, :], ALU.add).then_inc(c_w3v, 1)

            def body_c(g, par):
                nxt, npar, more = g + 1, 1 - par, has(g, 1)
                for k in range(KD):
                    dve.wait_ge(c_hi, KD * g + k + 1)
                    dve.tensor_tensor(cxt_lo[:, k % 2, :], T_C[k % 2][:, 0:G],
                                      cxt_hi[:, k % 2, :].bitcast(F32), ALU.subtract).then_inc(c_lo, 1)
                    if k in (3, 6) and more:
                        low_agg(k // 6, nxt)
                dve.wait_ge(c_mm, KD * (g + 1))
                wait(dve, c_rs, g)
                dve.tensor_copy(sc_t[:, :], Y[0][0:2 * NE, 0:G]).then_inc(c_sc, 1)
                low1(g, 0)
                if more:
                    residual(nxt, npar, 0)
                low1(g, 1)
                if more:
                    residual(nxt, npar, 1)
                low1(g, 2)
                route(g)
                if more:
                    residual(nxt, npar, 2)
                low1(g, 3)
                if more:
                    residual(nxt, npar, 3)
                weights_t(g)
                for m in range(MF):
                    if more:
                        residual(nxt, npar, 4 + m)
                    weight(g, m)
                    if m >= 1:
                        low2(g, m - 1)
                low2(g, MF - 1)
                for u in range(8):
                    if more:
                        bn_c(nxt, npar, u)
                    if more and u == 7:
                        moments_c(nxt, npar)
                    if u < 5:
                        result(g, par, u)
                if more:
                    bias_of(nxt, npar, c_rstd, c_nb)
                for u in range(5, 8):
                    result(g, par, u)

            for m in range(KH):
                low_agg(m, 0)
            for u in range(8):
                residual(0, 0, u)
                bn_c(0, 0, u)
            moments_c(0, 0)
            bias_of(0, 0, c_rstd, c_nb)
            dve.wait_ge(w3_split_s, 1)
            dve.tensor_tensor(w2_lo[:, :, :], w2_raw[:, :, :], w2_hi[:, :, :].bitcast(F32), ALU.subtract)
            dve.tensor_tensor(w3_lo[:, :, :], w3_raw[:, :, :], w3_hi[:, :, :].bitcast(F32), ALU.subtract
                              ).then_inc(w3_split_v, 1)
            pairs(dve, body_c)

        @block.tensor
        def _(pe):
            def product(out_ap, left, right, start, stop):
                pe.matmul(out_ap, left[0], right[0], start=start, stop=False, skip_group_check=True)
                pe.matmul(out_ap, left[0], right[1], start=False, stop=False, skip_group_check=True)
                return pe.matmul(out_ap, left[1], right[0], start=False, stop=stop, skip_group_check=True)

            def small_setup():
                pe.wait_ge(consts, 2)
                pe.wait_ge(setup_v, 3)
                for n in range(3):
                    last = pe.transpose(bank[0][0:P, NC * n:NC * (n + 1)], idx_f[:, n, :], ident[0:NC, 0:NC])
                last.then_inc(setup_t, 1)
                pe.wait_ge(raw_small, 16 * 6)
                for k in range(KD):
                    last = pe.transpose(bank[1][:, NE * k:NE * (k + 1)], tok_rows[:, 128 * k:128 * (k + 1)],
                                        ident[0:NE, 0:NE])
                last.then_inc(setup_t, 1)

            small_setup()
            pe.wait_ge(setup_v, 11)

            def turn(g, par, k):
                t = KD * g + k
                wait(pe, a_lo, t - 3)
                if k == 0:
                    pe.wait_ge(a_xn, J * (g + 1))
                for j in range(J):
                    last = pe.transpose(T_A[k % 4][:, P * j:P * (j + 1)], axn[:, par, j, 128 * k:128 * (k + 1)],
                                        ident[0:P, 0:P])
                last.then_inc(a_tp, 1)

            def left_right(g, par, j):
                if j == 0:
                    pe.wait_ge(a_hlo, KH * (g + 1))
                wait(pe, a_ev_s if j % 2 == 0 else a_ev_v, 2 * g + j // 2)
                for m in range(KH):
                    rows = slice(P * j, P * (j + 1))
                    last = product(X_A[j % 2][0:P, :], (ht_hi[:, par, m, rows], ht_lo[:, par, m, rows]),
                                   (wlr_hi[:, m, :], wlr_lo[:, m, :]), m == 0, m == KH - 1)
                last.then_inc(a_lr, 1)

            def body(g, par):
                for k in range(KD):
                    if k + 2 < KD:
                        turn(g, par, k + 2)
                    pe.wait_ge(a_lo, KD * g + k + 1)
                    if k == 0:
                        wait(pe, a_hlo, KH * g)
                    for m in range(KH):
                        cols = slice(128 * m, 128 * (m + 1))
                        last = product(H_A[m][:, 0:G], (wd_hi[:, k, cols], wd_lo[:, k, cols]),
                                       (axt_hi[:, k % 4, :], axt_lo[:, k % 4, :]), k == 0, k == KD - 1)
                    last.then_inc(a_mm, 1)
                for j in range(J):
                    if has(g, -1):
                        left_right(g - 1, 1 - par, j)
                    if j % 2 == 1 and has(g, 1):
                        turn(g + 1, 1 - par, j // 2)

            turn(0, 0, 0)
            turn(0, 0, 1)
            pairs(pe, body)
            for j in range(J):
                left_right(NG - 1, 1, j)

            pe.wait_ge(b_max, 1)
            for q in range(2):
                pe.transpose(bank[q][0:2 * NC, 0:P], pexp[:, 0, 2 * q:2 * q + 2, :].rearrange("p h c -> p (h c)"),
                             ident[0:P, 0:P]).then_inc(b_max_t, 1)
            pe.wait_ge(b_rows, 64)
            for q in range(2):
                pe.transpose(bank[2][0:P, 2 * NC * q:2 * NC * (q + 1)], max_t[:, q, :],
                             ident[0:2 * NC, 0:2 * NC]).then_inc(b_back, 1)

            def last_segments(b, par):
                pe.wait_ge(b_v, b + 1)
                first = isinstance(b, int) and b == 0
                final = isinstance(b, int) and b == NB - 1
                for q in range(CB):
                    z = zmat[:, par, q, :]
                    pe.matmul(bank[3][0:NC, 0:HID], z,
                              xls[:, bass.ds(CB * b + q, 1), :].rearrange("p c d -> p (c d)"),
                              start=first and q == 0, stop=final and q == CB - 1, skip_group_check=True)
                    last = pe.matmul(bank[4][0:NC, 0:H], z,
                                     pexp[:, 0, :, bass.ds(CB * b + q, 1)].rearrange("p h c -> p (h c)"),
                                     start=first and q == 0, stop=final and q == CB - 1, skip_group_check=True)
                last.then_inc(b_l, 1)

            last_segments(0, 0)
            last_segments(1, 1)
            with pe.Fori(1, NB // 2 - 1) as i:
                for par in range(2):
                    last_segments(2 * i + par, par)
            last_segments(NB - 2, 0)
            last_segments(NB - 1, 1)

            def segment_sums(b, par):
                pe.wait_ge(b_sb, b + 1)
                wait(pe, b_out, b - 1)
                for q in range(CB):
                    num = bank[5 * par + q // 2][0:P, HID * (q % 2):HID * (q % 2 + 1)]
                    den = bank[2 + 5 * par][0:P, H * q:H * (q + 1)]
                    pe.matmul(num, smat[:, par, q, :],
                              xls[:, bass.ds(CB * b + q, 1), :].rearrange("p c d -> p (c d)"),
                              start=True, stop=False, skip_group_check=True)
                    pe.matmul(num, bmat[:, par, q, :], lsb[:, 0:HID], start=False, stop=True,
                              skip_group_check=True)
                    pe.matmul(den, smat[:, par, q, :],
                              pexp[:, 0, :, bass.ds(CB * b + q, 1)].rearrange("p h c -> p (h c)"),
                              start=True, stop=False, skip_group_check=True)
                    last = pe.matmul(den, bmat[:, par, q, :], lsb[:, HID:HID + H], start=False, stop=True,
                                     skip_group_check=True)
                last.then_inc(b_num, 1)

            pe.wait_ge(b_lsb, 1)
            segment_sums(0, 0)
            segment_sums(1, 1)
            with pe.Fori(1, NB // 2) as i:
                for par in range(2):
                    segment_sums(2 * i + par, par)

            def turn_c(g, k):
                t = KD * g + k
                if k >= 2:
                    pe.wait_ge(c_lo, t - 1)
                else:
                    wait(pe, c_wmul, MF * g - 1 + k)
                if k == 0:
                    pe.wait_ge(c_xn, J * (g + 1))
                for j in range(J):
                    last = pe.transpose(T_C[k % 2][:, P * j:P * (j + 1)], cxn[:, j, 128 * k:128 * (k + 1)],
                                        ident[0:P, 0:P])
                last.then_inc(c_tp, 1)

            def turn_agg(g, m):
                if m == 0:
                    pe.wait_ge(agg_loaded, 16 * J * (g + 1))
                    wait(pe, c_w3v, 8 * (g - 1))
                else:
                    pe.wait_ge(c_alo, KH * g + m)
                for j in range(J):
                    last = pe.transpose(Y[1][:, P * j:P * (j + 1)], agg[:, j, 128 * m:128 * (m + 1)],
                                        ident[0:P, 0:P])
                last.then_inc(c_atp, 1)

            def up(g, u):
                j, n = u // 2, u % 2
                if u == 0:
                    pe.wait_ge(c_alo, KH * (g + 1))
                elif u == 1:
                    wait(pe, c_sc, g)
                else:
                    pe.wait_ge(c_upv, 8 * g + u - 1)
                for m in range(KH):
                    rows, cols = slice(P * j, P * (j + 1)), slice(HALF * n, HALF * (n + 1))
                    last = product(Y[(u + 1) % 2][0:P, :], (aggt_hi[:, m, rows], aggt_lo[:, m, rows]),
                                   (wup_hi[:, m, cols], wup_lo[:, m, cols]), m == 0, m == KH - 1)
                last.then_inc(c_up, 1)

            def hidden1(g, k):
                pe.wait_ge(c_lo, KD * g + k + 1)
                if k == 0:
                    wait(pe, c_g2, MF * g)
                for m in range(MF):
                    cols = slice(128 * m, 128 * (m + 1))
                    product(ACC[m][:, 0:G], (w1_hi[:, k, cols], w1_lo[:, k, cols]),
                            (cxt_hi[:, k % 2, :], cxt_lo[:, k % 2, :]), k == 0, k == KD - 1)
                if k == 0:
                    wait(pe, c_w3v, 8 * g)
                pe.matmul(Y[0][:, 0:G], tok_st[:, k, :], cxt_hi[:, k % 2, :], start=k == 0, stop=False,
                          skip_group_check=True)
                pe.matmul(Y[0][:, 0:G], tok_st[:, k, :], cxt_lo[:, k % 2, :], start=False, stop=k == KD - 1,
                          skip_group_check=True).then_inc(c_mm, 1)

            def score_rows(g):
                pe.wait_ge(c_sc, g + 1)
                for j in range(J):
                    last = pe.matmul(T_C[0][0:P, NE * j:NE * (j + 1)], sc_t[:, P * j:P * (j + 1)], comb[:, :],
                                     start=True, stop=True, skip_group_check=True)
                last.then_inc(c_rs, 1)

            def hidden2(g, m):
                pe.wait_ge(c_h1lo, MF * g + m + 1)
                product(ACC[m][:, 0:G], (w2_hi[:, m, :], w2_lo[:, m, :]), (h_hi[:, m, :], h_lo[:, m, :]),
                        True, True).then_inc(c_w2, 1)

            def weights_rows(g):
                pe.wait_ge(c_w, 3 * (g + 1))
                for j in range(J):
                    last = pe.transpose(T_C[1][0:2 * NE, P * j:P * (j + 1)],
                                        wdup[:, j, :, :].rearrange("p a e -> p (a e)"), ident[0:P, 0:P])
                last.then_inc(c_wtp, 1)

            def spread(g, m):
                if m == 0:
                    pe.wait_ge(c_wt, g + 1)
                if m >= 2:
                    pe.wait_ge(c_wmul, MF * g + m - 1)
                pe.matmul(T_C[m % 2][:, 0:G], expand[:, 128 * m:128 * (m + 1)], w_t[0:NE, :], start=True,
                          stop=True, skip_group_check=True).then_inc(c_wx, 1)

            def down(g, u, first_wait):
                j, n = u // 2, u % 2
                if u == 0:
                    pe.wait_ge(c_h2lo, MF * (g + 1))
                if u < 2:
                    if first_wait:
                        pe.wait_ge(c_upv, 8 * (g + 1) + 7 + u)
                else:
                    pe.wait_ge(c_w3v, 8 * g + u - 1)
                rows, cols = slice(P * j, P * (j + 1)), slice(HALF * n, HALF * (n + 1))
                y = Y[(u + 1) % 2][0:P, :]
                pe.matmul(y, w_t[:, rows], b3_hl[:, cols], start=True, stop=False, skip_group_check=True)
                for m in range(MF):
                    last = product(y, (h_hi[:, m, rows], h_lo[:, m, rows]), (w3_hi[:, m, cols], w3_lo[:, m, cols]),
                                   False, m == MF - 1)
                last.then_inc(c_w3, 1)

            def body_c(g, par):
                more = has(g, 1)
                for k in range(KD):
                    if k + 1 < KD:
                        turn_c(g, k + 1)
                    hidden1(g, k)
                    if k in (2, 5) and more:
                        turn_agg(g + 1, k // 5)
                if more:
                    up(g + 1, 0)
                    up(g + 1, 1)
                score_rows(g)
                if more:
                    up(g + 1, 2)
                    up(g + 1, 3)
                for m in range(MF):
                    hidden2(g, m)
                weights_rows(g)
                for m in range(MF):
                    if more:
                        up(g + 1, 4 + m)
                    spread(g, m)
                for u in range(8):
                    if u == 6 and more:
                        turn_c(g + 1, 0)
                    down(g, u, more)

            pe.wait_ge(b_split_v, 4)
            for m in range(KH):
                turn_agg(0, m)
            for u in range(8):
                up(0, u)
            turn_c(0, 0)
            pe.wait_ge(w3_split_v, 1)
            pairs(pe, body_c)


_INS = ["x", "src", "dst", "L0_gnn_rms_w", "L0_gnn_W_down", "L0_gnn_Wl", "L0_gnn_Wr", "L0_gnn_att", "L0_gnn_W_up",
        "L0_ffn_expert_tokens", "L0_ffn_W1", "L0_ffn_b1", "L0_ffn_W2", "L0_ffn_b2", "L0_ffn_W3", "L0_ffn_b3"]


def kernel(**inputs):
    import numpy as np
    import concourse.bacc as bacc
    from concourse.bass_utils import run_bass_kernel_spmd

    nc = bacc.Bacc("TRN2", target_bir_lowering=False, num_devices=1)
    arrays, args = {}, []
    for name in _INS:
        a = np.ascontiguousarray(inputs[name])
        arrays[f"in_{name}"] = a
        args.append(nc.dram_tensor(f"in_{name}", a.shape, mybir.dt.from_np(a.dtype), kind="ExternalInput").ap())
    args.append(nc.dram_tensor("out_0", (N, D), F32, kind="ExternalOutput").ap())
    build(nc, *args)
    r = run_bass_kernel_spmd(nc, [arrays], core_ids=[0])
    return r.results[0]["out_0"]
```

```python
from contextlib import ExitStack

import concourse.bass as bass
from concourse import mybir

N, D = 10000, 1024
E = 5000
HID, H = 256, 4
HD = HID // H
NE, EH = 8, 64
P, J = 125, 4
G = P * J
NG = N // G
KD = D // 128
KH = HID // 128
MF = NE * EH // 128
HALF = 512
NC = E // P
CB = 4
NB = NC // CB
SPLIT = 112
LN_EPS, RMS_EPS = 1e-5, 1e-6
SLOPE = 0.2
TABLE = N + E // 2
CPG = NC // NG
MAPW = 100
FAR = -3.0e38

F32, F32R, BF16, I32 = mybir.dt.float32, mybir.dt.float32r, mybir.dt.bfloat16, mybir.dt.int32
ALU = mybir.AluOpType
ACT = mybir.ActivationFunctionType
AX = mybir.AxisListType


def wait(engine, sem, value):
    if isinstance(value, int) and value <= 0:
        return
    engine.wait_ge(sem, value)


def build(nc, x, src, dst, rms_w, w_down, wl, wr, att, w_up, tok, w1, b1, w2, b2, w3, b3, out):
    ctx = ExitStack()
    with ctx:
        base = [(nc.sbuf_base + 31) // 32 * 32]
        origin = base[0]

        def put(name, shape, dt, at):
            return nc.alloc_sbuf_tensor_at(name, shape, dt, offset=origin + at)

        def run_of(at, *items):
            made = []
            for name, shape, dt in items:
                made.append(put(name, shape, dt, at))
                size = 2 if dt == BF16 else 4
                for n in shape[1:]:
                    size *= n
                at += (size + 31) // 32 * 32
            return (*made, at)

        def sem(name):
            return ctx.enter_context(nc.semaphore(name))

        bank = [ctx.enter_context(nc.psum_tensor(f"bank{i}", [128, HALF], F32)) for i in range(8)]
        table = nc.dram_tensor("node_table", [TABLE, 2 * HID], F32)
        where_from = nc.dram_tensor("where_from", [N + P, 1], I32)

        (ident, rmsw, b1c, b2c, neg_half, dup_mask, dup_rest, dst_col, dst_next_col, src_idx, dst_idx,
         scat_idx, row_of_edge, idx_now, row_now, from_idx, trash, last_of_chunk, eq_last, earlier, pe_pair, pexp, lsb, tie, at0) = run_of(
            0,
            ("ident", [128, 128], F32), ("rmsw", [128, KD], F32),
            ("b1c", [128, MF], F32), ("b2c", [128, MF], F32), ("neg_half", [P, J], F32),
            ("dup_mask", [2 * NE, 1], F32), ("dup_rest", [2 * NE, 1], F32),
            ("dst_col", [P, NC], F32), ("dst_next_col", [P, NC], F32), ("src_idx", [P, NC], I32),
            ("dst_idx", [P, NC], I32), ("scat_idx", [P, NC], I32), ("row_of_edge", [P, NC], I32), ("idx_now", [P, J], I32),
            ("row_now", [P, CPG], I32), ("from_idx", [P, NG, J], I32), ("trash", [P, 1], F32),
            ("last_of_chunk", [NC, 1], F32), ("eq_last", [P, NC], F32), ("earlier", [NC, NC], F32),
            ("pe_pair", [P, 2, H, NC], F32), ("pexp", [P, 2, H, NC], F32), ("lsb", [NC, HID + H], F32), ("tie", [P, NE, NE], F32))
        (att_bc, stat, mv, var, rstd, nbias, tok_st, b3_hl, expand, at1) = run_of(
            at0,
            ("att_bc", [P, HID], F32), ("stat", [P, J, 12], F32), ("mv", [P, 2, J, 2], F32),
            ("var", [P, 2, J], F32), ("rstd", [P, 2, J], F32), ("nbias", [P, 2, J], F32),
            ("tok_st", [128, KD, 128], F32R), ("b3_hl", [2 * NE, D], F32R), ("expand", [NE, NE * EH], F32R))

        wup_hi, wup_lo, w1_hi, w1_lo, at2 = run_of(
            at1,
            ("wup_hi", [128, KH, D], F32R), ("wup_lo", [128, KH, D], F32R),
            ("w1_hi", [128, KD, HALF], F32R), ("w1_lo", [128, KD, HALF], F32R))
        wup_raw = put("wup_raw", [128, KH, D], F32, at1 + KH * D * 4)
        w1_raw = put("w1_raw", [128, KD, HALF], F32, at1 + 2 * KH * D * 4 + KD * HALF * 4)
        w2_hi, w2_lo, w3_hi, w3_lo, at3 = run_of(
            at2,
            ("w2_hi", [128, MF, 128], F32R), ("w2_lo", [128, MF, 128], F32R), ("w3_hi", [128, MF, D], F32R), ("w3_lo", [128, MF, D], F32R))
        w2_raw = put("w2_raw", [128, MF, 128], F32, at2 + MF * 128 * 4)
        w3_raw = put("w3_raw", [128, MF, D], F32, at3 - MF * D * 4)

        (ax, axn, axt_hi, axt_lo, ht_hi, ht_lo, trow, wd_hi, wd_lo, wlr_hi, wlr_lo, a_end) = run_of(
            at2,
            ("ax", [P, 2, J * D], F32), ("axn", [P, 2, J, D], F32),
            ("axt_hi", [128, 4, G], F32R), ("axt_lo", [128, 4, G], F32R),
            ("ht_hi", [128, 2, KH, G], F32R), ("ht_lo", [128, 2, KH, G], F32R),
            ("trow", [P, 2, J * 2 * HID], F32),
            ("wd_hi", [128, KD, HID], F32R), ("wd_lo", [128, KD, HID], F32R),
            ("wlr_hi", [128, KH, 2 * HID], F32R), ("wlr_lo", [128, KH, 2 * HID], F32R))
        wd_raw = put("wd_raw", [128, KD, HID], F32, a_end - 2 * KH * 2 * HID * 4 - KD * HID * 4)
        wlr_raw = put("wlr_raw", [128, KH, 2 * HID], F32, a_end - KH * 2 * HID * 4)
        (idx_rows, idx_f, tok_rows, b3_raw, b3_hi, b3_lo, expand_raw, own_rows, _) = run_of(
            at1,
            ("idx_rows", [NC, 3, P], I32), ("idx_f", [NC, 3, P], F32), ("tok_rows", [NE, D], F32),
            ("b3_raw", [2 * NE, D], F32), ("b3_hi", [2 * NE, D], F32R), ("b3_lo", [2 * NE, D], F32),
            ("expand_raw", [NE, NE * EH], F32), ("own_rows", [MAPW, N // MAPW], I32))

        xls, xld, dst_row, at4 = run_of(
            at2, ("xls", [P, NC, HID], F32), ("xld", [P, NC, HID], F32), ("dst_row", [P, E], I32))
        td, msg, at5 = run_of(
            at4, ("td", [P, 2, CB, 2 * HID], F32), ("msg", [P, 2, 2 * CB, HID], F32))
        fresh, b_end = run_of(at5, ("fresh", [H, E + 8], BF16))
        max_row, max_t, _ = run_of(at4, ("max_row", [H, E], F32), ("max_t", [NC * 2, 2, P], F32))
        (zsel, zmat, smat, bmat, orow, tot, rden, psr, _) = run_of(
            at4,
            ("zsel", [P, NC, NC], F32), ("zmat", [P, 2, CB, NC], F32), ("smat", [P, 2, CB, P], F32),
            ("bmat", [NC, 2, CB, P], F32), ("orow", [P, 2, CB, HID], F32), ("tot", [P, H, CB], F32),
            ("rden", [P, H, CB], F32), ("psr", [P, 2, H, CB], F32))

        (cx, cxn, cxt_hi, cxt_lo, gl, h_hi, h_lo, agg, aggt_hi, aggt_lo, sc_t, w_t, score, beats, beats2, rank,
         wdup, c_end) = run_of(
            at3,
            ("cx", [P, 2, J, D], F32), ("cxn", [P, J, D], F32),
            ("cxt_hi", [128, 2, G], F32R), ("cxt_lo", [128, 2, G], F32R), ("gl", [128, MF, G], F32),
            ("h_hi", [128, MF, G], F32R), ("h_lo", [128, MF, G], F32R), ("agg", [P, J, HID], F32),
            ("aggt_hi", [128, KH, G], F32R), ("aggt_lo", [128, KH, G], F32R),
            ("sc_t", [128, G], F32), ("w_t", [2 * NE, G], F32R), ("score", [P, J, NE], F32),
            ("beats", [P, J, NE, NE], F32), ("beats2", [P, J, NE, NE], F32), ("rank", [P, J, NE], F32),
            ("wdup", [P, J, 2, NE], F32))
        assert origin + max(a_end, b_end, c_end, at3) <= nc.sbuf_usable_end, (a_end, b_end, c_end)

        consts = sem("consts")
        raw_idx, raw_small, raw_wa, raw_wlr, raw_wc = (
            sem("raw_idx"), sem("raw_small"), sem("raw_wa"), sem("raw_wlr"), sem("raw_wc"))
        raw_dst_row, raw_w3 = sem("raw_dst_row"), sem("raw_w3")
        setup_v, setup_t, setup_s, setup_p = sem("setup_v"), sem("setup_t"), sem("setup_s"), sem("setup_p")
        first_loaded = [sem(f"first_loaded{j}") for j in range(J)]
        ax_loaded = [sem("ax_loaded0"), sem("ax_loaded1")]
        a_bn, a_aggr, a_var, a_rstd, a_nb = sem("a_bn"), sem("a_aggr"), sem("a_var"), sem("a_rstd"), sem("a_nb")
        a_xn, a_tp, a_hi, a_lo, a_mm = sem("a_xn"), sem("a_tp"), sem("a_hi"), sem("a_lo"), sem("a_mm")
        a_hhi, a_hlo, a_lr = sem("a_hhi"), sem("a_hlo"), sem("a_lr")
        a_ev_s, a_ev_v = sem("a_ev_s"), sem("a_ev_v")
        t_stored = [sem("t_stored0"), sem("t_stored1")]
        gathered = [sem("gathered0"), sem("gathered1")]
        b_split_s, b_split_v, b_fresh = sem("b_split_s"), sem("b_split_v"), sem("b_fresh")
        b_add, b_xld, b_leak, b_mul, b_red = sem("b_add"), sem("b_xld"), sem("b_leak"), sem("b_mul"), sem("b_red")
        b_max, b_max_t, b_rows, b_scan, b_back, b_exp = (
            sem("b_max"), sem("b_max_t"), sem("b_rows"), sem("b_scan"), sem("b_back"), sem("b_exp"))
        b_zsel, b_v, b_z, b_l, b_lsb = sem("b_zsel"), sem("b_v"), sem("b_z"), sem("b_l"), sem("b_lsb")
        b_sb, b_num, b_den, b_self, b_out = sem("b_sb"), sem("b_num"), sem("b_den"), sem("b_self"), sem("b_out")
        b_scaled = sem("b_scaled")
        map_copied, map_put, map_loaded = sem("map_copied"), sem("map_put"), sem("map_loaded")
        rows_stored = [sem("rows_stored0"), sem("rows_stored1")]
        cx_loaded = [[sem(f"cx_loaded{par}_{j}") for j in range(J)] for par in range(2)]
        out_stored = [[sem(f"out_stored{par}_{j}") for j in range(J)] for par in range(2)]
        agg_loaded = sem("agg_loaded")
        c_tp, c_mm, c_atp, c_up, c_rs, c_w2, c_wtp, c_wx, c_w3 = (
            sem("c_tp"), sem("c_mm"), sem("c_atp"), sem("c_up"), sem("c_rs"), sem("c_w2"), sem("c_wtp"),
            sem("c_wx"), sem("c_w3"))
        c_hi, c_ahi, c_g1, c_h1hi, c_g2, c_h2hi, c_xn = (
            sem("c_hi"), sem("c_ahi"), sem("c_g1"), sem("c_h1hi"), sem("c_g2"), sem("c_h2hi"), sem("c_xn"))
        c_lo, c_alo, c_sc, c_h1lo, c_upv, c_w3v, c_rt, c_w, c_wt, c_wmul, c_h2lo = (
            sem("c_lo"), sem("c_alo"), sem("c_sc"), sem("c_h1lo"), sem("c_upv"), sem("c_w3v"), sem("c_rt"),
            sem("c_w"), sem("c_wt"), sem("c_wmul"), sem("c_h2lo"))
        c_h1lo_p = sem("c_h1lo_p")
        c_bn, c_aggr, c_var, c_rstd, c_nb = sem("c_bn"), sem("c_aggr"), sem("c_var"), sem("c_rstd"), sem("c_nb")
        turns, turns_p = sem("turns"), sem("turns_p")
        w3_split_s, w3_split_v = sem("w3_split_s"), sem("w3_split_v")

        x_g = x.rearrange("(g p j) d -> g p (j d)", p=P, j=J)
        out_g = out.rearrange("(g p j) d -> g p (j d)", p=P, j=J)
        t_g = table[0:N, :].rearrange("(g p j) d -> g p (j d)", p=P, j=J)
        t_half = table[:, :].rearrange("n (a d) -> (n a) d", a=2)
        t_edge = t_half[2 * N:2 * N + E, :].rearrange("(c p) d -> p c d", p=P)

        T_A, H_A, X_A = bank[0:4], bank[4:6], bank[6:8]
        ACC, T_C, Y = bank[0:4], bank[4:6], bank[6:8]
        UP_BANK = [Y[1]] * 6 + [Y[0], Y[1]]
        DOWN_BANK = [Y[0], Y[1], ACC[0], ACC[1], ACC[2], ACC[3], Y[0], Y[1]]
        KU = 5

        block = ctx.enter_context(nc.Block())

        def pairs(engine, body, last=NG):
            for par in range(2):
                body(par, par)
            with engine.Fori(1, last // 2 - 1) as i:
                for par in range(2):
                    body(2 * i + par, par)
            for par in range(2):
                body(last - 2 + par, par)

        def has(g, more):
            return not isinstance(g, int) or 0 <= g + more < NG

        def halves(g):
            return g // 2 + 1 if isinstance(g, int) else None

        @block.sync
        def _(sp):
            def load_x(g, par):
                wait(sp, a_xn, J * (g - 1))
                sp.dma_start(ax[0:SPLIT, par, :], x_g[g, 0:SPLIT, :]).then_inc(ax_loaded[par], 16)
                sp.dma_start(ax[SPLIT:P, par, :], x_g[g, SPLIT:P, :]).then_inc(ax_loaded[par], 16)

            for j in range(J):
                for rows in (slice(0, SPLIT), slice(SPLIT, P)):
                    sp.dma_start(ax[rows, 0, D * j:D * (j + 1)], x_g[0, rows, D * j:D * (j + 1)]
                                 ).then_inc(first_loaded[j], 16)
            sp.dma_start(wd_raw[:, :, :], w_down.rearrange("(k p) n -> p k n", p=128)).then_inc(raw_wa, 16)
            sp.dma_start(rmsw[:, :], rms_w.rearrange("(k p) -> p k", p=128),
                         allow_slow_non_contiguous=True).then_inc(raw_wa, 16)
            load_x(1, 1)
            sp.dma_start(wlr_raw[:, :, 0:HID], wl.rearrange("(k p) n -> p k n", p=128)).then_inc(raw_wlr, 16)
            sp.dma_start(wlr_raw[:, :, HID:], wr.rearrange("(k p) n -> p k n", p=128)).then_inc(raw_wlr, 16)
            sp.wait_ge(consts, 1)
            sp.dma_start(idx_rows[:, 0, :], src.rearrange("(c p) -> c p", p=P)).then_inc(raw_idx, 16)
            sp.dma_start(idx_rows[:, 1, :], dst.rearrange("(c p) -> c p", p=P)).then_inc(raw_idx, 16)
            sp.dma_start(idx_rows[0:NC - 1, 2, :],
                         dst[1:1 + (NC - 1) * P].rearrange("(c p) -> c p", p=P)).then_inc(raw_idx, 16)
            sp.dma_start(idx_rows[NC - 1:NC, 2, 0:P - 1],
                         dst[1 + (NC - 1) * P:E].rearrange("(c p) -> c p", c=1)).then_inc(raw_idx, 16)
            sp.dma_start(tok_rows[:, :], tok).then_inc(raw_small, 16)
            sp.dma_start(b3_raw[0:NE, :], b3).then_inc(raw_small, 16)
            sp.dma_start(b3_raw[NE:2 * NE, :], b3).then_inc(raw_small, 16)
            sp.dma_start(att_bc[:, :], att.rearrange("h d -> (h d)").partition_broadcast(P)).then_inc(raw_small, 16)
            sp.dma_start(b1c[:, :], b1.rearrange("(m a) h -> (a h) m", a=2),
                         allow_slow_non_contiguous=True).then_inc(raw_small, 16)
            sp.dma_start(b2c[:, :], b2.rearrange("(m a) h -> (a h) m", a=2),
                         allow_slow_non_contiguous=True).then_inc(raw_small, 16)

            def body(g, par):
                if has(g, 2):
                    load_x(g + 2, par)

            pairs(sp, body)

            sp.wait_ge(map_put, 16 * (1 + NC))
            sp.dma_start(from_idx[:, :, :],
                         where_from[0:N, :].rearrange("(g p j) a -> p g (j a)", p=P, j=J)).then_inc(map_loaded, 16)

            sp.wait_ge(setup_v, 12)
            sp.wait_ge(consts, 3)
            sp.dma_start(wup_raw[:, :, :], w_up.rearrange("(k p) n -> p k n", p=128)).then_inc(raw_wc, 16)
            for k in range(KD):
                sp.dma_start(w1_raw[:, k, :].rearrange("p (e h) -> p e h", e=NE),
                             w1[:, 128 * k:128 * (k + 1), :].rearrange("e p h -> p e h")).then_inc(raw_wc, 16)
            for par in range(2):
                sp.wait_ge(t_stored[par], 32 * (NG // 2))
            sp.dma_start(dst_row[:, :], dst.partition_broadcast(P)).then_inc(raw_dst_row, 16)

            sp.wait_ge(b_max, 3)
            sp.wait_ge(b_xld, NB)
            for q in range(2):
                sp.dma_start(max_row[2 * q:2 * q + 2, :].rearrange("h (c p) -> h c p", p=P),
                             max_t[:, q, :]).then_inc(b_rows, 16)
            sp.wait_ge(b_scan, 2)
            for q in range(2):
                sp.dma_start(max_t[:, q, :],
                             max_row[2 * q:2 * q + 2, :].rearrange("h (c p) -> h c p", p=P)).then_inc(b_rows, 16)

            def store_rows(b, par):
                sp.wait_ge(b_out, b + 1)
                sp.dma_start(t_edge[:, bass.ds(CB * b, CB), :], orow[:, par, :, :]).then_inc(rows_stored[par], 16)

            with sp.Fori(0, NB // 2) as i:
                for par in range(2):
                    store_rows(2 * i + par, par)

            for par in range(2):
                sp.wait_ge(rows_stored[par], 16 * (NB // 2))

            def load_cx(g, par, j):
                for rows in (slice(0, SPLIT), slice(SPLIT, P)):
                    sp.dma_start(cx[rows, par, j, :], x_g[g, rows, D * j:D * (j + 1)]
                                 ).then_inc(cx_loaded[par][j], 16)

            for j in range(J):
                load_cx(0, 0, j)
            sp.dma_start(w3_raw[:, :, :], w3.rearrange("(m a) h n -> (a h) m n", a=2)).then_inc(raw_w3, 16)
            sp.wait_ge(consts, 4)
            w2_pairs = w2.rearrange("(m a) h k -> a h m k", a=2)
            for a in range(2):
                sp.dma_start(w2_raw[EH * a:EH * (a + 1), :, EH * a:EH * (a + 1)], w2_pairs[a]).then_inc(raw_w3, 16)
            for j in range(J):
                load_cx(1, 1, j)

            def body_c(g, par):
                def reload(j):
                    sp.wait_ge(out_stored[par][j], 16 * (g + 2 - par))
                    load_cx(g + 2, par, j)

                for j in range(J):
                    sp.wait_ge(c_w3v, 8 * g + 2 * j + 2)
                    for rows in (slice(0, SPLIT), slice(SPLIT, P)):
                        sp.dma_start(out_g[g, rows, D * j:D * (j + 1)], cx[rows, par, j, :]
                                     ).then_inc(out_stored[par][j], 16)
                    if j >= 1 and has(g, 2):
                        reload(j - 1)
                if has(g, 2):
                    reload(J - 1)

            pairs(sp, body_c)
            for par in range(2):
                for j in range(J):
                    sp.wait_ge(out_stored[par][j], 16 * NG)

        @block.gpsimd
        def _(pool):
            pool.memset(idx_rows[:, :, :], -1)
            pool.memset(tok_st[:, :, :].bitcast(F32), 0.0)
            pool.memset(ident[:, :], 0.0).then_inc(consts, 1)
            pool.wait_ge(consts, 1)
            pool.affine_select(out=ident[:, :], in_=ident[:, :], compare_op=ALU.not_equal, fill=1.0, base=0,
                               pattern=[[-1, 128]], channel_multiplier=1).then_inc(consts, 1)
            pool.memset(neg_half[:, :], -0.5).then_inc(setup_p, 1)
            pool.memset(expand_raw[:, :], 1.0)
            pool.memset(dup_mask[:, :], 1.0)
            pool.memset(earlier[:, :], 1.0)
            pool.memset(tie[:, :, :], 1.0)
            pool.iota(own_rows[:, :], [[2, N // MAPW]], base=0, channel_multiplier=2 * N // MAPW)
            pool.iota(row_of_edge[:, :], [[P, NC]], base=2 * N, channel_multiplier=1)
            pool.iota(scat_idx[:, 0:1], [[0, 1]], base=N, channel_multiplier=1).then_inc(setup_p, 1)
            pool.wait_ge(setup_p, 2)
            pool.affine_select(out=dup_mask[:, :], in_=dup_mask[:, :], compare_op=ALU.is_gt, fill=0.0, base=NE,
                               pattern=[[0, 1]], channel_multiplier=-1)
            pool.affine_select(out=expand_raw[:, :], in_=expand_raw[:, :], compare_op=ALU.is_ge, fill=0.0, base=0,
                               pattern=[[1, NE * EH]], channel_multiplier=-EH)
            pool.affine_select(out=earlier[:, :], in_=earlier[:, :], compare_op=ALU.is_gt, fill=0.0, base=0,
                               pattern=[[1, NC]], channel_multiplier=-1)
            pool.affine_select(out=tie[:, :, :], in_=tie[:, :, :], compare_op=ALU.is_gt, fill=0.0, base=0,
                               pattern=[[1, NE], [-1, NE]], channel_multiplier=0).then_inc(setup_p, 1)
            pool.wait_ge(setup_p, 3)
            pool.affine_select(out=expand_raw[:, :], in_=expand_raw[:, :], compare_op=ALU.is_ge, fill=0.0,
                               base=EH - 1, pattern=[[-1, NE * EH]], channel_multiplier=EH).then_inc(consts, 1)

            pool.dma_start(where_from[0:N, :].rearrange("(p i) a -> p (i a)", p=MAPW), own_rows[:, :]
                           ).then_inc(map_put, 16)

            def rstd_a(g, par):
                pool.wait_ge(a_var, g + 1)
                pool.tensor_tensor(rstd[:, par, :], var[:, par, :], neg_half[:, :], ALU.pow).then_inc(a_rstd, 1)

            def body(g, par):
                if has(g, 2):
                    rstd_a(g + 2, par)
                if isinstance(g, int) and g == 0:
                    pool.wait_ge(setup_v, 9)
                pool.wait_ge(map_put, 16 * (CPG * g + 1))
                pool.sem_inc(turns_p, 1)
                pool.tensor_copy(idx_now[:, 0:CPG], scat_idx[:, bass.ds(CPG * g, CPG)])
                pool.tensor_copy(row_now[:, :], row_of_edge[:, bass.ds(CPG * g, CPG)]).then_inc(map_copied, 1)
                pool.wait_ge(map_copied, g + 1)
                pool.sem_inc(turns_p, 1)
                for q in range(CPG):
                    pool.wait_ge(map_put, 16 * (CPG * g + q + 1))
                    pool.sem_inc(turns_p, 1)
                    pool.indirect_dma_start(
                        out=where_from[:, :], out_offset=bass.IndirectOffsetOnAxis(ap=idx_now[:, q:q + 1], axis=0),
                        in_=row_now[:, q:q + 1], in_offset=None).then_inc(map_put, 16)

            rstd_a(0, 0)
            rstd_a(1, 1)

            pairs(pool, body)

            for par in range(2):
                pool.wait_ge(t_stored[par], 32 * (NG // 2))
            pool.wait_ge(setup_v, 9)
            for b in range(NB):
                if b >= 2:
                    pool.wait_ge(b_add, b - 1)
                    pool.wait_ge(b_xld, b - 1)
                for q in range(CB):
                    c = CB * b + q
                    pool.indirect_dma_start(
                        out=xls[:, c, :], out_offset=None, in_=t_half[0:2 * N, :],
                        in_offset=bass.IndirectOffsetOnAxis(ap=src_idx[:, c:c + 1], axis=0)
                    ).then_inc(gathered[b % 2], 16)
                    pool.indirect_dma_start(
                        out=td[:, b % 2, q, :], out_offset=None, in_=table[0:N, :],
                        in_offset=bass.IndirectOffsetOnAxis(ap=dst_idx[:, c:c + 1], axis=0)
                    ).then_inc(gathered[b % 2], 16)

            pool.wait_ge(b_back, 2)
            pool.memset(zsel[:, :, :], 0.0).then_inc(b_zsel, 1)
            pool.wait_ge(b_zsel, 1)
            pool.affine_select(out=zsel[:, :, :], in_=zsel[:, :, :], compare_op=ALU.not_equal, fill=1.0, base=0,
                               pattern=[[1, NC], [-1, NC]], channel_multiplier=0).then_inc(b_zsel, 1)

            for b in range(NB):
                pool.wait_ge(b_scaled, b + 1)
                rows = xld[:, CB * b:CB * (b + 1), :].rearrange("p c (h d) -> p c h d", h=H)
                pool.tensor_tensor(rows, rows,
                                   psr[:, b % 2, :, :].rearrange("p h c -> p c h").unsqueeze(3)
                                   .broadcast_to([P, CB, H, HD]), ALU.mult).then_inc(b_self, 1)
            pool.wait_ge(b_out, NB)
            pool.memset(w2_raw[:, :, :], 0.0).then_inc(consts, 1)

            def gather_rows(g):
                pool.tensor_copy(idx_now[:, :], from_idx[:, bass.ds(g, 1), :].rearrange("p g j -> p (g j)")
                                 ).then_inc(map_copied, 1)
                pool.wait_ge(map_copied, NG + 1 + g)
                pool.sem_inc(turns_p, 1)
                for j in range(J):
                    pool.indirect_dma_start(
                        out=agg[:, j, :], out_offset=None, in_=t_half,
                        in_offset=bass.IndirectOffsetOnAxis(ap=idx_now[:, j:j + 1], axis=0)
                    ).then_inc(agg_loaded, 16)

            def rstd_c(g, par):
                pool.wait_ge(c_var, g + 1)
                pool.tensor_tensor(rstd[:, par, :], var[:, par, :], neg_half[:, :], ALU.pow).then_inc(c_rstd, 1)

            pool.wait_ge(map_loaded, 16)
            for par in range(2):
                pool.wait_ge(rows_stored[par], 16 * (NB // 2))
            gather_rows(0)
            pool.wait_ge(c_atp, KH)
            gather_rows(1)
            rstd_c(0, 0)

            def body_c(g, par):
                if has(g, 2):
                    pool.wait_ge(c_atp, KH * (g + 2))
                    pool.sem_inc(turns_p, 1)
                    gather_rows(g + 2)
                for m in range(1, MF):
                    pool.wait_ge(c_h1hi, MF * g + m + 1)
                    pool.tensor_tensor(h_lo[:, m, :], gl[:, m, :], h_hi[:, m, :].bitcast(F32),
                                       ALU.subtract).then_inc(c_h1lo_p, 1)
                if has(g, 1):
                    rstd_c(g + 1, 1 - par)

            pairs(pool, body_c)

        @block.scalar
        def _(act):
            def split_weights():
                act.wait_ge(raw_wa, 16 * 2)
                for k in range(KD):
                    last = act.activation(wd_hi[:, k, :], wd_raw[:, k, :], ACT.Copy, scale=rmsw[:, k:k + 1])
                last.then_inc(setup_s, 1)
                act.wait_ge(raw_wlr, 16 * 2)
                act.activation(wlr_hi[:, :, :], wlr_raw[:, :, :], ACT.Copy).then_inc(setup_s, 1)

            def norm(g, par, j):
                act.wait_ge(a_nb, g + 1)
                wait(act, a_tp, KD * (g - 1))
                act.activation(axn[:, par, j, :], ax[:, par, D * j:D * (j + 1)], ACT.Identity,
                               bias=nbias[:, par, j:j + 1], scale=rstd[:, par, j:j + 1]).then_inc(a_xn, 1)

            def high(g, k):
                t = KD * g + k
                act.wait_ge(a_tp, t + 1)
                wait(act, a_mm, t - 3)
                act.activation(axt_hi[:, k % 4, :], T_A[k % 4][:, 0:G], ACT.Copy).then_inc(a_hi, 1)

            def body(g, par):
                norms = {5: (0,), 6: (1,), 7: (2, 3)} if isinstance(g, int) and g == 0 else {j + 2: (j,) for j in range(J)}
                for k in range(2, KD):
                    high(g, k)
                    for j in norms.get(k, ()):
                        if has(g, 1):
                            norm(g + 1, 1 - par, j)
                    if k == 5 and has(g, -2):
                        store_table(g - 2, par)
                for m in range(KH):
                    act.wait_ge(a_mm, KD * (g + 1))
                    wait(act, a_lr, J * (g - 1))
                    act.activation(ht_hi[:, par, m, :], H_A[m][:, 0:G], ACT.Copy).then_inc(a_hhi, 1)
                if has(g, -1):
                    empty_lr(g - 1, 1 - par, 0)
                if has(g, 1):
                    high(g + 1, 0)
                    high(g + 1, 1)
                if has(g, -1):
                    empty_lr(g - 1, 1 - par, 2)

            def empty_lr(g, par, j):
                act.wait_ge(a_lr, J * g + j + 1)
                wait(act, t_stored[par], 16 * (g - par))
                act.activation(trow[:, par, 2 * HID * j:2 * HID * (j + 1)], X_A[0][0:P, :],
                               ACT.Copy).then_inc(a_ev_s, 1)

            def store_table(g, par):
                act.wait_ge(a_ev_s, 2 * (g + 1))
                act.wait_ge(a_ev_v, 2 * (g + 1))
                act.dma_start(t_g[g, 0:SPLIT, :], trow[0:SPLIT, par, :]).then_inc(t_stored[par], 16)
                act.dma_start(t_g[g, SPLIT:P, :], trow[SPLIT:P, par, :]).then_inc(t_stored[par], 16)

            for j in range(J):
                norm(0, 0, j)
            high(0, 0)
            high(0, 1)
            split_weights()
            pairs(act, body)
            store_table(NG - 2, 0)
            empty_lr(NG - 1, 1, 0)
            empty_lr(NG - 1, 1, 2)
            store_table(NG - 1, 1)

            act.wait_ge(raw_wc, 16 * (1 + KD))
            act.activation(wup_hi[:, :, :], wup_raw[:, :, :], ACT.Copy).then_inc(b_split_s, 1)
            act.activation(w1_hi[:, :, :], w1_raw[:, :, :], ACT.Copy).then_inc(b_split_s, 1)

            def body_b(b, par):
                fills = 2 * CB * 16
                act.wait_ge(gathered[par], fills // 2 * (b - par) + fills)
                act.activation(xld[:, bass.ds(CB * b, CB), :], td[:, par, :, 0:HID], ACT.Copy).then_inc(b_xld, 1)

            with act.Fori(0, NB // 2) as i:
                for par in range(2):
                    body_b(2 * i + par, par)
            act.wait_ge(b_max, 6)
            act.activation(pexp[:, :, :, :], pe_pair[:, :, :, :], ACT.Exp).then_inc(b_exp, 1)

            def split_agg(m, g):
                act.wait_ge(c_atp, KH * g + m + 1)
                wait(act, c_up, 8 * g)
                act.activation(aggt_hi[:, m, :], T_C[m][:, 0:G], ACT.Copy).then_inc(c_ahi, 1)

            def norm_c(g, par):
                for j in range(J):
                    act.wait_ge(c_nb, g + 1)
                    wait(act, c_tp, KD * g)
                    act.activation(cxn[:, j, :], cx[:, par, j, :], ACT.Identity,
                                   bias=nbias[:, par, j:j + 1], scale=rstd[:, par, j:j + 1]).then_inc(c_xn, 1)

            def high_x(g, k):
                t = KD * g + k
                act.wait_ge(c_tp, t + 1)
                wait(act, c_mm, t - 1)
                act.activation(cxt_hi[:, k % 2, :], T_C[k % 2][:, 0:G], ACT.Copy).then_inc(c_hi, 1)

            def gelu1(g, m):
                act.wait_ge(c_mm, KD * (g + 1))
                wait(act, c_h2lo, MF * (g - 1) + m + 1)
                act.activation(gl[:, m, :], ACC[m][:, 0:G], ACT.Gelu, bias=b1c[:, m:m + 1]).then_inc(c_g1, 1)
                act.wait_ge(c_g1, MF * g + m + 1)
                wait(act, c_w3, 8 * g)
                act.activation(h_hi[:, m, :], gl[:, m, :], ACT.Copy).then_inc(c_h1hi, 1)

            def gelu2(g, m):
                act.wait_ge(c_w2, MF * g + m + 1)
                act.activation(gl[:, m, :], ACC[m][:, 0:G], ACT.Gelu, bias=b2c[:, m:m + 1]).then_inc(c_g2, 1)

            def high2(g, m):
                act.wait_ge(c_wmul, MF * g + m + 1)
                act.activation(h_hi[:, m, :], gl[:, m, :], ACT.Copy).then_inc(c_h2hi, 1)

            def body_c(g, par):
                for k in range(2, KD):
                    high_x(g, k)
                for m in range(MF):
                    gelu1(g, m)
                gelu2(g, 0)
                for m in range(1, MF):
                    gelu2(g, m)
                    high2(g, m - 1)
                high2(g, MF - 1)
                if has(g, 2):
                    for m in range(KH):
                        split_agg(m, g + 2)
                if has(g, 1):
                    norm_c(g + 1, 1 - par)
                    high_x(g + 1, 0)
                    high_x(g + 1, 1)

            for m in range(KH):
                split_agg(m, 0)
            act.wait_ge(raw_w3, 16 * 3)
            act.activation(w2_hi[:, :, :], w2_raw[:, :, :], ACT.Copy)
            act.activation(w3_hi[:, :, :], w3_raw[:, :, :], ACT.Copy).then_inc(w3_split_s, 1)
            for m in range(KH):
                split_agg(m, 1)
            norm_c(0, 0)
            high_x(0, 0)
            high_x(0, 1)
            pairs(act, body_c)

        @block.vector
        def _(dve):
            def bn(g, par, piece, src_tile, done):
                j, n = piece // 2, piece % 2
                dve.bn_stats(stat[:, j, 6 * n:6 * n + 6],
                             src_tile[:, HALF * n:HALF * (n + 1)]).then_inc(done, 1)

            def moments(g, par, bn_sem, aggr_sem, var_sem, scale, shift):
                dve.wait_ge(bn_sem, 8 * (g + 1))
                dve.sem_inc(turns, 1)
                for j in range(J):
                    last = dve.bn_aggr(mv[:, par, j, :], stat[:, j, :])
                last.then_inc(aggr_sem, 1)
                dve.wait_ge(aggr_sem, g + 1)
                dve.tensor_scalar(var[:, par, :], mv[:, par, :, 1], scale, shift, ALU.mult, ALU.add
                                  ).then_inc(var_sem, 1)

            def bias_of(g, par, rstd_sem, nb_sem):
                dve.wait_ge(rstd_sem, g + 1)
                dve.scalar_tensor_tensor(nbias[:, par, :], mv[:, par, :, 0], -1.0, rstd[:, par, :],
                                         ALU.mult, ALU.mult).then_inc(nb_sem, 1)

            def moments_a(g, par):
                moments(g, par, a_bn, a_aggr, a_var, 1.0 + RMS_EPS, LN_EPS * RMS_EPS)

            def bn_a(g, par, piece):
                if isinstance(g, int) and g == 0:
                    if piece % 2 == 0:
                        dve.wait_ge(first_loaded[piece // 2], 32)
                elif piece == 0:
                    dve.wait_ge(ax_loaded[par], 16 * (g + par))
                    wait(dve, a_aggr, g)
                bn(g, par, piece, ax[:, par, D * (piece // 2):D * (piece // 2 + 1)], a_bn)

            for piece in range(8):
                bn_a(0, 0, piece)
            moments_a(0, 0)
            bias_of(0, 0, a_rstd, a_nb)
            def low(g, k):
                dve.wait_ge(a_hi, KD * g + k + 1)
                dve.tensor_tensor(axt_lo[:, k % 4, :], T_A[k % 4][:, 0:G], axt_hi[:, k % 4, :].bitcast(F32),
                                  ALU.subtract).then_inc(a_lo, 1)

            low(0, 0)
            low(0, 1)
            dve.wait_ge(setup_s, 1)
            for k in range(KD):
                last = dve.scalar_tensor_tensor(wd_lo[:, k, :], wd_raw[:, k, :], rmsw[:, k:k + 1],
                                                wd_hi[:, k, :].bitcast(F32), ALU.mult, ALU.subtract)
            last.then_inc(setup_v, 1)

            def indices_setup():
                dve.wait_ge(raw_idx, 16 * 4)
                dve.tensor_copy(idx_f[:, :, :], idx_rows[:, :, :]).then_inc(setup_v, 1)
                dve.wait_ge(setup_t, 1)
                dve.tensor_scalar(src_idx[:, :], X_A[0][0:P, 0:NC], 2.0, None, ALU.mult)
                dve.tensor_copy(dst_idx[:, :], X_A[0][0:P, NC:2 * NC])
                dve.tensor_copy(dst_col[:, :], X_A[0][0:P, NC:2 * NC])
                dve.tensor_copy(dst_next_col[:, :], X_A[0][0:P, 2 * NC:3 * NC]).then_inc(setup_v, 1)
                dve.tensor_copy(last_of_chunk[:, :], idx_f[:, 1, P - 1:P])
                dve.wait_ge(setup_p, 2)
                dve.tensor_copy(trash[:, :], scat_idx[:, 0:1]).then_inc(setup_v, 1)
                dve.wait_ge(setup_v, 5)
                dve.tensor_tensor(dst_next_col[:, :], dst_next_col[:, :], dst_col[:, :],
                                  ALU.is_equal).then_inc(setup_v, 1)
                dve.tensor_scalar(eq_last[:, :], dst_col[:, :], -1.0, trash[:, 0:1], ALU.mult, ALU.add
                                  ).then_inc(setup_v, 1)
                dve.wait_ge(setup_v, 7)
                dve.tensor_tensor(dst_next_col[:, :], dst_next_col[:, :], eq_last[:, :],
                                  ALU.mult).then_inc(setup_v, 1)
                dve.wait_ge(setup_v, 8)
                dve.tensor_tensor(scat_idx[:, :], dst_col[:, :], dst_next_col[:, :], ALU.add
                                  ).then_inc(setup_v, 1)

            def experts_setup():
                dve.wait_ge(setup_t, 2)
                tok_t = X_A[1][:, 0:KD * NE].rearrange("p (k e) -> p k e", e=NE)
                dve.tensor_copy(tok_st[:, :, 0:NE], tok_t).then_inc(setup_v, 1)
                dve.wait_ge(setup_v, 10)
                dve.tensor_tensor(tok_st[:, :, NE:2 * NE], tok_t, tok_st[:, :, 0:NE].bitcast(F32), ALU.subtract)
                dve.tensor_copy(b3_hi[:, :], b3_raw[:, :])
                dve.tensor_scalar(dup_rest[:, :], dup_mask[:, :], -1.0, 1.0, ALU.mult, ALU.add)
                dve.wait_ge(consts, 3)
                dve.tensor_copy(expand[:, :], expand_raw[:, :]).then_inc(setup_v, 1)
                dve.wait_ge(setup_v, 11)
                dve.tensor_tensor(b3_lo[:, :], b3_raw[:, :], b3_hi[:, :].bitcast(F32), ALU.subtract
                                  ).then_inc(b_split_v, 1)
                dve.wait_ge(b_split_v, 1)
                dve.tensor_scalar(b3_lo[:, :], b3_lo[:, :], dup_rest[:, 0:1], None, ALU.mult).then_inc(b_split_v, 1)
                dve.wait_ge(b_split_v, 2)
                dve.scalar_tensor_tensor(b3_hl[:, :], b3_hi[:, :].bitcast(F32), dup_mask[:, 0:1], b3_lo[:, :],
                                         ALU.mult, ALU.add).then_inc(setup_v, 1)

            def empty_lr(g, par, j):
                dve.wait_ge(a_lr, J * g + j + 1)
                wait(dve, t_stored[par], 16 * (g - par))
                dve.tensor_copy(trow[:, par, 2 * HID * j:2 * HID * (j + 1)], X_A[1][0:P, :]).then_inc(a_ev_v, 1)

            def body(g, par):
                at_start = isinstance(g, int) and g == 0
                for k in range(2, KD):
                    low(g, k)
                    if at_start:
                        if k == 2:
                            for piece in range(8):
                                bn_a(1, 1, piece)
                            moments_a(1, 1)
                        elif k == 3:
                            bias_of(1, 1, a_rstd, a_nb)
                        elif k == 4:
                            dve.wait_ge(setup_s, 2)
                            dve.tensor_tensor(wlr_lo[:, :, :], wlr_raw[:, :, :], wlr_hi[:, :, :].bitcast(F32),
                                              ALU.subtract).then_inc(setup_v, 1)
                        else:
                            for piece in range(3 * (k - 5), min(3 * (k - 4), 8)):
                                bn_a(2, 0, piece)
                    elif has(g, 2):
                        bn_a(g + 2, par, k - 2)
                        if k >= 6:
                            bn_a(g + 2, par, k)
                for m in range(KH):
                    dve.wait_ge(a_hhi, KH * g + m + 1)
                    dve.tensor_tensor(ht_lo[:, par, m, :], H_A[m][:, 0:G],
                                      ht_hi[:, par, m, :].bitcast(F32), ALU.subtract).then_inc(a_hlo, 1)
                if has(g, 1):
                    low(g + 1, 0)
                if has(g, -1):
                    empty_lr(g - 1, 1 - par, 1)
                if has(g, 2):
                    moments_a(g + 2, par)
                if has(g, 1):
                    low(g + 1, 1)
                if has(g, 2):
                    bias_of(g + 2, par, a_rstd, a_nb)
                if has(g, -1):
                    empty_lr(g - 1, 1 - par, 3)
                if at_start:
                    dve.wait_ge(raw_small, 16 * 6)
                    indices_setup()
                    experts_setup()

            pairs(dve, body)
            empty_lr(NG - 1, 1, 1)
            empty_lr(NG - 1, 1, 3)

            dve.wait_ge(raw_dst_row, 16)
            dve.memset(fresh[:, :], 0.0).then_inc(b_fresh, 1)
            dve.tensor_tensor(eq_last[:, :], dst_col[:, :],
                              dst_row[:, P - 1:E:P], ALU.is_equal)
            dve.wait_ge(b_fresh, 1)
            dve.tensor_tensor(fresh[:, 1:E], dst_row[0:H, 1:E], dst_row[0:H, 0:E - 1], ALU.not_equal
                              ).then_inc(b_fresh, 1)
            dve.wait_ge(b_fresh, 2)
            dve.tensor_scalar(fresh[:, 1:E], fresh[:, 1:E], FAR, None, ALU.mult).then_inc(b_fresh, 1)
            for n, (lo, raw, hi) in enumerate(((wup_lo, wup_raw, wup_hi), (w1_lo, w1_raw, w1_hi))):
                dve.wait_ge(b_split_s, n + 1)
                dve.tensor_tensor(lo[:, :, :], raw[:, :, :], hi[:, :, :].bitcast(F32), ALU.subtract
                                  ).then_inc(b_split_v, 1)

            def add_messages(b, par):
                fills = 2 * CB * 16
                dve.wait_ge(gathered[par], fills // 2 * (b - par) + fills)
                wait(dve, b_red, 2 * (b - 1))
                dve.tensor_tensor(msg[:, par, 0:CB, :], xls[:, bass.ds(CB * b, CB), :],
                                  td[:, par, :, HID:2 * HID], ALU.add)
                dve.tensor_tensor(msg[:, par, CB:2 * CB, :], td[:, par, :, 0:HID],
                                  td[:, par, :, HID:2 * HID], ALU.add).then_inc(b_add, 1)

            def sum_scores(b, par):
                dve.wait_ge(b_add, b + 1)
                dve.scalar_tensor_tensor(msg[:, par, :, :], msg[:, par, :, :], SLOPE, msg[:, par, :, :],
                                         ALU.mult, ALU.max).then_inc(b_leak, 1)
                dve.wait_ge(b_leak, b + 1)
                dve.tensor_tensor(msg[:, par, :, :], msg[:, par, :, :],
                                  att_bc[:, :].unsqueeze(1).broadcast_to([P, 2 * CB, HID]),
                                  ALU.mult).then_inc(b_mul, 1)
                dve.wait_ge(b_mul, b + 1)
                for kind in range(2):
                    dve.tensor_reduce(
                        pe_pair[:, kind, :, bass.ds(CB * b, CB)].rearrange("p h c -> p c h"),
                        msg[:, par, CB * kind:CB * (kind + 1), :].rearrange("p c (h d) -> p c h d", h=H),
                        AX.X, ALU.add).then_inc(b_red, 1)

            add_messages(0, 0)
            add_messages(1, 1)
            sum_scores(0, 0)
            with dve.Fori(1, NB // 2) as i:
                add_messages(2 * i, 0)
                sum_scores(2 * i - 1, 1)
                add_messages(2 * i + 1, 1)
                sum_scores(2 * i, 0)
            sum_scores(NB - 1, 1)
            dve.wait_ge(b_red, 2 * NB)
            dve.tensor_tensor(pexp[:, 0, :, :], pe_pair[:, 0, :, :], pe_pair[:, 1, :, :], ALU.max
                              ).then_inc(b_max, 1)
            for q in range(2):
                dve.wait_ge(b_max_t, q + 1)
                dve.tensor_copy(max_t[:, q, :], bank[q][0:2 * NC, 0:P]).then_inc(b_max, 1)
            dve.wait_ge(b_rows, 32)
            dve.tensor_tensor_scan(max_row[:, :], fresh[:, 0:E], max_row[:, :], FAR, ALU.add, ALU.max
                                   ).then_inc(b_scan, 1)
            dve.wait_ge(b_scan, 1)
            dve.tensor_tensor_scan(max_row[:, ::-1], fresh[:, E:0:-1], max_row[:, ::-1], FAR, ALU.add, ALU.max
                                   ).then_inc(b_scan, 1)
            for kind in range(2):
                dve.wait_ge(b_back, 2)
                dve.tensor_tensor(pe_pair[:, kind, :, :], pe_pair[:, kind, :, :],
                                  bank[2][0:P, 0:H * NC].rearrange("p (h c) -> p h c", h=H),
                                  ALU.subtract).then_inc(b_max, 1)
            dve.wait_ge(b_max, 5)
            dve.tensor_copy(tot[:, :, :], pe_pair[:, 0, :, 0:CB]).then_inc(b_max, 1)

            dve.wait_ge(b_exp, 1)

            def weigh(b, par):
                wait(dve, b_l, b - 1)
                rows = xls[:, bass.ds(CB * b, CB), :].rearrange("p c (h d) -> p c h d", h=H)
                dve.tensor_tensor(rows, rows,
                                  pexp[:, 0, :, bass.ds(CB * b, CB)].rearrange("p h c -> p c h").unsqueeze(3)
                                  .broadcast_to([P, CB, H, HD]), ALU.mult)
                dve.tensor_tensor(zmat[:, par, :, :], zsel[:, bass.ds(CB * b, CB), :],
                                  eq_last[:, bass.ds(CB * b, CB)].unsqueeze(2).broadcast_to([P, CB, NC]),
                                  ALU.mult).then_inc(b_v, 1)

            dve.wait_ge(b_zsel, 2)
            weigh(0, 0)
            weigh(1, 1)
            with dve.Fori(1, NB // 2) as i:
                for par in range(2):
                    weigh(2 * i + par, par)
            dve.wait_ge(b_l, NB)
            dve.tensor_copy(lsb[:, 0:HID], bank[3][0:NC, 0:HID])
            dve.tensor_copy(lsb[:, HID:HID + H], bank[4][0:NC, 0:H]).then_inc(b_lsb, 1)

            def same_segment(b, par):
                wait(dve, b_num, b - 1)
                dve.tensor_tensor(smat[:, par, :, :],
                                  dst_row[:, bass.ds(CB * P * b, CB * P)].rearrange("p (c e) -> p c e", c=CB),
                                  dst_col[:, bass.ds(CB * b, CB)].unsqueeze(2).broadcast_to([P, CB, P]),
                                  ALU.is_equal)
                dve.scalar_tensor_tensor(
                    bmat[:, par, :, :],
                    dst_row[0:NC, bass.ds(CB * P * b, CB * P)].rearrange("p (c e) -> p c e", c=CB),
                    last_of_chunk[:, 0:1],
                    earlier[:, bass.ds(CB * b, CB)].unsqueeze(2).broadcast_to([NC, CB, P]),
                    ALU.is_equal, ALU.mult).then_inc(b_sb, 1)

            def finish(b, par):
                own = pexp[:, 1, :, bass.ds(CB * b, CB)]
                dve.wait_ge(b_num, b + 1)
                dve.scalar_tensor_tensor(tot[:, :, :],
                                         bank[2 + 5 * par][0:P, 0:CB * H].rearrange("p (c h) -> p h c", h=H),
                                         1e-16, own, ALU.add, ALU.add).then_inc(b_den, 1)
                dve.wait_ge(b_den, 3 * b + 1)
                dve.reciprocal(rden[:, :, :], tot[:, :, :]).then_inc(b_den, 1)
                dve.wait_ge(b_den, 3 * b + 2)
                wait(dve, b_self, b - 1)
                dve.tensor_tensor(psr[:, par, :, :], own, rden[:, :, :], ALU.mult).then_inc(b_scaled, 1)
                wait(dve, rows_stored[par], 8 * (b - par))
                for q in range(CB):
                    num = bank[5 * par + q // 2][0:P, HID * (q % 2):HID * (q % 2 + 1)]
                    last = dve.tensor_tensor(
                        orow[:, par, q, :].rearrange("p (h d) -> p h d", h=H),
                        num.rearrange("p (h d) -> p h d", h=H),
                        rden[:, :, q:q + 1].broadcast_to([P, H, HD]), ALU.mult)
                last.then_inc(b_den, 1)
                dve.wait_ge(b_den, 3 * b + 3)
                dve.wait_ge(b_self, b + 1)
                dve.tensor_tensor(orow[:, par, :, :], orow[:, par, :, :], xld[:, bass.ds(CB * b, CB), :],
                                  ALU.add).then_inc(b_out, 1)

            same_segment(0, 0)
            same_segment(1, 1)
            finish(0, 0)
            same_segment(2, 0)
            finish(1, 1)
            with dve.Fori(1, NB // 2 - 1) as i:
                same_segment(2 * i + 1, 1)
                finish(2 * i, 0)
                same_segment(2 * i + 2, 0)
                finish(2 * i + 1, 1)
            same_segment(NB - 1, 1)
            finish(NB - 2, 0)
            finish(NB - 1, 1)

            def low_agg(m, g):
                dve.wait_ge(c_ahi, KH * g + m + 1)
                dve.tensor_tensor(aggt_lo[:, m, :], T_C[m][:, 0:G], aggt_hi[:, m, :].bitcast(F32),
                                  ALU.subtract).then_inc(c_alo, 1)

            def low_x(g, k):
                dve.wait_ge(c_hi, KD * g + k + 1)
                dve.tensor_tensor(cxt_lo[:, k % 2, :], T_C[k % 2][:, 0:G], cxt_hi[:, k % 2, :].bitcast(F32),
                                  ALU.subtract).then_inc(c_lo, 1)

            def residual(g, par, u, y):
                j, n = u // 2, u % 2
                if n == 0:
                    dve.wait_ge(cx_loaded[par][j], 16 * (g + 2 - par))
                dve.wait_ge(c_up, 8 * g + u + 1)
                piece = cx[:, par, j, HALF * n:HALF * (n + 1)]
                dve.tensor_tensor(piece, piece, y[0:P, :], ALU.add).then_inc(c_upv, 1)

            def bn_c(g, par, u):
                if u == 0:
                    wait(dve, c_aggr, g)
                dve.wait_ge(c_upv, 8 * g + u + 1)
                bn(g, par, u, cx[:, par, u // 2, :], c_bn)

            def moments_c(g, par):
                moments(g, par, c_bn, c_aggr, c_var, 1.0, LN_EPS)

            def low1(g, m):
                dve.wait_ge(c_h1hi, MF * g + m + 1)
                dve.tensor_tensor(h_lo[:, m, :], gl[:, m, :], h_hi[:, m, :].bitcast(F32),
                                  ALU.subtract).then_inc(c_h1lo, 1)

            def low2(g, m):
                dve.wait_ge(c_h2hi, MF * g + m + 1)
                dve.tensor_tensor(h_lo[:, m, :], gl[:, m, :], h_hi[:, m, :].bitcast(F32),
                                  ALU.subtract).then_inc(c_h2lo, 1)

            def weight(g, m):
                dve.wait_ge(c_g2, MF * g + m + 1)
                dve.wait_ge(c_wx, MF * g + m + 1)
                dve.tensor_tensor(gl[:, m, :], gl[:, m, :], T_C[m % 2][:, 0:G], ALU.mult).then_inc(c_wmul, 1)

            def route(g):
                dve.wait_ge(c_rs, g + 1)
                parts = T_C[0][0:P, :].rearrange("p (j e) -> p j e", j=J)
                dve.tensor_copy(score[:, :, :], parts[:, :, 0:NE]).then_inc(c_rt, 1)
                dve.wait_ge(c_rt, 5 * g + 1)
                dve.tensor_tensor(score[:, :, :], score[:, :, :], parts[:, :, NE:2 * NE], ALU.add).then_inc(c_rt, 1)
                dve.wait_ge(c_rt, 5 * g + 2)
                other = score[:, :, :].unsqueeze(2).broadcast_to([P, J, NE, NE])
                own = score[:, :, :].unsqueeze(3).broadcast_to([P, J, NE, NE])
                dve.tensor_tensor(beats[:, :, :, :], other, own, ALU.is_gt)
                dve.tensor_tensor(beats2[:, :, :, :], other, own, ALU.is_equal).then_inc(c_rt, 1)
                dve.wait_ge(c_rt, 5 * g + 3)
                dve.tensor_tensor(beats2[:, :, :, :], beats2[:, :, :, :],
                                  tie[:, :, :].unsqueeze(1).broadcast_to([P, J, NE, NE]), ALU.mult
                                  ).then_inc(c_rt, 1)
                dve.wait_ge(c_rt, 5 * g + 4)
                dve.tensor_tensor(beats[:, :, :, :], beats[:, :, :, :], beats2[:, :, :, :], ALU.add
                                  ).then_inc(c_rt, 1)
                dve.wait_ge(c_rt, 5 * g + 5)
                dve.tensor_reduce(rank[:, :, :], beats[:, :, :, :], AX.X, ALU.add).then_inc(c_w, 1)
                dve.wait_ge(c_w, 3 * g + 1)
                for a in range(2):
                    dve.tensor_scalar(wdup[:, :, a, :], rank[:, :, :], 2.0, 0.5, ALU.is_lt, ALU.mult
                                      ).then_inc(c_w, 1)

            def weights_t(g):
                dve.wait_ge(c_wtp, g + 1)
                wait(dve, c_w3, 8 * g)
                dve.tensor_copy(w_t[:, :], T_C[1][0:2 * NE, 0:G]).then_inc(c_wt, 1)

            def result(g, par, u):
                j, n = u // 2, u % 2
                dve.wait_ge(c_w3, 8 * g + u + 1)
                piece = cx[:, par, j, HALF * n:HALF * (n + 1)]
                dve.tensor_tensor(piece, piece, DOWN_BANK[u][0:P, :], ALU.add).then_inc(c_w3v, 1)

            def body_c(g, par):
                nxt, npar, more = g + 1, 1 - par, has(g, 1)

                def next_residual(u):
                    if more:
                        residual(nxt, npar, u, UP_BANK[u])

                def next_bn(u):
                    if more:
                        bn_c(nxt, npar, u)

                for k in range(2, KD):
                    low_x(g, k)
                    if 0 <= k - (KD - KU) < KU:
                        next_residual(k - (KD - KU))
                        next_bn(k - (KD - KU))
                dve.wait_ge(c_mm, KD * (g + 1))
                wait(dve, c_rs, g)
                dve.tensor_copy(sc_t[:, :], Y[0][:, 0:G]).then_inc(c_sc, 1)
                low1(g, 0)
                next_residual(5)
                route(g)
                next_residual(6)
                weights_t(g)
                next_residual(7)
                weight(g, 0)
                weight(g, 1)
                low2(g, 0)
                weight(g, 2)
                low2(g, 1)
                weight(g, 3)
                low2(g, 2)
                next_bn(5)
                low2(g, 3)
                next_bn(6)
                next_bn(7)
                if more:
                    moments_c(nxt, npar)
                    bias_of(nxt, npar, c_rstd, c_nb)
                if has(g, 2):
                    for m in range(KH):
                        low_agg(m, g + 2)
                for u in range(6):
                    result(g, par, u)
                if more:
                    low_x(nxt, 0)
                result(g, par, 6)
                if more:
                    low_x(nxt, 1)
                result(g, par, 7)

            for m in range(KH):
                low_agg(m, 0)
            for u in range(8):
                residual(0, 0, u, Y[u % 2])
                bn_c(0, 0, u)
            moments_c(0, 0)
            bias_of(0, 0, c_rstd, c_nb)
            dve.wait_ge(w3_split_s, 1)
            dve.tensor_tensor(w2_lo[:, :, :], w2_raw[:, :, :], w2_hi[:, :, :].bitcast(F32), ALU.subtract)
            dve.tensor_tensor(w3_lo[:, :, :], w3_raw[:, :, :], w3_hi[:, :, :].bitcast(F32), ALU.subtract
                              ).then_inc(w3_split_v, 1)
            for m in range(KH):
                low_agg(m, 1)
            low_x(0, 0)
            low_x(0, 1)
            pairs(dve, body_c)

        @block.tensor
        def _(pe):
            def product(out_ap, left, right, start, stop):
                pe.matmul(out_ap, left[0], right[0], start=start, stop=False, skip_group_check=True)
                pe.matmul(out_ap, left[0], right[1], start=False, stop=False, skip_group_check=True)
                return pe.matmul(out_ap, left[1], right[0], start=False, stop=stop, skip_group_check=True)

            def small_setup():
                pe.wait_ge(setup_v, 3)
                for n in range(3):
                    last = pe.transpose(X_A[0][0:P, NC * n:NC * (n + 1)], idx_f[:, n, :], ident[0:NC, 0:NC])
                last.then_inc(setup_t, 1)
                pe.wait_ge(raw_small, 16 * 6)
                for k in range(KD):
                    last = pe.transpose(X_A[1][:, NE * k:NE * (k + 1)], tok_rows[:, 128 * k:128 * (k + 1)],
                                        ident[0:NE, 0:NE])
                last.then_inc(setup_t, 1)

            def turn(g, par, k):
                t = KD * g + k
                wait(pe, a_lo, t - 3)
                if k == 0:
                    pe.wait_ge(a_xn, J * (g + 1))
                for j in range(J):
                    last = pe.transpose(T_A[k % 4][:, P * j:P * (j + 1)], axn[:, par, j, 128 * k:128 * (k + 1)],
                                        ident[0:P, 0:P])
                last.then_inc(a_tp, 1)

            def left_right(g, par, j):
                if j == 0:
                    pe.wait_ge(a_hlo, KH * (g + 1))
                    if isinstance(g, int) and g == 0:
                        pe.wait_ge(setup_v, 11)
                wait(pe, a_ev_s if j % 2 == 0 else a_ev_v, 2 * g + j // 2)
                for m in range(KH):
                    rows = slice(P * j, P * (j + 1))
                    last = product(X_A[j % 2][0:P, :], (ht_hi[:, par, m, rows], ht_lo[:, par, m, rows]),
                                   (wlr_hi[:, m, :], wlr_lo[:, m, :]), m == 0, m == KH - 1)
                last.then_inc(a_lr, 1)

            def body(g, par):
                for k in range(KD):
                    if k + 2 < KD:
                        turn(g, par, k + 2)
                    pe.wait_ge(a_lo, KD * g + k + 1)
                    if k == 0:
                        wait(pe, a_hlo, KH * g)
                    for m in range(KH):
                        cols = slice(128 * m, 128 * (m + 1))
                        last = product(H_A[m][:, 0:G], (wd_hi[:, k, cols], wd_lo[:, k, cols]),
                                       (axt_hi[:, k % 4, :], axt_lo[:, k % 4, :]), k == 0, k == KD - 1)
                    last.then_inc(a_mm, 1)
                for j in range(J):
                    if has(g, -1):
                        left_right(g - 1, 1 - par, j)
                    if j < 2 and has(g, 1):
                        turn(g + 1, 1 - par, j)
                if isinstance(g, int) and g == 0:
                    small_setup()

            pe.wait_ge(consts, 2)
            turn(0, 0, 0)
            turn(0, 0, 1)
            pe.wait_ge(setup_v, 1)
            pairs(pe, body)
            for j in range(J):
                left_right(NG - 1, 1, j)

            pe.wait_ge(b_max, 1)
            for q in range(2):
                pe.transpose(bank[q][0:2 * NC, 0:P], pexp[:, 0, 2 * q:2 * q + 2, :].rearrange("p h c -> p (h c)"),
                             ident[0:P, 0:P]).then_inc(b_max_t, 1)
            pe.wait_ge(b_rows, 64)
            for q in range(2):
                pe.transpose(bank[2][0:P, 2 * NC * q:2 * NC * (q + 1)], max_t[:, q, :],
                             ident[0:2 * NC, 0:2 * NC]).then_inc(b_back, 1)

            def last_segments(b, par):
                pe.wait_ge(b_v, b + 1)
                first = isinstance(b, int) and b == 0
                final = isinstance(b, int) and b == NB - 1
                for q in range(CB):
                    z = zmat[:, par, q, :]
                    pe.matmul(bank[3][0:NC, 0:HID], z,
                              xls[:, bass.ds(CB * b + q, 1), :].rearrange("p c d -> p (c d)"),
                              start=first and q == 0, stop=final and q == CB - 1, skip_group_check=True)
                    last = pe.matmul(bank[4][0:NC, 0:H], z,
                                     pexp[:, 0, :, bass.ds(CB * b + q, 1)].rearrange("p h c -> p (h c)"),
                                     start=first and q == 0, stop=final and q == CB - 1, skip_group_check=True)
                last.then_inc(b_l, 1)

            last_segments(0, 0)
            last_segments(1, 1)
            with pe.Fori(1, NB // 2 - 1) as i:
                for par in range(2):
                    last_segments(2 * i + par, par)
            last_segments(NB - 2, 0)
            last_segments(NB - 1, 1)

            def segment_sums(b, par):
                pe.wait_ge(b_sb, b + 1)
                wait(pe, b_out, b - 1)
                for q in range(CB):
                    num = bank[5 * par + q // 2][0:P, HID * (q % 2):HID * (q % 2 + 1)]
                    den = bank[2 + 5 * par][0:P, H * q:H * (q + 1)]
                    pe.matmul(num, smat[:, par, q, :],
                              xls[:, bass.ds(CB * b + q, 1), :].rearrange("p c d -> p (c d)"),
                              start=True, stop=False, skip_group_check=True)
                    pe.matmul(num, bmat[:, par, q, :], lsb[:, 0:HID], start=False, stop=True,
                              skip_group_check=True)
                    pe.matmul(den, smat[:, par, q, :],
                              pexp[:, 0, :, bass.ds(CB * b + q, 1)].rearrange("p h c -> p (h c)"),
                              start=True, stop=False, skip_group_check=True)
                    last = pe.matmul(den, bmat[:, par, q, :], lsb[:, HID:HID + H], start=False, stop=True,
                                     skip_group_check=True)
                last.then_inc(b_num, 1)

            pe.wait_ge(b_lsb, 1)
            segment_sums(0, 0)
            segment_sums(1, 1)
            with pe.Fori(1, NB // 2) as i:
                for par in range(2):
                    segment_sums(2 * i + par, par)

            def turn_c(g, k):
                t = KD * g + k
                if k >= 2:
                    pe.wait_ge(c_lo, t - 1)
                else:
                    wait(pe, c_wmul, MF * g - 1 + k)
                    if has(g, 1):
                        pe.wait_ge(c_alo, KH * (g + 1) + k + 1)
                if k == 0:
                    pe.wait_ge(c_xn, J * (g + 1))
                for j in range(J):
                    last = pe.transpose(T_C[k % 2][:, P * j:P * (j + 1)], cxn[:, j, 128 * k:128 * (k + 1)],
                                        ident[0:P, 0:P])
                last.then_inc(c_tp, 1)

            def turn_agg(g, m):
                if m == 0:
                    pe.wait_ge(agg_loaded, 16 * J * (g + 1))
                wait(pe, c_wmul, MF * (g - 1) - 1 + m)
                for j in range(J):
                    last = pe.transpose(T_C[m][:, P * j:P * (j + 1)], agg[:, j, 128 * m:128 * (m + 1)],
                                        ident[0:P, 0:P])
                last.then_inc(c_atp, 1)

            def up(g, u, y):
                j, n = u // 2, u % 2
                for m in range(KH):
                    rows, cols = slice(P * j, P * (j + 1)), slice(HALF * n, HALF * (n + 1))
                    last = product(y[0:P, :], (aggt_hi[:, m, rows], aggt_lo[:, m, rows]),
                                   (wup_hi[:, m, cols], wup_lo[:, m, cols]), m == 0, m == KH - 1)
                last.then_inc(c_up, 1)

            def next_up(g, u):
                if u == 0:
                    pe.wait_ge(c_alo, KH * (g + 1))
                    wait(pe, c_w3v, 8 * (g - 1))
                if u == 6:
                    pe.wait_ge(c_sc, g)
                else:
                    pe.wait_ge(c_upv, 8 * g + min(u, 6))
                up(g, u, UP_BANK[u])

            def hidden1(g, k):
                pe.wait_ge(c_lo, KD * g + k + 1)
                if k == 0:
                    wait(pe, c_w3v, 8 * g - 2)
                for m in range(MF):
                    cols = slice(128 * m, 128 * (m + 1))
                    product(ACC[m][:, 0:G], (w1_hi[:, k, cols], w1_lo[:, k, cols]),
                            (cxt_hi[:, k % 2, :], cxt_lo[:, k % 2, :]), k == 0, k == KD - 1)
                if k == 0:
                    wait(pe, c_w3v, 8 * g - 1)
                pe.matmul(Y[0][:, 0:G], tok_st[:, k, :], cxt_hi[:, k % 2, :], start=k == 0, stop=False,
                          skip_group_check=True)
                pe.matmul(Y[0][:, 0:G], tok_st[:, k, :], cxt_lo[:, k % 2, :], start=False, stop=k == KD - 1,
                          skip_group_check=True).then_inc(c_mm, 1)

            def score_rows(g):
                pe.wait_ge(c_sc, g + 1)
                for j in range(J):
                    last = pe.transpose(T_C[0][0:P, 128 * j:128 * (j + 1)], sc_t[:, P * j:P * (j + 1)],
                                        ident[:, :])
                last.then_inc(c_rs, 1)

            def hidden2(g, m):
                if m == 0:
                    pe.wait_ge(c_h1lo, g + 1)
                else:
                    pe.wait_ge(c_h1lo_p, (MF - 1) * g + m)
                product(ACC[m][:, 0:G], (w2_hi[:, m, :], w2_lo[:, m, :]), (h_hi[:, m, :], h_lo[:, m, :]),
                        True, True).then_inc(c_w2, 1)

            def weights_rows(g):
                pe.wait_ge(c_w, 3 * (g + 1))
                for j in range(J):
                    last = pe.transpose(T_C[1][0:2 * NE, P * j:P * (j + 1)],
                                        wdup[:, j, :, :].rearrange("p a e -> p (a e)"), ident[0:P, 0:P])
                last.then_inc(c_wtp, 1)

            def spread(g, m):
                if m == 0:
                    pe.wait_ge(c_wt, g + 1)
                if m >= 2:
                    pe.wait_ge(c_wmul, MF * g + m - 1)
                pe.matmul(T_C[m % 2][:, 0:G], expand[:, 128 * m:128 * (m + 1)], w_t[0:NE, :], start=True,
                          stop=True, skip_group_check=True).then_inc(c_wx, 1)

            def down_begin(g, u, more):
                j, n = u // 2, u % 2
                if u < 2:
                    if more:
                        pe.wait_ge(c_upv, 8 * (g + 1) + 7 + u)
                elif u < 6:
                    pe.wait_ge(c_g2, MF * g + u - 1)
                else:
                    pe.wait_ge(c_w3v, 8 * g + u - 5)
                pe.matmul(DOWN_BANK[u][0:P, :], w_t[:, P * j:P * (j + 1)], b3_hl[:, HALF * n:HALF * (n + 1)],
                          start=True, stop=False, skip_group_check=True)

            def down_part(g, u, m):
                j, n = u // 2, u % 2
                rows, cols = slice(P * j, P * (j + 1)), slice(HALF * n, HALF * (n + 1))
                last = product(DOWN_BANK[u][0:P, :], (h_hi[:, m, rows], h_lo[:, m, rows]),
                               (w3_hi[:, m, cols], w3_lo[:, m, cols]), False, m == MF - 1)
                if m == MF - 1:
                    last.then_inc(c_w3, 1)

            def body_c(g, par):
                more = has(g, 1)
                for k in range(KD):
                    if 1 <= k and k + 1 < KD:
                        turn_c(g, k + 1)
                    hidden1(g, k)
                    if 0 <= k + 1 - (KD - KU) < KU and more:
                        next_up(g + 1, k + 1 - (KD - KU))
                if more:
                    next_up(g + 1, 5)
                score_rows(g)
                if more:
                    next_up(g + 1, 6)
                hidden2(g, 0)
                if more:
                    next_up(g + 1, 7)
                hidden2(g, 1)
                weights_rows(g)
                hidden2(g, 2)
                hidden2(g, 3)
                spread(g, 0)
                spread(g, 1)
                for u in range(4):
                    down_begin(g, u, more)
                for m in range(MF):
                    pe.wait_ge(c_h2lo, MF * g + m + 1)
                    if m == 0:
                        spread(g, 2)
                        spread(g, 3)
                    for u in range(4):
                        down_part(g, u, m)
                if has(g, 2):
                    for m in range(KH):
                        turn_agg(g + 2, m)
                for u in range(4, 8):
                    if u >= 6 and more:
                        turn_c(g + 1, u - 6)
                    down_begin(g, u, more)
                    for m in range(MF):
                        down_part(g, u, m)

            pe.wait_ge(b_split_v, 4)
            for m in range(KH):
                turn_agg(0, m)
            pe.wait_ge(c_alo, KH)
            for u in range(8):
                wait(pe, c_upv, u - 1)
                up(0, u, Y[u % 2])
            pe.wait_ge(w3_split_v, 1)
            for m in range(KH):
                turn_agg(1, m)
            turn_c(0, 0)
            turn_c(0, 1)
            pairs(pe, body_c)


_INS = ["x", "src", "dst", "L0_gnn_rms_w", "L0_gnn_W_down", "L0_gnn_Wl", "L0_gnn_Wr", "L0_gnn_att", "L0_gnn_W_up",
        "L0_ffn_expert_tokens", "L0_ffn_W1", "L0_ffn_b1", "L0_ffn_W2", "L0_ffn_b2", "L0_ffn_W3", "L0_ffn_b3"]


def kernel(**inputs):
    import numpy as np
    import concourse.bacc as bacc
    from concourse.bass_utils import run_bass_kernel_spmd

    nc = bacc.Bacc("TRN2", target_bir_lowering=False, num_devices=1)
    arrays, args = {}, []
    for name in _INS:
        a = np.ascontiguousarray(inputs[name])
        arrays[f"in_{name}"] = a
        args.append(nc.dram_tensor(f"in_{name}", a.shape, mybir.dt.from_np(a.dtype), kind="ExternalInput").ap())
    args.append(nc.dram_tensor("out_0", (N, D), F32, kind="ExternalOutput").ap())
    build(nc, *args)
    r = run_bass_kernel_spmd(nc, [arrays], core_ids=[0])
    return r.results[0]["out_0"]
```

```python
from contextlib import ExitStack

import concourse.bass as bass
from concourse import mybir

N, D = 10000, 1024
E = 5000
HID, H = 256, 4
HD = HID // H
NE, EH = 8, 64
P, J = 125, 4
G = P * J
NG = N // G
KD = D // 128
KH = HID // 128
MF = NE * EH // 128
HALF = 512
NC = E // P
CG = 2
NBG = NC // CG
TD = 4
CB = 4
NB = NC // CB
SPLIT = 112
LN_EPS, RMS_EPS = 1e-5, 1e-6
SLOPE = 0.2
TABLE = N + E // 2
CPG = NC // NG
MAPW = 100
HV = HID + H
FAR = -1.0e38

F32, F32R, BF16, I32 = mybir.dt.float32, mybir.dt.float32r, mybir.dt.bfloat16, mybir.dt.int32
ALU = mybir.AluOpType
ACT = mybir.ActivationFunctionType
AX = mybir.AxisListType


def wait(engine, sem, value):
    if isinstance(value, int) and value <= 0:
        return
    engine.wait_ge(sem, value)


def build(nc, x, src, dst, rms_w, w_down, wl, wr, att, w_up, tok, w1, b1, w2, b2, w3, b3, out):
    ctx = ExitStack()
    with ctx:
        origin = (nc.sbuf_base + 31) // 32 * 32

        def put(name, shape, dt, at):
            return nc.alloc_sbuf_tensor_at(name, shape, dt, offset=origin + at)

        def run_of(at, *items):
            made = []
            for name, shape, dt in items:
                made.append(put(name, shape, dt, at))
                size = 2 if dt == BF16 else 4
                for n in shape[1:]:
                    size *= n
                at += (size + 31) // 32 * 32
            return (*made, at)

        def sem(name):
            return ctx.enter_context(nc.semaphore(name))

        psum = ctx.enter_context(nc.psum_tensor("psum", [128, 8 * HALF], F32))
        bank = [psum[:, HALF * i:HALF * (i + 1)] for i in range(8)]
        table = nc.dram_tensor("node_table", [TABLE, 2 * HID], F32)
        where_from = nc.dram_tensor("where_from", [N + P, 1], I32)

        (ident, rmsw, b1c, b2c, neg_half, dup_mask, dup_rest, dst_col, dst_next_col, src_idx, dst_idx,
         scat_idx, row_of_edge, idx_now, row_now, from_idx, trash, last_of_chunk, eq_last, earlier,
         pe_pair, pexp, flags, through, chunk_flags, tie, at0) = run_of(
            0,
            ("ident", [128, 128], F32), ("rmsw", [128, KD], F32),
            ("b1c", [128, MF], F32), ("b2c", [128, MF], F32), ("neg_half", [P, J], F32),
            ("dup_mask", [2 * NE, 1], F32), ("dup_rest", [2 * NE, 1], F32),
            ("dst_col", [P + 1, NC], F32), ("dst_next_col", [P, NC], F32), ("src_idx", [P, NC], I32),
            ("dst_idx", [P, NC], I32), ("scat_idx", [P, NC], I32), ("row_of_edge", [P, NC], I32),
            ("idx_now", [P, J], I32),
            ("row_now", [P, CPG], I32), ("from_idx", [P, NG, J], I32), ("trash", [P, 1], F32),
            ("last_of_chunk", [NC, 1], F32), ("eq_last", [P, NC], F32), ("earlier", [NC, NC], F32),
            ("pe_pair", [P, 2, H, NC], F32), ("pexp", [P, 2, H, NC], F32), ("flags", [2 * NC, 2, P], F32),
            ("through", [2 * NC, 2, P], F32), ("chunk_flags", [2 * NC, 2, H], F32), ("tie", [P, NE, NE], F32))
        (att_bc, stat, mv, var, rstd, nbias, tok_st, b3_hl, expand, at1) = run_of(
            at0,
            ("att_bc", [P, HID], F32), ("stat", [P, J, 12], F32), ("mv", [P, 2, J, 2], F32),
            ("var", [P, 2, J], F32), ("rstd", [P, 2, J], F32), ("nbias", [P, 2, J], F32),
            ("tok_st", [128, KD, 128], F32R), ("b3_hl", [2 * NE, D], F32R), ("expand", [NE, NE * EH], F32R))

        wup_hi, wup_lo, w1_hi, w1_lo, at2 = run_of(
            at1,
            ("wup_hi", [128, KH, D], F32R), ("wup_lo", [128, KH, D], F32R),
            ("w1_hi", [128, KD, HALF], F32R), ("w1_lo", [128, KD, HALF], F32R))
        wup_raw = put("wup_raw", [128, KH, D], F32, at1 + KH * D * 4)
        w1_raw = put("w1_raw", [128, KD, HALF], F32, at1 + 2 * KH * D * 4 + KD * HALF * 4)
        w2_hi, w2_lo, w3_hi, w3_lo, at3 = run_of(
            at2,
            ("w2_hi", [128, MF, 128], F32R), ("w2_lo", [128, MF, 128], F32R),
            ("w3_hi", [128, MF, D], F32R), ("w3_lo", [128, MF, D], F32R))
        w2_raw = put("w2_raw", [128, MF, 128], F32, at2 + MF * 128 * 4)
        w3_raw = put("w3_raw", [128, MF, D], F32, at3 - MF * D * 4)

        (ax, axn, axt_hi, axt_lo, ht_hi, ht_lo, trow, wd_hi, wd_lo, wlr_hi, wlr_lo, a_end) = run_of(
            at2,
            ("ax", [P, 2, J * D], F32), ("axn", [P, 2, J, D], F32),
            ("axt_hi", [128, 4, G], F32R), ("axt_lo", [128, 4, G], F32R),
            ("ht_hi", [128, 2, KH, G], F32R), ("ht_lo", [128, 2, KH, G], F32R),
            ("trow", [P, 2, J * 2 * HID], F32),
            ("wd_hi", [128, KD, HID], F32R), ("wd_lo", [128, KD, HID], F32R),
            ("wlr_hi", [128, KH, 2 * HID], F32R), ("wlr_lo", [128, KH, 2 * HID], F32R))
        wd_raw = put("wd_raw", [128, KD, HID], F32, a_end - 2 * KH * 2 * HID * 4 - KD * HID * 4)
        wlr_raw = put("wlr_raw", [128, KH, 2 * HID], F32, a_end - KH * 2 * HID * 4)
        (idx_rows, idx_f, tok_rows, b3_raw, b3_hi, b3_lo, expand_raw, own_rows, _) = run_of(
            at1,
            ("idx_rows", [2 * NC, 3, P + 1], I32), ("idx_f", [2 * NC, 3, P + 1], F32), ("tok_rows", [NE, D], F32),
            ("b3_raw", [2 * NE, D], F32), ("b3_hi", [2 * NE, D], F32R), ("b3_lo", [2 * NE, D], F32),
            ("expand_raw", [NE, NE * EH], F32), ("own_rows", [MAPW, N // MAPW], I32))

        xls, xld, dst_row, at4 = run_of(
            at2, ("xls", [P + 1, NC, HV], F32), ("xld", [P, NC, HID], F32), ("dst_row", [P + 1, E], I32))
        td, msg, at5 = run_of(
            at4, ("td", [P, TD, CG, 2 * HID], F32), ("msg", [P, 2, 2, CG, HID], F32))
        zmat, b_end = run_of(at5, ("zmat", [P, NC, NC], F32))
        max_t, seg, tips, tip_row, carried, carried_t, _ = run_of(
            at4, ("max_t", [2 * NC, 2, P], F32), ("seg", [2 * NC, 2, 2, P], F32), ("tips", [2 * NC, 2, 2], F32),
            ("tip_row", [H, 3, 2 * NC], F32), ("carried", [H, 2, 2 * NC + 1], F32), ("carried_t", [2 * NC, 2, H], F32))
        (smat, orow, tot, rden, lsb, carry, _) = run_of(
            at4,
            ("smat", [P + 1, 2, CB, P], F32), ("orow", [P, 2, CB, HID], F32), ("tot", [P, CB, H], F32),
            ("rden", [P, CB, H], F32), ("lsb", [NC, HV], F32), ("carry", [NC, HV], F32))

        (cx1, cxn, cxt_hi, cxt_lo, gl, h_hi, h_lo, agg, aggt_hi, aggt_lo, sc_t, w_t, score, beats, beats2, rank,
         wdup, c_end) = run_of(
            at3,
            ("cx1", [P, J, D], F32), ("cxn", [P, J, D], F32),
            ("cxt_hi", [128, 2, G], F32R), ("cxt_lo", [128, 2, G], F32R), ("gl", [128, MF, G], F32),
            ("h_hi", [128, MF, G], F32R), ("h_lo", [128, MF, G], F32R), ("agg", [P, J, HID], F32),
            ("aggt_hi", [128, KH, G], F32R), ("aggt_lo", [128, KH, G], F32R),
            ("sc_t", [128, G], F32), ("w_t", [2 * NE, G], F32R), ("score", [P, J, NE], F32),
            ("beats", [P, J, NE, NE], F32), ("beats2", [P, J, NE, NE], F32), ("rank", [P, J, NE], F32),
            ("wdup", [P, J, 2, NE], F32))
        at_cx0 = (nc.sbuf_usable_end - origin - J * D * 4) // 32 * 32
        cx = [put("cx0", [P, J, D], F32, at_cx0), cx1]
        assert c_end <= at_cx0
        assert origin + max(a_end, b_end, c_end, at3) <= nc.sbuf_usable_end, (a_end, b_end, c_end)

        consts = sem("consts")
        raw_idx, raw_small, raw_wa, raw_wlr, raw_wc = (
            sem("raw_idx"), sem("raw_small"), sem("raw_wa"), sem("raw_wlr"), sem("raw_wc"))
        raw_dst_row, raw_w3 = sem("raw_dst_row"), sem("raw_w3")
        setup_v, setup_t, setup_s, setup_p = sem("setup_v"), sem("setup_t"), sem("setup_s"), sem("setup_p")
        first_loaded = [sem(f"first_loaded{j}") for j in range(J)]
        ax_loaded = [sem("ax_loaded0"), sem("ax_loaded1")]
        a_bn, a_aggr, a_var, a_rstd, a_nb = sem("a_bn"), sem("a_aggr"), sem("a_var"), sem("a_rstd"), sem("a_nb")
        a_xn, a_tp, a_hi, a_lo, a_mm = sem("a_xn"), sem("a_tp"), sem("a_hi"), sem("a_lo"), sem("a_mm")
        a_hhi, a_hlo, a_lr = sem("a_hhi"), sem("a_hlo"), sem("a_lr")
        a_ev_s, a_ev_v = sem("a_ev_s"), sem("a_ev_v")
        t_stored = [sem("t_stored0"), sem("t_stored1")]
        gathered = [sem(f"gathered{t}") for t in range(TD)]
        b_split_s, b3_split = sem("b_split_s"), sem("b3_split")
        b_xld, b_leak, b_mul, b_red = sem("b_xld"), sem("b_leak"), sem("b_mul"), sem("b_red")
        b_max, b_max_t, b_seg, b_tip, b_carried, b_back, b_exp = (
            sem("b_max"), sem("b_max_t"), sem("b_seg"), sem("b_tip"), sem("b_carried"), sem("b_back"), sem("b_exp"))
        b_zsel, b_v, b_l, b_lsb = sem("b_zsel"), sem("b_v"), sem("b_l"), sem("b_lsb")
        b_sb, b_num, b_den, b_self, b_out = sem("b_sb"), sem("b_num"), sem("b_den"), sem("b_self"), sem("b_out")
        h_aggr, h_var, h_rstd, h_nb = sem("h_aggr"), sem("h_var"), sem("h_rstd"), sem("h_nb")
        wd_split, wlr_split, b_flags = sem("wd_split"), sem("wlr_split"), sem("b_flags")
        b_sum, b_slope = sem("b_sum"), sem("b_slope")
        b_mask, carry_put, w1_split_p = sem("b_mask"), sem("carry_put"), sem("w1_split_p")
        map_copied, map_put, map_loaded = sem("map_copied"), sem("map_put"), sem("map_loaded")
        rows_stored = [sem("rows_stored0"), sem("rows_stored1")]
        cx_loaded = [[sem(f"cx_loaded{par}_{j}") for j in range(J)] for par in range(2)]
        out_stored = [[sem(f"out_stored{par}_{j}") for j in range(J)] for par in range(2)]
        agg_loaded = sem("agg_loaded")
        c_tp, c_mm, c_atp, c_up, c_rs, c_w2, c_wtp, c_wx, c_w3 = (
            sem("c_tp"), sem("c_mm"), sem("c_atp"), sem("c_up"), sem("c_rs"), sem("c_w2"), sem("c_wtp"),
            sem("c_wx"), sem("c_w3"))
        c_hi, c_ahi, c_g1, c_h1hi, c_g2, c_h2hi, c_xn = (
            sem("c_hi"), sem("c_ahi"), sem("c_g1"), sem("c_h1hi"), sem("c_g2"), sem("c_h2hi"), sem("c_xn"))
        c_lo, c_alo, c_sc, c_h1lo, c_upv, c_w3v, c_rt, c_w, c_wt, c_wmul, c_h2lo = (
            sem("c_lo"), sem("c_alo"), sem("c_sc"), sem("c_h1lo"), sem("c_upv"), sem("c_w3v"), sem("c_rt"),
            sem("c_w"), sem("c_wt"), sem("c_wmul"), sem("c_h2lo"))
        c_h1lo_p = sem("c_h1lo_p")
        c_bn, c_aggr, c_var, c_rstd, c_nb = sem("c_bn"), sem("c_aggr"), sem("c_var"), sem("c_rstd"), sem("c_nb")
        turns, turns_p = sem("turns"), sem("turns_p")
        w3_split_s, w3_split_v = sem("w3_split_s"), sem("w3_split_v")

        x_g = x.rearrange("(g p j) d -> g p (j d)", p=P, j=J)
        out_g = out.rearrange("(g p j) d -> g p (j d)", p=P, j=J)
        t_g = table[0:N, :].rearrange("(g p j) d -> g p (j d)", p=P, j=J)
        t_half = table[:, :].rearrange("n (a d) -> (n a) d", a=2)
        t_edge = t_half[2 * N:2 * N + E, :].rearrange("(c p) d -> p c d", p=P)

        T_A, H_A, X_A = bank[0:4], bank[4:6], bank[6:8]
        ACC, T_C, Y = bank[0:4], bank[4:6], bank[6:8]
        UP_BANK = [Y[1]] * 5 + [Y[0], Y[1], Y[0]]
        DOWN_BANK = [ACC[0], ACC[1], Y[1], Y[0], ACC[2], ACC[3], Y[0], Y[1]]
        W2P = MF + 1
        KU = 4

        WEIGHTING = [(0, slice(0, G // 2)), (0, slice(G // 2, G))] + [(m, slice(0, G)) for m in range(1, MF)]

        def messages(par):
            return psum[0:P, 2 * CG * HID * par:2 * CG * HID * (par + 1)].rearrange(
                "p (k c d) -> p k c d", k=2, c=CG)

        def batches_of_gathers(engine, body):
            for t in range(TD):
                body(t, t)
            with engine.Fori(1, NBG // TD) as i:
                for t in range(TD):
                    body(TD * i + t, t)

        FILL = 2 * CG * 16

        def wait_gathered(engine, b, t):
            wait(engine, gathered[t], FILL // TD * (b - t) + FILL)

        T_STORED = [32 * (NG // 2), 32 * (NG // 2) + 32]

        block = ctx.enter_context(nc.Block())

        def pairs(engine, body, peeled=1):
            for g in range(2 * peeled):
                body(g, g % 2)
            with engine.Fori(peeled, NG // 2 - 1) as i:
                for par in range(2):
                    body(2 * i + par, par)
            for par in range(2):
                body(NG - 2 + par, par)

        def has(g, more):
            return not isinstance(g, int) or 0 <= g + more < NG

        @block.sync
        def _(sp):
            def load_x(g, par):
                wait(sp, a_xn, J * (g - 1))
                sp.dma_start(ax[0:SPLIT, par, :], x_g[g, 0:SPLIT, :]).then_inc(ax_loaded[par], 16)
                sp.dma_start(ax[SPLIT:P, par, :], x_g[g, SPLIT:P, :]).then_inc(ax_loaded[par], 16)

            for j in range(J):
                for rows in (slice(0, SPLIT), slice(SPLIT, P)):
                    sp.dma_start(ax[rows, 0, D * j:D * (j + 1)], x_g[0, rows, D * j:D * (j + 1)]
                                 ).then_inc(first_loaded[j], 16)
            sp.dma_start(wd_raw[:, :, :], w_down.rearrange("(k p) n -> p k n", p=128)).then_inc(raw_wa, 16)
            sp.dma_start(rmsw[:, :], rms_w.rearrange("(k p) -> p k", p=128),
                         allow_slow_non_contiguous=True).then_inc(raw_wa, 16)
            load_x(1, 1)
            sp.dma_start(wlr_raw[:, :, 0:HID], wl.rearrange("(k p) n -> p k n", p=128)).then_inc(raw_wlr, 16)
            sp.dma_start(wlr_raw[:, :, HID:], wr.rearrange("(k p) n -> p k n", p=128)).then_inc(raw_wlr, 16)
            sp.wait_ge(consts, 1)
            sp.dma_start(idx_rows[0:NC, 0, 0:P], src.rearrange("(c p) -> c p", p=P)).then_inc(raw_idx, 16)
            for r in (0, NC):
                sp.dma_start(idx_rows[r:r + NC, 1, 0:P], dst.rearrange("(c p) -> c p", p=P)).then_inc(raw_idx, 16)
                sp.dma_start(idx_rows[r + 1:r + NC, 1, P:P + 1],
                             dst[0:(NC - 1) * P].rearrange("(c p) -> c p", p=P)[:, P - 1:P],
                             allow_slow_non_contiguous=True).then_inc(raw_idx, 16)
                sp.dma_start(idx_rows[r:r + NC - 1, 2, 0:P],
                             dst[1:1 + (NC - 1) * P].rearrange("(c p) -> c p", p=P)).then_inc(raw_idx, 16)
                sp.dma_start(idx_rows[r + NC - 1:r + NC, 2, 0:P - 1],
                             dst[1 + (NC - 1) * P:E].rearrange("(c p) -> c p", c=1)).then_inc(raw_idx, 16)
            sp.dma_start(tok_rows[:, :], tok).then_inc(raw_small, 16)
            sp.dma_start(b3_raw[0:NE, :], b3).then_inc(raw_small, 16)
            sp.dma_start(b3_raw[NE:2 * NE, :], b3).then_inc(raw_small, 16)
            sp.dma_start(att_bc[:, :], att.rearrange("h d -> (h d)").partition_broadcast(P)).then_inc(raw_small, 16)
            sp.dma_start(b1c[:, :], b1.rearrange("(m a) h -> (a h) m", a=2),
                         allow_slow_non_contiguous=True).then_inc(raw_small, 16)
            sp.dma_start(b2c[:, :], b2.rearrange("(m a) h -> (a h) m", a=2),
                         allow_slow_non_contiguous=True).then_inc(raw_small, 16)

            def body(g, par):
                if has(g, 2):
                    load_x(g + 2, par)

            pairs(sp, body)

            sp.wait_ge(map_put, 16 * (1 + NC))
            sp.dma_start(from_idx[:, :, :],
                         where_from[0:N, :].rearrange("(g p j) a -> p g (j a)", p=P, j=J)).then_inc(map_loaded, 16)

            sp.wait_ge(setup_v, 13)
            sp.wait_ge(consts, 3)
            sp.dma_start(wup_raw[:, :, :], w_up.rearrange("(k p) n -> p k n", p=128)).then_inc(raw_wc, 16)
            for k in range(KD):
                sp.dma_start(w1_raw[:, k, :].rearrange("p (e h) -> p e h", e=NE),
                             w1[:, 128 * k:128 * (k + 1), :].rearrange("e p h -> p e h")).then_inc(raw_wc, 16)
            for par in range(2):
                sp.wait_ge(t_stored[par], T_STORED[par])
            sp.wait_ge(b_xld, NBG)
            sp.dma_start(dst_row[:, :], dst.partition_broadcast(P + 1)).then_inc(raw_dst_row, 16)

            def load_cx(g, par, j):
                for rows in (slice(0, SPLIT), slice(SPLIT, P)):
                    sp.dma_start(cx[par][rows, j, :], x_g[g, rows, D * j:D * (j + 1)]
                                 ).then_inc(cx_loaded[par][j], 16)

            sp.wait_ge(b_lsb, 2)
            sp.dma_start(xls[P:P + 1, :, :], carry[:, :]).then_inc(carry_put, 16)
            for j in range(J):
                load_cx(0, 0, j)

            def store_rows(b, par):
                sp.wait_ge(b_out, b + 1)
                sp.dma_start(t_edge[:, bass.ds(CB * b, CB), :], orow[:, par, :, :]).then_inc(rows_stored[par], 16)

            with sp.Fori(0, NB // 2) as i:
                for par in range(2):
                    store_rows(2 * i + par, par)

            for par in range(2):
                sp.wait_ge(rows_stored[par], 16 * (NB // 2))
            sp.wait_ge(agg_loaded, 16 * J)
            for j in range(J):
                load_cx(1, 1, j)
            sp.wait_ge(consts, 4)
            w2_pairs = w2.rearrange("(m a) h k -> a h m k", a=2)
            for a in range(2):
                sp.dma_start(w2_raw[EH * a:EH * (a + 1), :, EH * a:EH * (a + 1)], w2_pairs[a]).then_inc(raw_w3, 16)
            sp.dma_start(w3_raw[:, :, :], w3.rearrange("(m a) h n -> (a h) m n", a=2)).then_inc(raw_w3, 16)

            def body_c(g, par):
                def reload(j):
                    sp.wait_ge(out_stored[par][j], 16 * (g + 2 - par))
                    load_cx(g + 2, par, j)

                for j in range(J):
                    sp.wait_ge(c_w3v, 8 * g + 2 * j + 2)
                    for rows in (slice(0, SPLIT), slice(SPLIT, P)):
                        sp.dma_start(out_g[g, rows, D * j:D * (j + 1)], cx[par][rows, j, :]
                                     ).then_inc(out_stored[par][j], 16)
                    if j >= 1 and has(g, 2):
                        reload(j - 1)
                if has(g, 2):
                    reload(J - 1)

            pairs(sp, body_c)
            for par in range(2):
                for j in range(J):
                    sp.wait_ge(out_stored[par][j], 16 * NG)

        @block.gpsimd
        def _(pool):
            pool.memset(idx_rows[:, :, :], -1)
            pool.memset(tok_st[:, :, :].bitcast(F32), 0.0)
            pool.memset(ident[:, :], 0.0).then_inc(consts, 1)
            pool.wait_ge(consts, 1)
            pool.affine_select(out=ident[:, :], in_=ident[:, :], compare_op=ALU.not_equal, fill=1.0, base=0,
                               pattern=[[-1, 128]], channel_multiplier=1).then_inc(consts, 1)
            pool.memset(neg_half[:, :], -0.5).then_inc(setup_p, 1)
            pool.memset(expand_raw[:, :], 1.0)
            pool.memset(dup_mask[:, :], 1.0)
            pool.memset(earlier[:, :], 1.0)
            pool.memset(tie[:, :, :], 1.0)
            pool.iota(own_rows[:, :], [[2, N // MAPW]], base=0, channel_multiplier=2 * N // MAPW)
            pool.iota(row_of_edge[:, :], [[P, NC]], base=2 * N, channel_multiplier=1)
            pool.iota(scat_idx[:, 0:1], [[0, 1]], base=N, channel_multiplier=1).then_inc(setup_p, 1)
            pool.wait_ge(setup_p, 2)
            pool.affine_select(out=dup_mask[:, :], in_=dup_mask[:, :], compare_op=ALU.is_gt, fill=0.0, base=NE,
                               pattern=[[0, 1]], channel_multiplier=-1)
            pool.affine_select(out=expand_raw[:, :], in_=expand_raw[:, :], compare_op=ALU.is_ge, fill=0.0, base=0,
                               pattern=[[1, NE * EH]], channel_multiplier=-EH)
            pool.affine_select(out=earlier[:, :], in_=earlier[:, :], compare_op=ALU.is_gt, fill=0.0, base=0,
                               pattern=[[1, NC]], channel_multiplier=-1)
            pool.affine_select(out=tie[:, :, :], in_=tie[:, :, :], compare_op=ALU.is_gt, fill=0.0, base=0,
                               pattern=[[1, NE], [-1, NE]], channel_multiplier=0).then_inc(setup_p, 1)
            pool.wait_ge(setup_p, 3)
            pool.affine_select(out=expand_raw[:, :], in_=expand_raw[:, :], compare_op=ALU.is_ge, fill=0.0,
                               base=EH - 1, pattern=[[-1, NE * EH]], channel_multiplier=EH).then_inc(consts, 1)

            pool.dma_start(where_from[0:N, :].rearrange("(p i) a -> p (i a)", p=MAPW), own_rows[:, :]
                           ).then_inc(map_put, 16)

            def rstd_a(g, par):
                pool.wait_ge(a_var, g + 1)
                pool.tensor_tensor(rstd[:, par, :], var[:, par, :], neg_half[:, :], ALU.pow).then_inc(a_rstd, 1)

            def body(g, par):
                if has(g, 2):
                    rstd_a(g + 2, par)
                if isinstance(g, int) and g == 0:
                    pool.wait_ge(setup_v, 9)
                pool.wait_ge(map_put, 16 * (CPG * g + 1))
                pool.sem_inc(turns_p, 1)
                pool.tensor_copy(idx_now[:, 0:CPG], scat_idx[:, bass.ds(CPG * g, CPG)])
                pool.tensor_copy(row_now[:, :], row_of_edge[:, bass.ds(CPG * g, CPG)]).then_inc(map_copied, 1)
                pool.wait_ge(map_copied, g + 1)
                pool.sem_inc(turns_p, 1)
                for q in range(CPG):
                    pool.wait_ge(map_put, 16 * (CPG * g + q + 1))
                    pool.sem_inc(turns_p, 1)
                    pool.indirect_dma_start(
                        out=where_from[:, :], out_offset=bass.IndirectOffsetOnAxis(ap=idx_now[:, q:q + 1], axis=0),
                        in_=row_now[:, q:q + 1], in_offset=None).then_inc(map_put, 16)

            rstd_a(0, 0)
            rstd_a(1, 1)
            pool.wait_ge(setup_s, 1)
            pool.tensor_tensor(wlr_lo[:, :, :], wlr_raw[:, :, :], wlr_hi[:, :, :].bitcast(F32), ALU.subtract
                               ).then_inc(wlr_split, 1)

            pairs(pool, body)

            for par in range(2):
                pool.wait_ge(t_stored[par], T_STORED[par])
            pool.wait_ge(setup_v, 9)
            for b in range(NBG):
                t = b % TD
                if b >= TD:
                    pool.wait_ge(b_xld, b - TD + 1)
                    pool.wait_ge(b_sum, b - TD + 1)
                for q in range(CG):
                    c = CG * b + q
                    pool.indirect_dma_start(
                        out=xls[0:P, c, 0:HID], out_offset=None, in_=t_half[0:2 * N, :],
                        in_offset=bass.IndirectOffsetOnAxis(ap=src_idx[:, c:c + 1], axis=0)
                    ).then_inc(gathered[t], 16)
                    pool.indirect_dma_start(
                        out=td[:, t, q, :], out_offset=None, in_=table[0:N, :],
                        in_offset=bass.IndirectOffsetOnAxis(ap=dst_idx[:, c:c + 1], axis=0)
                    ).then_inc(gathered[t], 16)

            pool.memset(zmat[:, :, :], 0.0).then_inc(b_zsel, 1)
            for n, (lo, raw, hi) in enumerate(((wup_lo, wup_raw, wup_hi), (w1_lo, w1_raw, w1_hi))):
                pool.wait_ge(b_split_s, n + 1)
                pool.tensor_tensor(lo[:, :, :], raw[:, :, :], hi[:, :, :].bitcast(F32), ALU.subtract
                                   ).then_inc(w1_split_p, 1)

            pool.wait_ge(b_exp, 1)
            with pool.Fori(0, NB) as b:
                rows = xld[:, bass.ds(CB * b, CB), :].rearrange("p c (h d) -> p c h d", h=H)
                pool.tensor_tensor(rows, rows,
                                   pexp[:, 1, :, bass.ds(CB * b, CB)].rearrange("p h c -> p c h").unsqueeze(3)
                                   .broadcast_to([P, CB, H, HD]), ALU.mult).then_inc(b_self, 1)
            pool.wait_ge(b_out, NB)
            pool.memset(w2_raw[:, :, :], 0.0).then_inc(consts, 1)

            def gather_rows(g):
                pool.tensor_copy(idx_now[:, :], from_idx[:, bass.ds(g, 1), :].rearrange("p g j -> p (g j)")
                                 ).then_inc(map_copied, 1)
                pool.wait_ge(map_copied, NG + 1 + g)
                pool.sem_inc(turns_p, 1)
                for j in range(J):
                    pool.indirect_dma_start(
                        out=agg[:, j, :], out_offset=None, in_=t_half,
                        in_offset=bass.IndirectOffsetOnAxis(ap=idx_now[:, j:j + 1], axis=0)
                    ).then_inc(agg_loaded, 16)

            def rstd_c(g, par):
                pool.wait_ge(c_var, g + 1)
                pool.tensor_tensor(rstd[:, par, :], var[:, par, :], neg_half[:, :], ALU.pow).then_inc(c_rstd, 1)

            pool.wait_ge(map_loaded, 16)
            for par in range(2):
                pool.wait_ge(rows_stored[par], 16 * (NB // 2))
            gather_rows(0)
            pool.wait_ge(c_atp, KH)
            gather_rows(1)
            for half, (var_sem, rstd_sem) in enumerate(((h_var, h_rstd), (c_var, c_rstd))):
                tiles = slice(2 * half, 2 * half + 2)
                pool.wait_ge(var_sem, 1)
                pool.tensor_tensor(rstd[:, 0, tiles], var[:, 0, tiles], neg_half[:, tiles], ALU.pow
                                   ).then_inc(rstd_sem, 1)

            def body_c(g, par):
                if has(g, 2):
                    pool.wait_ge(c_atp, KH * (g + 2))
                    pool.sem_inc(turns_p, 1)
                    gather_rows(g + 2)
                for m in range(1, MF):
                    pool.wait_ge(c_h1hi, MF * g + m + 1)
                    pool.tensor_tensor(h_lo[:, m, :], gl[:, m, :], h_hi[:, m, :].bitcast(F32),
                                       ALU.subtract).then_inc(c_h1lo_p, 1)
                if has(g, 1):
                    rstd_c(g + 1, 1 - par)

            pairs(pool, body_c)

        @block.scalar
        def _(act):
            def norm(g, par, j):
                act.wait_ge(a_nb, g + 1)
                wait(act, a_tp, KD * (g - 1))
                act.activation(axn[:, par, j, :], ax[:, par, D * j:D * (j + 1)], ACT.Identity,
                               bias=nbias[:, par, j:j + 1], scale=rstd[:, par, j:j + 1]).then_inc(a_xn, 1)

            def high(g, k):
                t = KD * g + k
                act.wait_ge(a_tp, t + 1)
                wait(act, a_mm, t - 3)
                act.activation(axt_hi[:, k % 4, :], T_A[k % 4][:, 0:G], ACT.Copy).then_inc(a_hi, 1)

            def body(g, par):
                norms = {j + 2: (j,) for j in range(J)}
                if isinstance(g, int) and g == 0:
                    norms = {5: (0,), 6: (1,), 7: (2, 3)}
                for k in range(2, KD):
                    high(g, k)
                    for j in norms.get(k, ()):
                        if has(g, 1):
                            norm(g + 1, 1 - par, j)
                    if k == 5 and has(g, -2):
                        store_table(g - 2, par)
                for m in range(KH):
                    act.wait_ge(a_mm, KD * (g + 1))
                    wait(act, a_lr, J * (g - 1))
                    act.activation(ht_hi[:, par, m, :], H_A[m][:, 0:G], ACT.Copy).then_inc(a_hhi, 1)
                if has(g, -1):
                    empty_lr(g - 1, 1 - par, 0)
                if has(g, 1):
                    high(g + 1, 0)
                    high(g + 1, 1)
                if has(g, -1):
                    empty_lr(g - 1, 1 - par, 2)

            def empty_lr(g, par, j):
                act.wait_ge(a_lr, J * g + j + 1)
                wait(act, t_stored[par], 16 * (g - par))
                act.activation(trow[:, par, 2 * HID * j:2 * HID * (j + 1)], X_A[0][0:P, :],
                               ACT.Copy).then_inc(a_ev_s, 1)

            def store_table(g, par):
                act.wait_ge(a_ev_s, 2 * (g + 1))
                act.wait_ge(a_ev_v, 2 * (g + 1))
                act.dma_start(t_g[g, 0:SPLIT, :], trow[0:SPLIT, par, :]).then_inc(t_stored[par], 16)
                act.dma_start(t_g[g, SPLIT:P, :], trow[SPLIT:P, par, :]).then_inc(t_stored[par], 16)

            for j in range(J):
                norm(0, 0, j)
            high(0, 0)
            high(0, 1)
            act.wait_ge(raw_wlr, 16 * 2)
            act.activation(wlr_hi[:, :, :], wlr_raw[:, :, :], ACT.Copy).then_inc(setup_s, 1)
            pairs(act, body, 2)
            store_table(NG - 2, 0)
            for half in range(2):
                empty_lr(NG - 1, 1, 2 * half)
                act.wait_ge(a_ev_v, 2 * (NG - 1) + half + 1)
                act.wait_ge(a_ev_s, 2 * (NG - 1) + half + 1)
                columns = slice(4 * HID * half, 4 * HID * (half + 1))
                for rows in (slice(0, SPLIT), slice(SPLIT, P)):
                    act.dma_start(t_g[NG - 1, rows, columns], trow[rows, 1, columns]).then_inc(t_stored[1], 16)

            act.wait_ge(raw_wc, 16 * (1 + KD))
            act.activation(wup_hi[:, :, :], wup_raw[:, :, :], ACT.Copy).then_inc(b_split_s, 1)
            act.activation(w1_hi[:, :, :], w1_raw[:, :, :], ACT.Copy).then_inc(b_split_s, 1)

            def body_b(b, t):
                wait_gathered(act, b, t)
                act.activation(xld[:, bass.ds(CG * b, CG), :], td[:, t, :, 0:HID], ACT.Copy).then_inc(b_xld, 1)
                act.wait_ge(b_sum, b + 1)
                wait(act, b_red, 2 * (b - 1))
                act.activation(msg[:, t % 2, :, :, :], messages(t % 2), ACT.Copy, scale=SLOPE).then_inc(b_slope, 1)

            batches_of_gathers(act, body_b)
            act.wait_ge(b_max, 5)
            act.activation(pexp[:, :, :, :], pe_pair[:, :, :, :], ACT.Exp).then_inc(b_exp, 1)

            def split_agg(m, g):
                act.wait_ge(c_atp, KH * g + m + 1)
                wait(act, c_up, 8 * g)
                act.activation(aggt_hi[:, m, :], T_C[m][:, 0:G], ACT.Copy).then_inc(c_ahi, 1)

            def norm_c(g, par, tiles=range(J), nb_sem=c_nb):
                for j in tiles:
                    act.wait_ge(nb_sem, g + 1)
                    wait(act, c_tp, KD * g)
                    act.activation(cxn[:, j, :], cx[par][:, j, :], ACT.Identity,
                                   bias=nbias[:, par, j:j + 1], scale=rstd[:, par, j:j + 1]).then_inc(c_xn, 1)

            def high_x(g, k):
                t = KD * g + k
                act.wait_ge(c_tp, t + 1)
                wait(act, c_mm, t - 1)
                act.activation(cxt_hi[:, k % 2, :], T_C[k % 2][:, 0:G], ACT.Copy).then_inc(c_hi, 1)

            def gelu1(g, m):
                act.wait_ge(c_mm, KD * (g + 1))
                wait(act, c_h2lo, W2P * (g - 1) + m + 2)
                act.activation(gl[:, m, :], ACC[m][:, 0:G], ACT.Gelu, bias=b1c[:, m:m + 1]).then_inc(c_g1, 1)
                act.wait_ge(c_g1, MF * g + m + 1)
                wait(act, c_w3, 8 * g)
                act.activation(h_hi[:, m, :], gl[:, m, :], ACT.Copy).then_inc(c_h1hi, 1)

            def gelu2(g, m):
                act.wait_ge(c_w2, MF * g + m + 1)
                act.activation(gl[:, m, :], ACC[m][:, 0:G], ACT.Gelu, bias=b2c[:, m:m + 1]).then_inc(c_g2, 1)

            def high2(g, step):
                m, rows = WEIGHTING[step]
                act.wait_ge(c_wmul, W2P * g + step + 1)
                act.activation(h_hi[:, m, rows], gl[:, m, rows], ACT.Copy).then_inc(c_h2hi, 1)

            def body_c(g, par):
                for k in range(2, KD):
                    high_x(g, k)
                    if isinstance(g, int) and g == 0:
                        if k == 2:
                            act.wait_ge(raw_w3, 16 * 3)
                            act.activation(w2_hi[:, :, :], w2_raw[:, :, :], ACT.Copy).then_inc(w3_split_s, 1)
                        elif k < 3 + MF:
                            act.activation(w3_hi[:, k - 3, :], w3_raw[:, k - 3, :], ACT.Copy
                                           ).then_inc(w3_split_s, 1)
                for m in range(MF):
                    gelu1(g, m)
                for m in range(MF):
                    gelu2(g, m)
                for step in range(W2P):
                    high2(g, step)
                if has(g, 2):
                    for m in range(KH):
                        split_agg(m, g + 2)
                if has(g, 1):
                    norm_c(g + 1, 1 - par)
                    high_x(g + 1, 0)
                    high_x(g + 1, 1)

            for m in range(KH):
                split_agg(m, 0)
            norm_c(0, 0, range(0, 2), h_nb)
            for m in range(KH):
                split_agg(m, 1)
            norm_c(0, 0, range(2, J))
            high_x(0, 0)
            high_x(0, 1)
            pairs(act, body_c)

        @block.vector
        def _(dve):
            def bn(g, par, piece, src_tile, done):
                j, n = piece // 2, piece % 2
                dve.bn_stats(stat[:, j, 6 * n:6 * n + 6],
                             src_tile[:, HALF * n:HALF * (n + 1)]).then_inc(done, 1)

            def moments(g, par, bn_sem, aggr_sem, var_sem, scale, shift):
                dve.wait_ge(bn_sem, 8 * (g + 1))
                dve.sem_inc(turns, 1)
                for j in range(J):
                    last = dve.bn_aggr(mv[:, par, j, :], stat[:, j, :])
                last.then_inc(aggr_sem, 1)
                dve.wait_ge(aggr_sem, g + 1)
                dve.tensor_scalar(var[:, par, :], mv[:, par, :, 1], scale, shift, ALU.mult, ALU.add
                                  ).then_inc(var_sem, 1)

            def bias_of(g, par, rstd_sem, nb_sem):
                dve.wait_ge(rstd_sem, g + 1)
                dve.scalar_tensor_tensor(nbias[:, par, :], mv[:, par, :, 0], -1.0, rstd[:, par, :],
                                         ALU.mult, ALU.mult).then_inc(nb_sem, 1)

            def moments_a(g, par):
                moments(g, par, a_bn, a_aggr, a_var, 1.0 + RMS_EPS, LN_EPS * RMS_EPS)

            def bn_a(g, par, piece):
                if isinstance(g, int) and g == 0:
                    if piece % 2 == 0:
                        dve.wait_ge(first_loaded[piece // 2], 32)
                elif piece == 0:
                    dve.wait_ge(ax_loaded[par], 16 * (g + par))
                    wait(dve, a_aggr, g)
                bn(g, par, piece, ax[:, par, D * (piece // 2):D * (piece // 2 + 1)], a_bn)

            for piece in range(8):
                bn_a(0, 0, piece)
            moments_a(0, 0)
            bias_of(0, 0, a_rstd, a_nb)

            def low(g, k):
                dve.wait_ge(a_hi, KD * g + k + 1)
                dve.tensor_tensor(axt_lo[:, k % 4, :], T_A[k % 4][:, 0:G], axt_hi[:, k % 4, :].bitcast(F32),
                                  ALU.subtract).then_inc(a_lo, 1)

            dve.wait_ge(raw_wa, 16 * 2)
            for k in range(KD):
                dve.tensor_scalar(wd_hi[:, k, :], wd_raw[:, k, :], rmsw[:, k:k + 1], None, ALU.mult
                                  ).then_inc(wd_split, 1)
            for k in range(KD):
                dve.wait_ge(wd_split, k + 1)
                last = dve.scalar_tensor_tensor(wd_lo[:, k, :], wd_raw[:, k, :], rmsw[:, k:k + 1],
                                                wd_hi[:, k, :].bitcast(F32), ALU.mult, ALU.subtract)
            last.then_inc(setup_v, 2)
            low(0, 0)
            low(0, 1)

            def indices_setup():
                dve.wait_ge(setup_t, 1)
                dve.tensor_scalar(src_idx[:, :], X_A[0][0:P, 0:NC], 2.0, None, ALU.mult)
                dve.tensor_copy(dst_idx[:, :], X_A[0][0:P, NC:2 * NC])
                dve.tensor_copy(dst_col[:, :], X_A[0][0:P + 1, NC:2 * NC])
                dve.tensor_copy(dst_next_col[:, :], X_A[0][0:P, 2 * NC:3 * NC]).then_inc(setup_v, 1)
                dve.tensor_copy(last_of_chunk[:, :], idx_f[0:NC, 1, P - 1:P])
                dve.tensor_tensor(flags[:, 0, 1:P], idx_f[:, 1, 1:P], idx_f[:, 1, 0:P - 1], ALU.not_equal)
                dve.tensor_tensor(flags[:, 0, 0:1], idx_f[:, 1, 0:1], idx_f[:, 1, P:P + 1], ALU.not_equal)
                dve.tensor_tensor(flags[:, 1, :], idx_f[:, 1, 0:P], idx_f[:, 2, 0:P], ALU.not_equal)
                dve.wait_ge(setup_p, 2)
                dve.tensor_copy(trash[:, :], scat_idx[:, 0:1]).then_inc(setup_v, 1)
                dve.wait_ge(setup_v, 5)
                dve.tensor_scalar(flags[:, :, :], flags[:, :, :], FAR, None, ALU.mult)
                dve.tensor_tensor(dst_next_col[:, :], dst_next_col[:, :], dst_col[0:P, :],
                                  ALU.is_equal).then_inc(setup_v, 1)
                dve.tensor_scalar(eq_last[:, :], dst_col[0:P, :], -1.0, trash[:, 0:1], ALU.mult, ALU.add
                                  ).then_inc(setup_v, 1)
                dve.wait_ge(setup_v, 7)
                dve.tensor_tensor(dst_next_col[:, :], dst_next_col[:, :], eq_last[:, :],
                                  ALU.mult).then_inc(setup_v, 1)
                dve.wait_ge(setup_v, 8)
                dve.tensor_tensor(scat_idx[:, :], dst_col[0:P, :], dst_next_col[:, :], ALU.add
                                  ).then_inc(setup_v, 1)

            def experts_setup():
                dve.wait_ge(setup_t, 2)
                tok_t = X_A[1][:, 0:KD * NE].rearrange("p (k e) -> p k e", e=NE)
                dve.tensor_copy(tok_st[:, :, 0:NE], tok_t).then_inc(setup_v, 1)
                dve.wait_ge(setup_v, 10)
                dve.tensor_tensor(tok_st[:, :, NE:2 * NE], tok_t, tok_st[:, :, 0:NE].bitcast(F32), ALU.subtract
                                  ).then_inc(setup_v, 1)

            def late_setup(k):
                if k == 3:
                    dve.tensor_tensor_scan(through[:, 0, :], flags[:, 0, :], flags[:, 0, :], 0.0, ALU.min, ALU.min)
                    dve.tensor_tensor_scan(through[:, 1, ::-1], flags[:, 1, ::-1], flags[:, 1, ::-1], 0.0,
                                           ALU.min, ALU.min).then_inc(b_flags, 1)
                    dve.wait_ge(b_flags, 1)
                    for way, at in ((0, P - 1), (1, 0)):
                        dve.tensor_copy(chunk_flags[:, way, :], through[:, way, at:at + 1].broadcast_to([2 * NC, H])
                                        ).then_inc(b_flags, 1)
                elif k == 4:
                    dve.tensor_copy(b3_hi[:, :], b3_raw[:, :])
                    dve.tensor_scalar(dup_rest[:, :], dup_mask[:, :], -1.0, 1.0, ALU.mult, ALU.add)
                    dve.wait_ge(consts, 3)
                    dve.tensor_copy(expand[:, :], expand_raw[:, :]).then_inc(setup_v, 1)
                elif k == 5:
                    dve.wait_ge(setup_v, 12)
                    dve.tensor_tensor(b3_lo[:, :], b3_raw[:, :], b3_hi[:, :].bitcast(F32), ALU.subtract
                                      ).then_inc(b3_split, 1)
                elif k == 6:
                    dve.wait_ge(b3_split, 1)
                    dve.tensor_scalar(b3_lo[:, :], b3_lo[:, :], dup_rest[:, 0:1], None, ALU.mult
                                      ).then_inc(b3_split, 1)
                elif k == 7:
                    dve.wait_ge(b3_split, 2)
                    dve.scalar_tensor_tensor(b3_hl[:, :], b3_hi[:, :].bitcast(F32), dup_mask[:, 0:1],
                                             b3_lo[:, :], ALU.mult, ALU.add).then_inc(setup_v, 1)

            def empty_lr(g, par, j):
                dve.wait_ge(a_lr, J * g + j + 1)
                wait(dve, t_stored[par], 16 * (g - par))
                dve.tensor_copy(trow[:, par, 2 * HID * j:2 * HID * (j + 1)], X_A[1][0:P, :]).then_inc(a_ev_v, 1)

            def body(g, par):
                at_start = isinstance(g, int) and g == 0
                for k in range(2, KD):
                    low(g, k)
                    if at_start:
                        if k == 2:
                            for piece in range(8):
                                bn_a(1, 1, piece)
                            moments_a(1, 1)
                        elif k == 3:
                            bias_of(1, 1, a_rstd, a_nb)
                        else:
                            for piece in range(2 * (k - 4), 2 * (k - 3)):
                                bn_a(2, 0, piece)
                    elif isinstance(g, int) and g == NG - 2:
                        late_setup(k)
                    elif has(g, 2):
                        bn_a(g + 2, par, k - 2)
                        if k >= 6:
                            bn_a(g + 2, par, k)
                if at_start:
                    dve.wait_ge(raw_idx, 16 * 9)
                    dve.tensor_copy(idx_f[:, :, :], idx_rows[:, :, :]).then_inc(setup_v, 1)
                for m in range(KH):
                    dve.wait_ge(a_hhi, KH * g + m + 1)
                    dve.tensor_tensor(ht_lo[:, par, m, :], H_A[m][:, 0:G],
                                      ht_hi[:, par, m, :].bitcast(F32), ALU.subtract).then_inc(a_hlo, 1)
                if has(g, 1):
                    low(g + 1, 0)
                if has(g, -1):
                    empty_lr(g - 1, 1 - par, 1)
                if has(g, 2):
                    moments_a(g + 2, par)
                if has(g, 1):
                    low(g + 1, 1)
                if has(g, 2):
                    bias_of(g + 2, par, a_rstd, a_nb)
                if has(g, -1):
                    empty_lr(g - 1, 1 - par, 3)
                if at_start:
                    dve.wait_ge(raw_small, 16 * 6)
                    indices_setup()
                    experts_setup()

            pairs(dve, body, 2)
            empty_lr(NG - 1, 1, 1)
            empty_lr(NG - 1, 1, 3)

            def sum_scores(b, t):
                par = t % 2
                dve.wait_ge(b_slope, b + 1)
                dve.tensor_tensor(msg[:, par, :, :, :], messages(par), msg[:, par, :, :, :], ALU.max
                                  ).then_inc(b_leak, 1)
                dve.wait_ge(b_leak, b + 1)
                rows = msg[:, par, :, :, :].rearrange("p k c d -> p (k c) d")
                dve.tensor_tensor(rows, rows, att_bc[:, :].unsqueeze(1).broadcast_to([P, 2 * CG, HID]),
                                  ALU.mult).then_inc(b_mul, 1)
                dve.wait_ge(b_mul, b + 1)
                for kind in range(2):
                    dve.tensor_reduce(
                        pe_pair[:, kind, :, bass.ds(CG * b, CG)].rearrange("p h c -> p c h"),
                        msg[:, par, kind, :, :].rearrange("p c (h d) -> p c h d", h=H),
                        AX.X, ALU.add).then_inc(b_red, 1)

            batches_of_gathers(dve, sum_scores)
            dve.wait_ge(b_red, 2 * NBG)
            dve.tensor_tensor(pexp[:, 0, :, :], pe_pair[:, 0, :, :], pe_pair[:, 1, :, :], ALU.max
                              ).then_inc(b_max, 1)
            dve.wait_ge(b_xld, NBG)
            for q in range(2):
                dve.wait_ge(b_max_t, q + 1)
                dve.tensor_copy(max_t[:, q, :], bank[q][0:2 * NC, 0:P]).then_inc(b_max, 1)
            for q in range(2):
                dve.wait_ge(b_max, q + 2)
                dve.tensor_tensor_scan(seg[:, 0, q, :], flags[:, 0, :], max_t[:, q, :], FAR, ALU.add, ALU.max
                                       ).then_inc(b_seg, 1)
                dve.tensor_tensor_scan(seg[:, 1, q, ::-1], flags[:, 1, ::-1], max_t[:, q, ::-1], FAR, ALU.add,
                                       ALU.max).then_inc(b_seg, 1)
            dve.wait_ge(b_seg, 4)
            dve.tensor_copy(tips[:, 0, :], seg[:, 0, :, P - 1])
            dve.tensor_copy(tips[:, 1, :], seg[:, 1, :, 0]).then_inc(b_tip, 1)
            dve.memset(carried[:, 0, 0:1], FAR)
            dve.memset(carried[:, 1, 2 * NC:2 * NC + 1], FAR)
            dve.wait_ge(b_max_t, 3)
            dve.tensor_copy(tip_row[:, :, :], bank[2][0:H, 0:3 * 2 * NC].rearrange("p (a c) -> p a c", a=3)
                            ).then_inc(b_tip, 1)
            dve.wait_ge(b_tip, 2)
            dve.tensor_tensor_scan(carried[:, 0, 1:2 * NC + 1], tip_row[:, 1, :], tip_row[:, 0, :], FAR,
                                   ALU.add, ALU.max)
            dve.tensor_tensor_scan(carried[:, 1, 0:2 * NC][:, ::-1], tip_row[:, 2, ::-1], tip_row[:, 0, ::-1], FAR,
                                   ALU.add, ALU.max).then_inc(b_tip, 1)
            dve.wait_ge(b_max_t, 4)
            dve.tensor_copy(carried_t[:, :, :], bank[3][0:2 * NC, 0:2 * H].rearrange("p (a r) -> p a r", a=2)
                            ).then_inc(b_carried, 1)
            dve.wait_ge(b_carried, 1)
            for way in range(2):
                for q in range(2):
                    dve.scalar_tensor_tensor(seg[:, way, q, :], through[:, way, :],
                                             carried_t[:, way, 2 * way + q:2 * way + q + 1], seg[:, way, q, :],
                                             ALU.add, ALU.max).then_inc(b_carried, 1)
            dve.wait_ge(b_carried, 5)
            dve.tensor_tensor(max_t[:, :, :], seg[:, 0, :, :], seg[:, 1, :, :], ALU.max).then_inc(b_carried, 1)
            dve.wait_ge(raw_dst_row, 16)
            dve.tensor_tensor(eq_last[:, :], dst_col[0:P, :], dst_row[0:P, P - 1:E:P], ALU.is_equal
                              ).then_inc(b_mask, 1)
            dve.scalar_tensor_tensor(earlier[:, 1:NC], dst_row[0:NC, P - 1:E - P:P], last_of_chunk[:, 0:1],
                                     earlier[:, 1:NC], ALU.is_equal, ALU.mult).then_inc(b_mask, 1)
            dve.wait_ge(b_zsel, 1)
            dve.wait_ge(b_mask, 1)
            dve.tensor_copy(zmat[:, :, :].rearrange("p a b -> p (a b)")[:, 0:NC * NC:NC + 1], eq_last[:, :]
                            ).then_inc(b_mask, 1)
            for kind in range(2):
                dve.wait_ge(b_back, 2)
                dve.tensor_tensor(pe_pair[:, kind, :, :], pe_pair[:, kind, :, :],
                                  bank[2][0:P, 0:H * NC].rearrange("p (h c) -> p h c", h=H),
                                  ALU.subtract).then_inc(b_max, 1)
            dve.wait_ge(b_exp, 1)

            dve.tensor_copy(xls[0:P, :, HID:HV], pexp[:, 0, :, :].rearrange("p h c -> p c h"))

            def weigh(b):
                rows = xls[0:P, bass.ds(CB * b, CB), 0:HID].rearrange("p c (h d) -> p c h d", h=H)
                dve.tensor_tensor(rows, rows,
                                  pexp[:, 0, :, bass.ds(CB * b, CB)].rearrange("p h c -> p c h").unsqueeze(3)
                                  .broadcast_to([P, CB, H, HD]), ALU.mult).then_inc(b_v, 1)

            with dve.Fori(0, NB) as b:
                weigh(b)

            def same_segment(b, par):
                wait(dve, b_num, b - 1)
                dve.tensor_tensor(smat[:, par, :, :],
                                  dst_row[:, bass.ds(CB * P * b, CB * P)].rearrange("p (c e) -> p c e", c=CB),
                                  dst_col[:, bass.ds(CB * b, CB)].unsqueeze(2).broadcast_to([P + 1, CB, P]),
                                  ALU.is_equal).then_inc(b_sb, 1)

            same_segment(0, 0)
            same_segment(1, 1)
            dve.wait_ge(b_l, 1)
            dve.tensor_copy(lsb[:, :], bank[3][0:NC, 0:HV]).then_inc(b_lsb, 1)
            dve.wait_ge(b_l, 2)
            dve.tensor_copy(carry[:, :], bank[4][0:NC, 0:HV]).then_inc(b_lsb, 1)

            def finish(b, par):
                sums = psum[0:P, 4 * HALF * par:4 * HALF * (par + 1)].rearrange("p (q n) -> p q n", q=CB)
                own = pexp[:, 1, :, bass.ds(CB * b, CB)].rearrange("p h c -> p c h")
                rows = orow[:, par, :, :].rearrange("p q (h d) -> p q h d", h=H)
                dve.wait_ge(b_num, b + 1)
                dve.scalar_tensor_tensor(tot[:, :, :], sums[:, :, HID:HV], 1e-16, own, ALU.add, ALU.add
                                         ).then_inc(b_den, 1)
                dve.wait_ge(b_self, b + 1)
                wait(dve, rows_stored[par], 8 * (b - par))
                dve.tensor_tensor(orow[:, par, :, :], sums[:, :, 0:HID], xld[:, bass.ds(CB * b, CB), :], ALU.add
                                  ).then_inc(b_den, 1)
                dve.wait_ge(b_den, 3 * b + 1)
                dve.reciprocal(rden[:, :, :], tot[:, :, :]).then_inc(b_den, 1)
                if has_batch(b, 2):
                    same_segment(b + 2, par)
                dve.wait_ge(b_den, 3 * b + 3)
                dve.tensor_tensor(rows, rows, rden[:, :, :].unsqueeze(3).broadcast_to([P, CB, H, HD]), ALU.mult
                                  ).then_inc(b_out, 1)

            def has_batch(b, more):
                return not isinstance(b, int) or b + more < NB

            for par in range(2):
                finish(par, par)
            with dve.Fori(1, NB // 2 - 1) as i:
                for par in range(2):
                    finish(2 * i + par, par)
            for par in range(2):
                finish(NB - 2 + par, par)

            def low_agg(m, g):
                dve.wait_ge(c_ahi, KH * g + m + 1)
                dve.tensor_tensor(aggt_lo[:, m, :], T_C[m][:, 0:G], aggt_hi[:, m, :].bitcast(F32),
                                  ALU.subtract).then_inc(c_alo, 1)

            def low_x(g, k):
                dve.wait_ge(c_hi, KD * g + k + 1)
                dve.tensor_tensor(cxt_lo[:, k % 2, :], T_C[k % 2][:, 0:G], cxt_hi[:, k % 2, :].bitcast(F32),
                                  ALU.subtract).then_inc(c_lo, 1)

            def residual(g, par, u, y):
                j, n = u // 2, u % 2
                if n == 0:
                    dve.wait_ge(cx_loaded[par][j], 16 * (g + 2 - par))
                dve.wait_ge(c_up, 8 * g + u + 1)
                piece = cx[par][:, j, HALF * n:HALF * (n + 1)]
                dve.tensor_tensor(piece, piece, y[0:P, :], ALU.add).then_inc(c_upv, 1)

            def bn_c(g, par, u):
                if u == 0:
                    wait(dve, c_aggr, g)
                dve.wait_ge(c_upv, 8 * g + u + 1)
                bn(g, par, u, cx[par][:, u // 2, :], c_bn)

            def moments_c(g, par):
                moments(g, par, c_bn, c_aggr, c_var, 1.0, LN_EPS)

            def low1(g, m):
                dve.wait_ge(c_h1hi, MF * g + m + 1)
                dve.tensor_tensor(h_lo[:, m, :], gl[:, m, :], h_hi[:, m, :].bitcast(F32),
                                  ALU.subtract).then_inc(c_h1lo, 1)

            def low2(g, step):
                m, rows = WEIGHTING[step]
                dve.wait_ge(c_h2hi, W2P * g + step + 1)
                dve.tensor_tensor(h_lo[:, m, rows], gl[:, m, rows], h_hi[:, m, rows].bitcast(F32),
                                  ALU.subtract).then_inc(c_h2lo, 1)

            def weight(g, step):
                m, rows = WEIGHTING[step]
                dve.wait_ge(c_g2, MF * g + m + 1)
                dve.wait_ge(c_wx, MF * g + m + 1)
                dve.tensor_tensor(gl[:, m, rows], gl[:, m, rows], T_C[m % 2][:, rows], ALU.mult
                                  ).then_inc(c_wmul, 1)

            def route(g):
                dve.wait_ge(c_rs, g + 1)
                parts = T_C[0][0:P, :].rearrange("p (j e) -> p j e", j=J)
                dve.tensor_copy(score[:, :, :], parts[:, :, 0:NE]).then_inc(c_rt, 1)
                dve.wait_ge(c_rt, 5 * g + 1)
                dve.tensor_tensor(score[:, :, :], score[:, :, :], parts[:, :, NE:2 * NE], ALU.add).then_inc(c_rt, 1)
                dve.wait_ge(c_rt, 5 * g + 2)
                other = score[:, :, :].unsqueeze(2).broadcast_to([P, J, NE, NE])
                own = score[:, :, :].unsqueeze(3).broadcast_to([P, J, NE, NE])
                dve.tensor_tensor(beats[:, :, :, :], other, own, ALU.is_gt)
                dve.tensor_tensor(beats2[:, :, :, :], other, own, ALU.is_equal).then_inc(c_rt, 1)
                dve.wait_ge(c_rt, 5 * g + 3)
                dve.tensor_tensor(beats2[:, :, :, :], beats2[:, :, :, :],
                                  tie[:, :, :].unsqueeze(1).broadcast_to([P, J, NE, NE]), ALU.mult
                                  ).then_inc(c_rt, 1)
                dve.wait_ge(c_rt, 5 * g + 4)
                dve.tensor_tensor(beats[:, :, :, :], beats[:, :, :, :], beats2[:, :, :, :], ALU.add
                                  ).then_inc(c_rt, 1)
                dve.wait_ge(c_rt, 5 * g + 5)
                dve.tensor_reduce(rank[:, :, :], beats[:, :, :, :], AX.X, ALU.add).then_inc(c_w, 1)
                dve.wait_ge(c_w, 3 * g + 1)
                for a in range(2):
                    dve.tensor_scalar(wdup[:, :, a, :], rank[:, :, :], 2.0, 0.5, ALU.is_lt, ALU.mult
                                      ).then_inc(c_w, 1)

            def weights_t(g):
                dve.wait_ge(c_wtp, g + 1)
                wait(dve, c_w3, 8 * g)
                dve.tensor_copy(w_t[:, :], T_C[1][0:2 * NE, 0:G]).then_inc(c_wt, 1)

            def result(g, par, u):
                j, n = u // 2, u % 2
                dve.wait_ge(c_w3, 8 * g + u + 1)
                piece = cx[par][:, j, HALF * n:HALF * (n + 1)]
                dve.tensor_tensor(piece, piece, DOWN_BANK[u][0:P, :], ALU.add).then_inc(c_w3v, 1)

            def body_c(g, par):
                nxt, npar, more = g + 1, 1 - par, has(g, 1)

                def next_residual(u):
                    if more:
                        residual(nxt, npar, u, UP_BANK[u])

                def next_bn(u):
                    if more:
                        bn_c(nxt, npar, u)

                for k in range(2, KD):
                    low_x(g, k)
                    if 0 <= k - (KD - KU) < KU:
                        next_residual(k - (KD - KU))
                        next_bn(k - (KD - KU))
                    if isinstance(g, int) and g == 0:
                        if k == 2:
                            dve.wait_ge(w3_split_s, 1)
                            dve.tensor_tensor(w2_lo[:, :, :], w2_raw[:, :, :], w2_hi[:, :, :].bitcast(F32),
                                              ALU.subtract).then_inc(w3_split_v, 1)
                        elif k < 3 + MF:
                            m = k - 3
                            dve.wait_ge(w3_split_s, m + 2)
                            dve.tensor_tensor(w3_lo[:, m, :], w3_raw[:, m, :], w3_hi[:, m, :].bitcast(F32),
                                              ALU.subtract).then_inc(w3_split_v, 1)
                dve.wait_ge(c_mm, KD * (g + 1))
                wait(dve, c_rs, g)
                dve.tensor_copy(sc_t[:, :], Y[0][:, 0:G]).then_inc(c_sc, 1)
                low1(g, 0)
                next_residual(4)
                route(g)
                next_residual(5)
                weights_t(g)
                next_residual(6)
                weight(g, 0)
                weight(g, 1)
                low2(g, 0)
                next_residual(7)
                low2(g, 1)
                weight(g, 2)
                weight(g, 3)
                low2(g, 2)
                weight(g, 4)
                low2(g, 3)
                next_bn(4)
                low2(g, 4)
                for u in range(5, 8):
                    next_bn(u)
                if more:
                    moments_c(nxt, npar)
                    bias_of(nxt, npar, c_rstd, c_nb)
                if has(g, 2):
                    for m in range(KH):
                        low_agg(m, g + 2)
                for u in range(6):
                    result(g, par, u)
                if more:
                    low_x(nxt, 0)
                result(g, par, 6)
                if more:
                    low_x(nxt, 1)
                result(g, par, 7)

            def first_bias(tiles, rstd_sem, nb_sem):
                dve.wait_ge(rstd_sem, 1)
                dve.scalar_tensor_tensor(nbias[:, 0, tiles], mv[:, 0, tiles, 0], -1.0, rstd[:, 0, tiles],
                                         ALU.mult, ALU.mult).then_inc(nb_sem, 1)

            for m in range(KH):
                low_agg(m, 0)
            for half in range(2):
                tiles = slice(2 * half, 2 * half + 2)
                for u in range(4 * half, 4 * half + 4):
                    residual(0, 0, u, Y[u % 2])
                    bn_c(0, 0, u)
                    if u == 5:
                        first_bias(slice(0, 2), h_rstd, h_nb)
                dve.wait_ge(c_bn, 4 * half + 4)
                for j in (2 * half, 2 * half + 1):
                    last = dve.bn_aggr(mv[:, 0, j, :], stat[:, j, :])
                last.then_inc((h_aggr, c_aggr)[half], 1)
                dve.wait_ge((h_aggr, c_aggr)[half], 1)
                dve.tensor_scalar(var[:, 0, tiles], mv[:, 0, tiles, 1], 1.0, LN_EPS, ALU.mult, ALU.add
                                  ).then_inc((h_var, c_var)[half], 1)
            first_bias(slice(2, 4), c_rstd, c_nb)
            for m in range(KH):
                low_agg(m, 1)
            low_x(0, 0)
            low_x(0, 1)
            pairs(dve, body_c)

        @block.tensor
        def _(pe):
            def product(out_ap, left, right, start, stop):
                pe.matmul(out_ap, left[0], right[0], start=start, stop=False, skip_group_check=True)
                pe.matmul(out_ap, left[0], right[1], start=False, stop=False, skip_group_check=True)
                return pe.matmul(out_ap, left[1], right[0], start=False, stop=stop, skip_group_check=True)

            def small_setup():
                pe.wait_ge(setup_v, 3)
                for n in range(3):
                    last = pe.transpose(X_A[0][0:P + 1, NC * n:NC * (n + 1)], idx_f[0:NC, n, :], ident[0:NC, 0:NC])
                last.then_inc(setup_t, 1)
                pe.wait_ge(raw_small, 16 * 6)
                for k in range(KD):
                    last = pe.transpose(X_A[1][:, NE * k:NE * (k + 1)], tok_rows[:, 128 * k:128 * (k + 1)],
                                        ident[0:NE, 0:NE])
                last.then_inc(setup_t, 1)

            def turn(g, par, k):
                t = KD * g + k
                wait(pe, a_lo, t - 3)
                if k == 0:
                    pe.wait_ge(a_xn, J * (g + 1))
                for j in range(J):
                    last = pe.transpose(T_A[k % 4][:, P * j:P * (j + 1)], axn[:, par, j, 128 * k:128 * (k + 1)],
                                        ident[0:P, 0:P])
                last.then_inc(a_tp, 1)

            def left_right(g, par, j):
                if j == 0:
                    pe.wait_ge(a_hlo, KH * (g + 1))
                    if isinstance(g, int) and g == 0:
                        pe.wait_ge(setup_v, 11)
                        pe.wait_ge(wlr_split, 1)
                wait(pe, a_ev_s if j % 2 == 0 else a_ev_v, 2 * g + j // 2)
                for m in range(KH):
                    rows = slice(P * j, P * (j + 1))
                    last = product(X_A[j % 2][0:P, :], (ht_hi[:, par, m, rows], ht_lo[:, par, m, rows]),
                                   (wlr_hi[:, m, :], wlr_lo[:, m, :]), m == 0, m == KH - 1)
                last.then_inc(a_lr, 1)

            def body(g, par):
                for k in range(KD):
                    if k + 2 < KD:
                        turn(g, par, k + 2)
                    pe.wait_ge(a_lo, KD * g + k + 1)
                    if k == 0:
                        wait(pe, a_hlo, KH * g)
                    for m in range(KH):
                        cols = slice(128 * m, 128 * (m + 1))
                        last = product(H_A[m][:, 0:G], (wd_hi[:, k, cols], wd_lo[:, k, cols]),
                                       (axt_hi[:, k % 4, :], axt_lo[:, k % 4, :]), k == 0, k == KD - 1)
                    last.then_inc(a_mm, 1)
                for j in range(J):
                    if has(g, -1):
                        left_right(g - 1, 1 - par, j)
                    if j < 2 and has(g, 1):
                        turn(g + 1, 1 - par, j)
                if isinstance(g, int) and g == 0:
                    small_setup()

            pe.wait_ge(consts, 2)
            turn(0, 0, 0)
            turn(0, 0, 1)
            pe.wait_ge(setup_v, 2)
            pairs(pe, body)
            for j in range(J):
                left_right(NG - 1, 1, j)

            def add_rows(b, t):
                wait_gathered(pe, b, t)
                wait(pe, b_leak, b - 1)
                ahead = (xls[0:P, bass.ds(CG * b, CG), 0:HID], td[:, t, :, 0:HID])
                for kind in range(2):
                    for n, rows in enumerate((ahead[kind], td[:, t, :, HID:2 * HID])):
                        last = pe.matmul(bank[2 * (t % 2) + kind][0:P, :], ident[0:P, 0:P], rows,
                                         start=n == 0, stop=n == 1, skip_group_check=True)
                last.then_inc(b_sum, 1)

            batches_of_gathers(pe, add_rows)

            pe.wait_ge(b_max, 1)
            for q in range(2):
                pe.transpose(bank[q][0:2 * NC, 0:P], pexp[:, 0, 2 * q:2 * q + 2, :].rearrange("p h c -> p (h c)"),
                             ident[0:P, 0:P]).then_inc(b_max_t, 1)
            pe.wait_ge(b_flags, 3)
            pe.wait_ge(b_tip, 1)
            for n, columns in enumerate((tips[:, :, :].rearrange("p a q -> p (a q)"), chunk_flags[:, 0, :],
                                         chunk_flags[:, 1, :])):
                last = pe.transpose(bank[2][0:H, 2 * NC * n:2 * NC * (n + 1)], columns, ident[0:2 * NC, 0:2 * NC])
            last.then_inc(b_max_t, 1)
            pe.wait_ge(b_tip, 3)
            pe.transpose(bank[3][0:2 * NC, 0:H], carried[:, 0, 0:2 * NC], ident[0:H, 0:H])
            pe.transpose(bank[3][0:2 * NC, H:2 * H], carried[:, 1, 1:2 * NC + 1], ident[0:H, 0:H]
                         ).then_inc(b_max_t, 1)
            pe.wait_ge(b_carried, 6)
            for q in range(2):
                pe.transpose(bank[2][0:P, 2 * NC * q:2 * NC * (q + 1)], max_t[:, q, :],
                             ident[0:2 * NC, 0:2 * NC]).then_inc(b_back, 1)

            pe.wait_ge(b_mask, 3)
            for c in range(NC):
                pe.wait_ge(b_v, c // CB + 1)
                last = pe.matmul(bank[3][0:NC, 0:HV], zmat[:, c, :], xls[0:P, c, :], start=c == 0,
                                 stop=c == NC - 1, skip_group_check=True)
            last.then_inc(b_l, 1)
            pe.wait_ge(b_lsb, 1)
            pe.matmul(bank[4][0:NC, 0:HV], earlier[:, :], lsb[:, :], start=True, stop=True,
                      skip_group_check=True).then_inc(b_l, 1)

            def segment_sums(b, par):
                pe.wait_ge(b_sb, b + 1)
                wait(pe, b_out, b - 1)
                for q in range(CB):
                    last = pe.matmul(bank[4 * par + q][0:P, 0:HV], smat[:, par, q, :],
                                     xls[:, bass.ds(CB * b + q, 1), :].rearrange("p c d -> p (c d)"),
                                     start=True, stop=True, skip_group_check=True)
                last.then_inc(b_num, 1)

            pe.wait_ge(carry_put, 16)
            segment_sums(0, 0)
            segment_sums(1, 1)
            with pe.Fori(1, NB // 2) as i:
                for par in range(2):
                    segment_sums(2 * i + par, par)

            def turn_c(g, k):
                t = KD * g + k
                if k >= 2:
                    pe.wait_ge(c_lo, t - 1)
                else:
                    wait(pe, c_wmul, W2P * g - 1 + k)
                    if has(g, 1):
                        pe.wait_ge(c_alo, KH * (g + 1) + k + 1)
                if k == 0:
                    pe.wait_ge(c_xn, J * (g + 1))
                for j in range(J):
                    last = pe.transpose(T_C[k % 2][:, P * j:P * (j + 1)], cxn[:, j, 128 * k:128 * (k + 1)],
                                        ident[0:P, 0:P])
                last.then_inc(c_tp, 1)

            def turn_agg(g, m):
                if m == 0:
                    pe.wait_ge(agg_loaded, 16 * J * (g + 1))
                wait(pe, c_wmul, W2P * (g - 1) - 1 + m)
                for j in range(J):
                    last = pe.transpose(T_C[m][:, P * j:P * (j + 1)], agg[:, j, 128 * m:128 * (m + 1)],
                                        ident[0:P, 0:P])
                last.then_inc(c_atp, 1)

            def up(g, u, y):
                j, n = u // 2, u % 2
                for m in range(KH):
                    rows, cols = slice(P * j, P * (j + 1)), slice(HALF * n, HALF * (n + 1))
                    last = product(y[0:P, :], (aggt_hi[:, m, rows], aggt_lo[:, m, rows]),
                                   (wup_hi[:, m, cols], wup_lo[:, m, cols]), m == 0, m == KH - 1)
                last.then_inc(c_up, 1)

            def next_up(g, u):
                if u == 0:
                    pe.wait_ge(c_alo, KH * (g + 1))
                    wait(pe, c_w3v, 8 * (g - 1))
                if u == 5:
                    pe.wait_ge(c_sc, g)
                else:
                    pe.wait_ge(c_upv, 8 * g + (u if u < 5 else u - 1))
                up(g, u, UP_BANK[u])

            def hidden1(g, k):
                pe.wait_ge(c_lo, KD * g + k + 1)
                if k == 0:
                    wait(pe, c_w3v, 8 * g - 2)
                for m in range(MF):
                    cols = slice(128 * m, 128 * (m + 1))
                    product(ACC[m][:, 0:G], (w1_hi[:, k, cols], w1_lo[:, k, cols]),
                            (cxt_hi[:, k % 2, :], cxt_lo[:, k % 2, :]), k == 0, k == KD - 1)
                if k == 0:
                    wait(pe, c_w3v, 8 * g - 1)
                pe.matmul(Y[0][:, 0:G], tok_st[:, k, :], cxt_hi[:, k % 2, :], start=k == 0, stop=False,
                          skip_group_check=True)
                pe.matmul(Y[0][:, 0:G], tok_st[:, k, :], cxt_lo[:, k % 2, :], start=False, stop=k == KD - 1,
                          skip_group_check=True).then_inc(c_mm, 1)

            def score_rows(g):
                pe.wait_ge(c_sc, g + 1)
                for j in range(J):
                    last = pe.transpose(T_C[0][0:P, 128 * j:128 * (j + 1)], sc_t[:, P * j:P * (j + 1)],
                                        ident[:, :])
                last.then_inc(c_rs, 1)

            def hidden2(g, m):
                if m == 0:
                    if isinstance(g, int) and g == 0:
                        pe.wait_ge(w3_split_v, 1 + MF)
                    pe.wait_ge(c_h1lo, g + 1)
                else:
                    pe.wait_ge(c_h1lo_p, (MF - 1) * g + m)
                product(ACC[m][:, 0:G], (w2_hi[:, m, :], w2_lo[:, m, :]), (h_hi[:, m, :], h_lo[:, m, :]),
                        True, True).then_inc(c_w2, 1)

            def weights_rows(g):
                pe.wait_ge(c_w, 3 * (g + 1))
                for j in range(J):
                    last = pe.transpose(T_C[1][0:2 * NE, P * j:P * (j + 1)],
                                        wdup[:, j, :, :].rearrange("p a e -> p (a e)"), ident[0:P, 0:P])
                last.then_inc(c_wtp, 1)

            def spread(g, m):
                if m == 0:
                    pe.wait_ge(c_wt, g + 1)
                if m >= 2:
                    pe.wait_ge(c_wmul, W2P * g + m)
                pe.matmul(T_C[m % 2][:, 0:G], expand[:, 128 * m:128 * (m + 1)], w_t[0:NE, :], start=True,
                          stop=True, skip_group_check=True).then_inc(c_wx, 1)

            def down_begin(g, u, more):
                j, n = u // 2, u % 2
                if u in (2, 3):
                    if more:
                        pe.wait_ge(c_upv, 8 * (g + 1) + 5 + u)
                elif u < 6:
                    pe.wait_ge(c_g2, MF * g + (u + 1 if u < 2 else u - 1))
                else:
                    pe.wait_ge(c_w3v, 8 * g + (4 if u == 6 else 3))
                pe.matmul(DOWN_BANK[u][0:P, :], w_t[:, P * j:P * (j + 1)], b3_hl[:, HALF * n:HALF * (n + 1)],
                          start=True, stop=False, skip_group_check=True)

            def down_part(g, u, m):
                j, n = u // 2, u % 2
                rows, cols = slice(P * j, P * (j + 1)), slice(HALF * n, HALF * (n + 1))
                last = product(DOWN_BANK[u][0:P, :], (h_hi[:, m, rows], h_lo[:, m, rows]),
                               (w3_hi[:, m, cols], w3_lo[:, m, cols]), False, m == MF - 1)
                if m == MF - 1:
                    last.then_inc(c_w3, 1)

            def body_c(g, par):
                more = has(g, 1)
                for k in range(KD):
                    if 1 <= k and k + 1 < KD:
                        turn_c(g, k + 1)
                    hidden1(g, k)
                    if 0 <= k + 1 - (KD - KU) < KU and more:
                        next_up(g + 1, k + 1 - (KD - KU))
                if more:
                    next_up(g + 1, 4)
                score_rows(g)
                if more:
                    next_up(g + 1, 5)
                hidden2(g, 0)
                if more:
                    next_up(g + 1, 6)
                hidden2(g, 1)
                weights_rows(g)
                hidden2(g, 2)
                hidden2(g, 3)
                spread(g, 0)
                spread(g, 1)
                if more:
                    next_up(g + 1, 7)
                down_begin(g, 0, more)
                down_begin(g, 1, more)
                for m in range(MF):
                    pe.wait_ge(c_h2lo, W2P * g + (1 if m == 0 else m + 2))
                    for u in range(4):
                        if m == 0 and u >= 2:
                            spread(g, u)
                            down_begin(g, u, more)
                        down_part(g, u, m)
                if has(g, 2):
                    for m in range(KH):
                        turn_agg(g + 2, m)
                for u in range(4, 8):
                    if u >= 6 and more:
                        turn_c(g + 1, u - 6)
                    down_begin(g, u, more)
                    for m in range(MF):
                        down_part(g, u, m)

            pe.wait_ge(w1_split_p, 2)
            for m in range(KH):
                turn_agg(0, m)
            pe.wait_ge(c_alo, KH)
            for u in range(8):
                wait(pe, c_upv, u - 1)
                up(0, u, Y[u % 2])
            for m in range(KH):
                turn_agg(1, m)
            turn_c(0, 0)
            turn_c(0, 1)
            pairs(pe, body_c)


_INS = ["x", "src", "dst", "L0_gnn_rms_w", "L0_gnn_W_down", "L0_gnn_Wl", "L0_gnn_Wr", "L0_gnn_att", "L0_gnn_W_up",
        "L0_ffn_expert_tokens", "L0_ffn_W1", "L0_ffn_b1", "L0_ffn_W2", "L0_ffn_b2", "L0_ffn_W3", "L0_ffn_b3"]


def kernel(**inputs):
    import numpy as np
    import concourse.bacc as bacc
    from concourse.bass_utils import run_bass_kernel_spmd

    nc = bacc.Bacc("TRN2", target_bir_lowering=False, num_devices=1)
    arrays, args = {}, []
    for name in _INS:
        a = np.ascontiguousarray(inputs[name])
        arrays[f"in_{name}"] = a
        args.append(nc.dram_tensor(f"in_{name}", a.shape, mybir.dt.from_np(a.dtype), kind="ExternalInput").ap())
    args.append(nc.dram_tensor("out_0", (N, D), F32, kind="ExternalOutput").ap())
    build(nc, *args)
    r = run_bass_kernel_spmd(nc, [arrays], core_ids=[0])
    return r.results[0]["out_0"]
```
